# Optimizing a Trainium2 kernel written in Bass

```python
import numpy as np
import jax
import jax.numpy as jnp

def _softmax(x, axis=-1):
    return jax.nn.softmax(x, axis=axis)

def _gelu(x):
    return jax.nn.gelu(x, approximate=True)

def _silu(x):
    return jax.nn.silu(x)

def _sigmoid(x):
    return jax.nn.sigmoid(x)

def _layernorm(x, axis=-1, eps=1e-05):
    m = jnp.mean(x, axis=axis, keepdims=True)
    v = jnp.var(x, axis=axis, keepdims=True)
    return (x - m) / jnp.sqrt(v + eps)

def _scatter_add(tgt, idx, src, axis=0):
    return tgt.at[idx].add(src)

def _segment_sum(src, seg, n):
    return jax.ops.segment_sum(src, seg, n)
kernel_name = 'mk_conv_seq_d2_conv_nhwc512_r4_3c9ce2'

def setup_inputs(seed: int=0):
    np.random.seed(seed)
    _w = jnp.asarray

    def _rec_inputs():
        import jax
        import jax.numpy as jnp
        _gk = jax.random.key(seed)
        x = -0.000125 + 0.9999 * jax.random.normal(jax.random.fold_in(_gk, 1), (4, 32, 32, 128), jnp.float32)
        return x
    x = _rec_inputs()

    def _L0_conv_setup():
        import jax, jax.numpy as jnp
        import numpy as np
        WS = (8, 8)
        SS = (4, 4)
        DIM = 128
        HEADS = 16
        HD = DIM // HEADS
        D1 = HD // 2 // 2
        D2 = HD // 2 - D1
        EPS = 1e-05
        B, H, W = (4, 32, 32)
        HIDDEN = int(DIM * 4.0)

        def _layer_norm(x, g, b):
            m = jnp.mean(x, -1, keepdims=True)
            v = jnp.mean((x - m) ** 2, -1, keepdims=True)
            return (x - m) * jax.lax.rsqrt(v + EPS) * g + b

        def _rope_tables():
            wh, ww = WS
            inv1 = 10000.0 ** (-(jnp.arange(D1, dtype=jnp.float32) / D1))
            inv2 = 10000.0 ** (-(jnp.arange(D2, dtype=jnp.float32) / D2))
            rows = jnp.arange(wh, dtype=jnp.float32)[:, None] * inv1
            cols = jnp.arange(ww, dtype=jnp.float32)[:, None] * inv2
            sin1 = jnp.broadcast_to(jnp.sin(rows)[:, None, :], (wh, ww, D1))
            cos1 = jnp.broadcast_to(jnp.cos(rows)[:, None, :], (wh, ww, D1))
            sin2 = jnp.broadcast_to(jnp.sin(cols)[None, :, :], (wh, ww, D2))
            cos2 = jnp.broadcast_to(jnp.cos(cols)[None, :, :], (wh, ww, D2))
            return (sin1, cos1, sin2, cos2)

        def _rope2d(t, tabs):
            sin1, cos1, sin2, cos2 = tabs
            x11 = t[..., :D1]
            x21 = t[..., D1:D1 + D2]
            x12 = t[..., D1 + D2:D1 + D2 + D1]
            x22 = t[..., D1 + D2 + D1:]
            return jnp.concatenate([x11 * cos1 - x12 * sin1, x21 * cos2 - x22 * sin2, x12 * cos1 + x11 * sin1, x22 * cos2 + x21 * sin2], axis=-1)

        def _swin_mask():
            wh, ww = WS
            img = np.zeros((H, W), dtype=np.float32)
            cnt = 0
            for hs in (slice(0, -wh), slice(-wh, -SS[0]), slice(-SS[0], None)):
                for ws in (slice(0, -ww), slice(-ww, -SS[1]), slice(-SS[1], None)):
                    img[hs, ws] = cnt
                    cnt += 1
            mw = img.reshape(H // wh, wh, W // ww, ww).transpose(0, 2, 1, 3).reshape(-1, wh * ww)
            diff = mw[:, None, :] - mw[:, :, None]
            return jnp.asarray(np.where(diff != 0, -100.0, 0.0).astype(np.float32))
        key = jax.random.key(seed)
        ks = jax.random.split(key, 14)
        s = 0.02
        return {'x': jax.random.normal(ks[0], (B, H, W, DIM), jnp.float32), 'attn_mask': _swin_mask(), 'norm1_g': jnp.ones((DIM,), jnp.float32), 'norm1_b': jnp.zeros((DIM,), jnp.float32), 'qkv_w': jax.random.normal(ks[1], (3 * DIM, DIM), jnp.float32) * s, 'qkv_b': jnp.zeros((3 * DIM,), jnp.float32), 'proj_w': jax.random.normal(ks[2], (DIM, DIM), jnp.float32) * s, 'proj_b': jnp.zeros((DIM,), jnp.float32), 'norm2_g': jnp.ones((DIM,), jnp.float32), 'norm2_b': jnp.zeros((DIM,), jnp.float32), 'fc1_w': jax.random.normal(ks[3], (2 * HIDDEN, DIM), jnp.float32) * s, 'fc1_b': jnp.zeros((2 * HIDDEN,), jnp.float32), 'fc2_w': jax.random.normal(ks[4], (DIM, HIDDEN), jnp.float32) * s, 'fc2_b': jnp.zeros((DIM,), jnp.float32)}
    _L0_conv_all = _L0_conv_setup()
    _L0_conv_in = {k: v for k, v in _L0_conv_all.items() if k in ('attn_mask', 'norm1_g', 'norm1_b', 'qkv_w', 'qkv_b', 'proj_w', 'proj_b', 'norm2_g', 'norm2_b', 'fc1_w', 'fc1_b', 'fc2_w', 'fc2_b')}
    del _L0_conv_all

    def _L1_conv_setup():
        import jax, jax.numpy as jnp
        import numpy as np
        C = 128
        CQK = C // 8
        key = jax.random.key(seed)
        ks = jax.random.split(key, 8)
        B, H, W = (4, 16, 16)
        inputs = jax.random.normal(ks[0], (B, H, W, C), dtype=jnp.float32)
        Wq = jax.random.normal(ks[1], (C, CQK), dtype=jnp.float32) * (1.0 / np.sqrt(C))
        bq = jnp.zeros((CQK,), dtype=jnp.float32)
        Wk = jax.random.normal(ks[2], (C, CQK), dtype=jnp.float32) * (1.0 / np.sqrt(C))
        bk = jnp.zeros((CQK,), dtype=jnp.float32)
        Wv = jax.random.normal(ks[3], (C, C), dtype=jnp.float32) * (1.0 / np.sqrt(C))
        bv = jnp.zeros((C,), dtype=jnp.float32)
        gamma = jnp.zeros((1,), dtype=jnp.float32) + 0.5
        return {'inputs': inputs, 'Wq': Wq, 'bq': bq, 'Wk': Wk, 'bk': bk, 'Wv': Wv, 'bv': bv, 'gamma': gamma}
    _L1_conv_all = _L1_conv_setup()
    _L1_conv_in = {k: v for k, v in _L1_conv_all.items() if k in ('Wq', 'bq', 'Wk', 'bk', 'Wv', 'bv', 'gamma')}
    del _L1_conv_all
    return {'x': x, 'L0_conv_attn_mask': _L0_conv_in['attn_mask'], 'L0_conv_norm1_g': _L0_conv_in['norm1_g'], 'L0_conv_norm1_b': _L0_conv_in['norm1_b'], 'L0_conv_qkv_w': _L0_conv_in['qkv_w'], 'L0_conv_qkv_b': _L0_conv_in['qkv_b'], 'L0_conv_proj_w': _L0_conv_in['proj_w'], 'L0_conv_proj_b': _L0_conv_in['proj_b'], 'L0_conv_norm2_g': _L0_conv_in['norm2_g'], 'L0_conv_norm2_b': _L0_conv_in['norm2_b'], 'L0_conv_fc1_w': _L0_conv_in['fc1_w'], 'L0_conv_fc1_b': _L0_conv_in['fc1_b'], 'L0_conv_fc2_w': _L0_conv_in['fc2_w'], 'L0_conv_fc2_b': _L0_conv_in['fc2_b'], 'L1_conv_Wq': _L1_conv_in['Wq'], 'L1_conv_bq': _L1_conv_in['bq'], 'L1_conv_Wk': _L1_conv_in['Wk'], 'L1_conv_bk': _L1_conv_in['bk'], 'L1_conv_Wv': _L1_conv_in['Wv'], 'L1_conv_bv': _L1_conv_in['bv'], 'L1_conv_gamma': _L1_conv_in['gamma']}

def reference(x, L0_conv_attn_mask, L0_conv_norm1_g, L0_conv_norm1_b, L0_conv_qkv_w, L0_conv_qkv_b, L0_conv_proj_w, L0_conv_proj_b, L0_conv_norm2_g, L0_conv_norm2_b, L0_conv_fc1_w, L0_conv_fc1_b, L0_conv_fc2_w, L0_conv_fc2_b, L1_conv_Wq, L1_conv_bq, L1_conv_Wk, L1_conv_bk, L1_conv_Wv, L1_conv_bv, L1_conv_gamma):
    import jax
    import jax.numpy as jnp

    def _L0_conv_ref(x, attn_mask, norm1_g, norm1_b, qkv_w, qkv_b, proj_w, proj_b, norm2_g, norm2_b, fc1_w, fc1_b, fc2_w, fc2_b):
        import jax, jax.numpy as jnp
        import numpy as np
        WS = (8, 8)
        SS = (4, 4)
        DIM = 128
        HEADS = 16
        HD = DIM // HEADS
        D1 = HD // 2 // 2
        D2 = HD // 2 - D1
        EPS = 1e-05
        B, H, W = (4, 32, 32)
        HIDDEN = int(DIM * 4.0)

        def _layer_norm(x, g, b):
            m = jnp.mean(x, -1, keepdims=True)
            v = jnp.mean((x - m) ** 2, -1, keepdims=True)
            return (x - m) * jax.lax.rsqrt(v + EPS) * g + b

        def _rope_tables():
            wh, ww = WS
            inv1 = 10000.0 ** (-(jnp.arange(D1, dtype=jnp.float32) / D1))
            inv2 = 10000.0 ** (-(jnp.arange(D2, dtype=jnp.float32) / D2))
            rows = jnp.arange(wh, dtype=jnp.float32)[:, None] * inv1
            cols = jnp.arange(ww, dtype=jnp.float32)[:, None] * inv2
            sin1 = jnp.broadcast_to(jnp.sin(rows)[:, None, :], (wh, ww, D1))
            cos1 = jnp.broadcast_to(jnp.cos(rows)[:, None, :], (wh, ww, D1))
            sin2 = jnp.broadcast_to(jnp.sin(cols)[None, :, :], (wh, ww, D2))
            cos2 = jnp.broadcast_to(jnp.cos(cols)[None, :, :], (wh, ww, D2))
            return (sin1, cos1, sin2, cos2)

        def _rope2d(t, tabs):
            sin1, cos1, sin2, cos2 = tabs
            x11 = t[..., :D1]
            x21 = t[..., D1:D1 + D2]
            x12 = t[..., D1 + D2:D1 + D2 + D1]
            x22 = t[..., D1 + D2 + D1:]
            return jnp.concatenate([x11 * cos1 - x12 * sin1, x21 * cos2 - x22 * sin2, x12 * cos1 + x11 * sin1, x22 * cos2 + x21 * sin2], axis=-1)

        def _swin_mask():
            wh, ww = WS
            img = np.zeros((H, W), dtype=np.float32)
            cnt = 0
            for hs in (slice(0, -wh), slice(-wh, -SS[0]), slice(-SS[0], None)):
                for ws in (slice(0, -ww), slice(-ww, -SS[1]), slice(-SS[1], None)):
                    img[hs, ws] = cnt
                    cnt += 1
            mw = img.reshape(H // wh, wh, W // ww, ww).transpose(0, 2, 1, 3).reshape(-1, wh * ww)
            diff = mw[:, None, :] - mw[:, :, None]
            return jnp.asarray(np.where(diff != 0, -100.0, 0.0).astype(np.float32))
        wh, ww = WS
        N = wh * ww
        nH, nW = (H // wh, W // ww)
        nWin = nH * nW
        B_ = B * nWin
        tabs = _rope_tables()
        shortcut = x
        xn = _layer_norm(x, norm1_g, norm1_b)
        xs = jnp.roll(xn, (-SS[0], -SS[1]), axis=(1, 2))
        xw = xs.reshape(B, nH, wh, nW, ww, DIM).transpose(0, 1, 3, 2, 4, 5).reshape(B_, N, DIM)
        qkv = xw @ qkv_w.T + qkv_b
        qkv = qkv.reshape(B_, N, 3, HEADS, HD).transpose(2, 0, 3, 1, 4)
        q, k, v = (qkv[0], qkv[1], qkv[2])
        q = _rope2d(q.reshape(-1, wh, ww, HD), tabs).reshape(B_, HEADS, N, HD)
        k = _rope2d(k.reshape(-1, wh, ww, HD), tabs).reshape(B_, HEADS, N, HD)
        scale = HD ** (-0.5)
        attn = jnp.einsum('bhnd,bhmd->bhnm', q * scale, k)
        attn = attn.reshape(B, nWin, HEADS, N, N) + attn_mask[None, :, None]
        attn = jax.nn.softmax(attn.reshape(B_, HEADS, N, N), axis=-1)
        out = jnp.einsum('bhnm,bhmd->bhnd', attn, v).transpose(0, 2, 1, 3).reshape(B_, N, DIM)
        out = out @ proj_w.T + proj_b
        out = out.reshape(B, nH, nW, wh, ww, DIM).transpose(0, 1, 3, 2, 4, 5).reshape(B, H, W, DIM)
        out = jnp.roll(out, (SS[0], SS[1]), axis=(1, 2))
        x = shortcut + out
        y = _layer_norm(x, norm2_g, norm2_b)
        h = y @ fc1_w.T + fc1_b
        a, gate = jnp.split(h, 2, axis=-1)
        h = jax.nn.silu(gate) * a
        y = h @ fc2_w.T + fc2_b
        return x + y

    def _L1_conv_ref(inputs, Wq, bq, Wk, bk, Wv, bv, gamma):
        import jax, jax.numpy as jnp
        import numpy as np
        C = 128
        CQK = C // 8
        B, H, W, Cc = inputs.shape
        N = H * W
        f = jnp.einsum('bhwc,cd->bhwd', inputs, Wq) + bq
        g = jnp.einsum('bhwc,cd->bhwd', inputs, Wk) + bk
        h = jnp.einsum('bhwc,cd->bhwd', inputs, Wv) + bv
        f = f.reshape(B, N, -1)
        g = g.reshape(B, N, -1)
        h = h.reshape(B, N, -1)
        s = jnp.einsum('bnd,bmd->bnm', f, g)
        beta = jax.nn.softmax(s, axis=-1)
        o = jnp.einsum('bnm,bmc->bnc', beta, h)
        o = o.reshape(B, H, W, Cc)
        return gamma * o + inputs

    def _gn(v, G=32, eps=1e-05):
        B_, H_, W_, C_ = v.shape
        g = v.reshape(B_, H_, W_, G, C_ // G)
        m = jnp.mean(g, axis=(1, 2, 4), keepdims=True)
        s = jnp.var(g, axis=(1, 2, 4), keepdims=True)
        return ((g - m) / jnp.sqrt(s + eps)).reshape(v.shape)

    def _ln_c(v, eps=1e-06):
        m = jnp.mean(v, axis=-1, keepdims=True)
        s = jnp.var(v, axis=-1, keepdims=True)
        return (v - m) / jnp.sqrt(s + eps)

    def _ln_t(v, eps=1e-05):
        m = jnp.mean(v, axis=-1, keepdims=True)
        s = jnp.var(v, axis=-1, keepdims=True)
        return (v - m) / jnp.sqrt(s + eps)

    def _to_tokens(v):
        B_, H_, W_, C_ = v.shape
        return v.reshape(B_, H_ * W_, C_)

    def _from_tokens(t, like):
        return t.reshape(like.shape)
    x = _L0_conv_ref(x, L0_conv_attn_mask, L0_conv_norm1_g, L0_conv_norm1_b, L0_conv_qkv_w, L0_conv_qkv_b, L0_conv_proj_w, L0_conv_proj_b, L0_conv_norm2_g, L0_conv_norm2_b, L0_conv_fc1_w, L0_conv_fc1_b, L0_conv_fc2_w, L0_conv_fc2_b)
    x = _L1_conv_ref(x, L1_conv_Wq, L1_conv_bq, L1_conv_Wk, L1_conv_bk, L1_conv_Wv, L1_conv_bv, L1_conv_gamma)
    return x

_drawn_inputs = setup_inputs


def setup_inputs(seed=0):
    import zlib

    import numpy as np

    out = dict(_drawn_inputs(seed))
    spreads = {'L0_conv_norm1_g': (1.0, 0.6),
     'L0_conv_norm1_b': (0.0, 0.8),
     'L0_conv_qkv_b': (0.0, 0.1),
     'L0_conv_proj_b': (0.0, 0.1),
     'L0_conv_norm2_g': (1.0, 0.6),
     'L0_conv_norm2_b': (0.0, 0.8),
     'L0_conv_fc1_b': (0.0, 0.758),
     'L0_conv_fc2_b': (0.0, 0.1),
     'L1_conv_bq': (0.0, 0.1),
     'L1_conv_bk': (0.0, 2.0),
     'L1_conv_bv': (0.0, 0.271)}
    factors = {'L0_conv_qkv_w': 4.637, 'L0_conv_fc1_w': 2.988, 'L0_conv_fc2_w': 2.933}
    for name, (base, spread) in spreads.items():
        noise = np.random.default_rng([zlib.crc32(name.encode()), seed]).standard_normal(out[name].shape)
        drawn = base * np.exp(spread * noise) if base else spread * noise
        out[name] = jnp.asarray(drawn.astype(out[name].dtype))
    for name, factor in factors.items():
        out[name] = (out[name] * factor).astype(out[name].dtype)
    return out
```

```python
from contextlib import ExitStack

import concourse.bass as bass
import numpy as np
from concourse import mybir

F32 = mybir.dt.float32
F16 = mybir.dt.float16
BF16 = mybir.dt.bfloat16
ALU = mybir.AluOpType
ACT = mybir.ActivationFunctionType
AX = mybir.AxisListType

B, H, W, DIM = 4, 32, 32, 128
WIN, SHIFT = 8, 4
HEADS, HD = 16, 8
NWIN = (H // WIN) * (W // WIN)
WTOK = WIN * WIN
PAIRS = NWIN * B // 2
TOK = B * H * W
CHUNK = 512
CHUNKS = TOK // CHUNK
TPC = CHUNK // 128
HIDDEN = 4 * DIM
HBLK = HIDDEN // 128
CQK = DIM // 8
NB = H * W
BT = NB // 128
EPS = 1e-5
WSCALE = 64.0
MSCALE = 256.0
ROWS = 32
HP = HEADS // 2
MAXROW = 3 * HD


def at(start, size):
    return bass.ds(start, size)


def build(nc, t):
    ctx = ExitStack()
    with ctx:
        def sb(name, shape, dt=F32):
            return ctx.enter_context(nc.sbuf_tensor(name, shape, dt))

        def sem(name):
            return ctx.enter_context(nc.semaphore(name))

        qkv_w = sb("qkv_w", [128, 3 * DIM])
        qkv_b = sb("qkv_b", [33, 3 * DIM])
        g1b1 = sb("g1b1", [128, 4])
        w_scaled = sb("w_scaled", [128, 2 * HIDDEN])
        qkv_w16 = sb("qkv_w16", [128, 2, 3 * DIM], F16)
        qkv_b16 = sb("qkv_b16", [33, 3 * DIM], F16)
        sel33 = sb("sel33", [33, 128], F16)
        rope = sb("rope", [128, 2, 2, HD])
        ident = sb("ident", [128, 128])
        ident16 = sb("ident16", [128, 128], F16)
        identb = sb("identb", [128, 128], BF16)
        proj_w = sb("proj_w", [64, 2, DIM])
        proj_b = sb("proj_b", [128, DIM])
        fc1_w = sb("fc1_w", [128, 2 * HIDDEN])
        fc1_w16 = sb("fc1_w16", [128, 2, 2 * HIDDEN], F16)
        fc1_b = sb("fc1_b", [128, 2 * HBLK])
        fc1_bias = sb("fc1_bias", [128, 2 * HBLK])
        fc2_w = sb("fc2_w", [128, HBLK, DIM])
        fc2_ws = sb("fc2_ws", [128, HBLK, DIM])
        cols = sb("cols", [128, 4])
        fg_w = sb("fg_w", [128, 2, 64])
        fg_b = sb("fg_b", [64, 4])
        wv = sb("wv", [128, DIM])
        ln_const = sb("ln_const", [128, 3, TPC])
        ones = sb("ones", [128, 128])
        mask_f = sb("mask_f", [128, 2, NWIN, WTOK])
        mask16 = sb("mask16", [128, 3, 2, NWIN, WTOK], BF16)

        x_all = sb("x_all", [128, PAIRS, DIM])
        a_all = sb("a_all", [128, PAIRS, 2, HP, HD])
        until_mlp = ExitStack()
        xn_all = until_mlp.enter_context(nc.sbuf_tensor("xn_all", [128, CHUNKS, 2, TPC, 128], F16))
        v_hi = until_mlp.enter_context(nc.sbuf_tensor("v_hi", [128, PAIRS, HP, 2, 2, HD + 1], F16))
        v_lo = until_mlp.enter_context(nc.sbuf_tensor("v_lo", [128, PAIRS, HP, 2, 2, HD + 1], F16))

        ps = ctx.enter_context(nc.psum_tensor("ps", [128, 8, 512], F32))

        loaded = sem("loaded")
        x_loaded = [sem(f"x_loaded{c}") for c in range(CHUNKS)]
        prep_dve = sem("prep_dve")
        prep_pe = sem("prep_pe")
        prep_pool = sem("prep_pool")
        ln_stats = sem("ln_stats")
        ln_pool = sem("ln_pool")
        ln_rstd = sem("ln_rstd")
        ln_norm = sem("ln_norm")
        ln_hi = sem("ln_hi")
        ln_lo = sem("ln_lo")
        ln_turned = sem("ln_turned")
        ln_ready = sem("ln_ready")

        qkv_done = sem("qkv_done")
        rope_done = sem("rope_done")
        vhi_done = sem("vhi_done")
        vlo_done = sem("vlo_done")
        r_done = sem("r_done")
        hi_done = sem("hi_done")
        lo_done = sem("lo_done")
        t1_done = sem("t1_done")
        qk_ready = sem("qk_ready")
        s_done = sem("s_done")
        max_done = sem("max_done")
        mhi_done = sem("mhi_done")
        mlo_done = sem("mlo_done")
        t2_done = sem("t2_done")
        q2_ready = sem("q2_ready")
        st_done = sem("st_done")
        exp_done = sem("exp_done")
        phi_done = sem("phi_done")
        plo_done = sem("plo_done")
        pv_done = sem("pv_done")
        rec_done = sem("rec_done")
        norm_done = sem("norm_done")

        def wait(eng, s, value):
            if not isinstance(value, int) or value > 0:
                eng.wait_ge(s, value)

        N_LOADS = 20
        with ExitStack() as st:
            def tmp(name, shape, dt=F32):
                return st.enter_context(nc.sbuf_tensor(name, shape, dt))

            stats = tmp("stats", [128, 2, TPC, 6])
            mv = tmp("mv", [128, 2, TPC, 2])
            veps = tmp("veps", [128, 2, TPC])
            rstd = tmp("rstd", [128, 2, TPC])
            nmean = tmp("nmean", [128, 2, TPC])
            nmr = tmp("nmr", [128, 2, TPC])
            xn = tmp("xn", [128, 2, CHUNK])
            xh = tmp("xh", [128, 2, CHUNK], F16)
            xl = tmp("xl", [128, 2, CHUNK], F16)
            mrest = tmp("mrest", [128, 2, NWIN, WTOK])

            with nc.Block() as block:
                @block.sync
                def _(sp):
                    for c in range(CHUNKS):
                        sp.dma_start(x_all[:, TPC * c:TPC * c + TPC, :],
                                     t["x"][:, TPC * c:TPC * c + TPC, :]).then_inc(x_loaded[c], 16)
                        if c == 0:
                            for dst, name in ((qkv_w, "qkv_w"), (qkv_b, "qkv_b"), (g1b1, "g1b1"), (ident16, "ident16"),
                                              (ident, "ident"), (sel33, "sel33")):
                                sp.dma_start(dst[:], t[name]).then_inc(loaded, 16)
                    for dst, name in ((rope, "rope"), (mask_f, "mask"), (identb, "identb"), (proj_w, "proj_w"),
                                      (proj_b, "proj_b"), (fc1_w, "fc1_w"), (fc1_b, "fc1_b"), (fc2_w, "fc2_w"),
                                      (cols, "cols"), (fg_w, "fg_w"), (fg_b, "fg_b"), (wv, "wv"), (ln_const, "ln_const"),
                                      (ones, "ones")):
                        sp.dma_start(dst[:], t[name]).then_inc(loaded, 16)

                @block.vector
                def _(dve):
                    def norm(c):
                        dve.wait_ge(ln_rstd, c + 1)
                        if c >= 2:
                            dve.wait_ge(ln_lo, c - 1)
                            dve.wait_ge(ln_hi, c - 1)
                        for k in range(TPC):
                            last = dve.tensor_scalar(xn[:, c % 2, 128 * k:128 * k + 128], x_all[:, TPC * c + k, :],
                                                     rstd[:, c % 2, k:k + 1], nmr[:, c % 2, k:k + 1], ALU.mult, ALU.add)
                        last.then_inc(ln_norm, 1)

                    def ready(c):
                        dve.wait_ge(ln_turned, c + 1)
                        dve.tensor_copy(xn_all[:, c].rearrange("p s t q -> p (s t q)"),
                                        ps[:, c % 2, :].bitcast(F16)).then_inc(ln_ready, 1)

                    for c in range(CHUNKS + 2):
                        if c < CHUNKS:
                            dve.wait_ge(x_loaded[c], 16)
                            if c >= 2:
                                dve.wait_ge(ln_rstd, c - 1)
                            for k in range(TPC):
                                last = dve.bn_stats(stats[:, c % 2, k, :], x_all[:, TPC * c + k, :])
                            last.then_inc(ln_stats, 1)
                            dve.wait_ge(ln_stats, 2 * c + 1)
                            for k in range(TPC):
                                last = dve.bn_aggr(mv[:, c % 2, k, :], stats[:, c % 2, k, :])
                            last.then_inc(ln_stats, 1)
                        if 1 <= c <= CHUNKS:
                            norm(c - 1)
                        if c >= 2:
                            ready(c - 2)
                    dve.wait_ge(loaded, 16 * N_LOADS)
                    dve.tensor_scalar(w_scaled[:, 0:3 * DIM], qkv_w[:], g1b1[:, 0:1], WSCALE, ALU.mult, ALU.mult)\
                        .then_inc(prep_dve, 1)
                    dve.wait_ge(prep_dve, 1)
                    dve.tensor_copy(qkv_w16[:, 0, :], w_scaled[:, 0:3 * DIM]).then_inc(prep_dve, 1)
                    dve.wait_ge(prep_dve, 2)
                    dve.tensor_tensor(qkv_w16[:, 1, :], w_scaled[:, 0:3 * DIM], qkv_w16[:, 0, :], ALU.subtract)\
                        .then_inc(prep_dve, 1)
                    dve.wait_ge(prep_pe, 1)
                    dve.wait_ge(prep_dve, 3)
                    dve.tensor_tensor(w_scaled[0:33, 0:3 * DIM], ps[0:33, 2, 0:3 * DIM], qkv_b[:], ALU.add)\
                        .then_inc(prep_dve, 1)
                    dve.wait_ge(prep_dve, 4)
                    dve.tensor_scalar(qkv_b16[:], w_scaled[0:33, 0:3 * DIM], WSCALE, None, ALU.mult)\
                        .then_inc(prep_dve, 1)
                    dve.wait_ge(prep_dve, 5)
                    dve.scalar_tensor_tensor(out=qkv_b16[32:33, :], in0=w_scaled[32:33, 0:3 * DIM], scalar=WSCALE,
                                             in1=qkv_b16[32:33, :], op0=ALU.mult, op1=ALU.subtract)\
                        .then_inc(prep_dve, 1)
                    dve.wait_ge(prep_dve, 6)
                    dve.tensor_scalar(w_scaled[:], fc1_w[:], g1b1[:, 2:3], WSCALE, ALU.mult, ALU.mult)\
                        .then_inc(prep_dve, 1)
                    dve.wait_ge(prep_dve, 7)
                    dve.tensor_copy(fc1_w16[:, 0, :], w_scaled[:]).then_inc(prep_dve, 1)
                    dve.wait_ge(prep_dve, 8)
                    dve.tensor_tensor(fc1_w16[:, 1, :], w_scaled[:], fc1_w16[:, 0, :], ALU.subtract)\
                        .then_inc(prep_dve, 1)
                    dve.wait_ge(prep_pe, 2)
                    dve.tensor_tensor(fc1_bias[:], ps[:, 3, 0:2 * HBLK], fc1_b[:], ALU.add).then_inc(prep_dve, 1)
                    dve.wait_ge(prep_dve, 10)
                    dve.tensor_scalar(fc1_bias[:, 0:HBLK], fc1_bias[:, 0:HBLK], WSCALE, None, ALU.mult)\
                        .then_inc(prep_dve, 1)
                    dve.tensor_scalar(fc2_ws[:], fc2_w[:], 1.0 / WSCALE, None, ALU.mult).then_inc(prep_dve, 1)
                    m = mask_f[:]
                    dve.tensor_copy(mask16[:, 0], m).then_inc(prep_dve, 1)
                    dve.wait_ge(prep_dve, 13)
                    dve.tensor_tensor(mrest[:], m, mask16[:, 0], ALU.subtract).then_inc(prep_dve, 1)
                    dve.wait_ge(prep_dve, 14)
                    dve.tensor_copy(mask16[:, 1], mrest[:]).then_inc(prep_dve, 1)
                    dve.wait_ge(prep_dve, 15)
                    dve.tensor_tensor(mask16[:, 2], mrest[:], mask16[:, 1], ALU.subtract).then_inc(prep_dve, 1)

                @block.gpsimd
                def _(pool):
                    pool.wait_ge(loaded, 16 * N_LOADS)
                    for c in range(CHUNKS):
                        pool.wait_ge(ln_stats, 2 * c + 2)
                        if c >= 2:
                            pool.wait_ge(ln_norm, c - 1)
                        pool.tensor_tensor(veps[:, c % 2, :], mv[:, c % 2, :, 1], ln_const[:, 1, :], ALU.add)\
                            .then_inc(ln_pool, 1)
                        pool.tensor_tensor(nmean[:, c % 2, :], mv[:, c % 2, :, 0], ln_const[:, 2, :], ALU.mult)\
                            .then_inc(ln_pool, 1)
                        pool.wait_ge(ln_pool, 3 * c + 2)
                        pool.tensor_tensor(rstd[:, c % 2, :], veps[:, c % 2, :], ln_const[:, 0, :], ALU.pow)\
                            .then_inc(ln_pool, 1)
                        pool.wait_ge(ln_pool, 3 * c + 3)
                        pool.tensor_tensor(nmr[:, c % 2, :], nmean[:, c % 2, :], rstd[:, c % 2, :], ALU.mult)\
                            .then_inc(ln_rstd, 1)
                        pool.wait_ge(ln_hi, c + 1)
                        if c >= 2:
                            pool.wait_ge(ln_turned, c - 1)
                        pool.tensor_tensor(xl[:, c % 2, :], xn[:, c % 2, :], xh[:, c % 2, :], ALU.subtract)\
                            .then_inc(ln_lo, 1)
                    pool.memset(v_hi[:], 0.0).then_inc(prep_pool, 1)
                    pool.memset(v_lo[:], 0.0).then_inc(prep_pool, 1)
                    pool.wait_ge(prep_pool, 2)
                    for e in range(2):
                        pool.memset(v_hi[64 * e:64 * e + 64, :, :, e, :, HD:HD + 1], WSCALE).then_inc(prep_pool, 1)

                @block.scalar
                def _(act):
                    for c in range(CHUNKS):
                        act.wait_ge(ln_norm, c + 1)
                        if c >= 2:
                            act.wait_ge(ln_turned, c - 1)
                            act.wait_ge(ln_lo, c - 1)
                        act.activation(xh[:, c % 2, :], xn[:, c % 2, :], ACT.Copy).then_inc(ln_hi, 1)

                @block.tensor
                def _(pe):
                    pe.wait_ge(loaded, 16 * N_LOADS)
                    for c in range(CHUNKS):
                        pe.wait_ge(ln_lo, c + 1)
                        if c >= 2:
                            pe.wait_ge(ln_ready, c - 1)
                        out = ps[:, c % 2, :].bitcast(F16).rearrange("p (s t q) -> p s t q", s=2, t=TPC)
                        for s, src in enumerate((xh, xl)):
                            for k in range(TPC):
                                last = pe.transpose(out[:, s, k, :], src[:, c % 2, 128 * k:128 * k + 128], ident16[:])
                        last.then_inc(ln_turned, 1)
                    pe.matmul(ps[0:33, 2, 0:3 * DIM], g1b1[:, 1:2].broadcast_to([128, 33]), qkv_w[:], start=True,
                              stop=True).then_inc(prep_pe, 1)
                    for k in range(2 * HBLK):
                        last = pe.matmul(ps[:, 3, k:k + 1], fc1_w[:, 128 * k:128 * k + 128], g1b1[:, 3:4],
                                         start=True, stop=True)
                    last.then_inc(prep_pe, 1)

        with ExitStack() as st:
            def tmp(name, shape, dt=F32):
                return st.enter_context(nc.sbuf_tensor(name, shape, dt))

            ta = tmp("ta", [128, 2, 2, HEADS, HD])
            tb = tmp("tb", [128, 2, 2, HEADS, HD])
            rot = tmp("rot", [128, 2, 2, HEADS, HD])
            q_rows = tmp("q_rows", [128, 2, HEADS, ROWS], F16)
            k_rows = tmp("k_rows", [128, 2, HEADS, ROWS], F16)
            q_t = tmp("q_t", [128, 2, 4, 128], F16)
            k_t = tmp("k_t", [128, 2, 4, 128], F16)
            q_t2 = tmp("q_t2", [128, 2, 4, 128], F16)
            mx = tmp("mx", [128, 2, HEADS])
            e_buf = tmp("e_buf", [128, 2, 4, 256])
            p_hi = tmp("p_hi", [128, 2, 4, 256], F16)
            p_lo = tmp("p_lo", [128, 2, 4, 256], F16)
            rec = tmp("rec", [128, 2, 2, 4, 2])
            rows_set = st.enter_context(nc.semaphore("rows_set"))

            FIRST, LAST = -2, PAIRS + 1
            LOOP_FROM, LOOP_TO = 4, PAIRS - 2

            def steps(eng, body):
                for n in range(FIRST, LOOP_FROM):
                    body(n, n // 2, n % 2)
                with eng.Fori(LOOP_FROM // 2, LOOP_TO // 2) as it:
                    for u in range(2):
                        body(it * 2 + u, it, u)
                for n in range(LOOP_TO, LAST + 1):
                    body(n, n // 2, n % 2)

            def valid(n, lag):
                return not isinstance(n, int) or 0 <= n - lag < PAIRS

            def qk_bank(u):
                return ps[:, 0, 256:512]

            with nc.Block() as block:
                @block.tensor
                def _(pe):
                    pe.wait_ge(ln_ready, CHUNKS)
                    pe.wait_ge(prep_dve, 16)
                    pe.wait_ge(prep_pool, 4)
                    pe.wait_ge(rows_set, 3)

                    def project(i, it, u):
                        c, k = it // 2 if isinstance(it, int) else None, None
                        first = True
                        for xs, ws in ((0, 0), (0, 1), (1, 0)):
                            x = tokens(i, xs)
                            pe.matmul(ps[:, 0, 256:512], x, qkv_w16[:, ws, 0:256], start=first, stop=False,
                                      skip_group_check=True)
                            pe.matmul(ps[:, 1, 256:384], x, qkv_w16[:, ws, 256:384], start=first, stop=False,
                                      skip_group_check=True)
                            first = False
                        pe.matmul(ps[:, 0, 256:512], sel33[:], qkv_b16[:, 0:256], start=False, stop=True,
                                  skip_group_check=True)
                        pe.matmul(ps[:, 1, 256:384], sel33[:], qkv_b16[:, 256:384], start=False, stop=True,
                                  skip_group_check=True).then_inc(qkv_done, 1)

                    def tokens(i, s):
                        if isinstance(i, int):
                            return xn_all[:, i // TPC, s, i % TPC, :]
                        return xn_flat[:, at((i // TPC) * (2 * CHUNK) + (i % TPC) * 128 + s * CHUNK, 128)]

                    xn_flat = xn_all[:].rearrange("p c s t q -> p (c s t q)")

                    def scores(out_bank, left, right, w, side, depth):
                        for j in range(4):
                            for m in range(3):
                                mm = mask16[:, m, side, at(w, 1), :].broadcast_to([128, 4, WTOK])
                                pe.matmul(ps[:, out_bank + j, 0:256].rearrange("p (c k) -> p c k", c=4),
                                          identb[:], mm, start=(m == 0), stop=False, skip_group_check=True)
                        for c in range(4):
                            for j in range(4):
                                for e in range(2):
                                    last = pe.matmul(
                                        ps[64 * e:64 * e + 64, out_bank + j, 64 * c:64 * c + 64],
                                        left[ROWS * j:ROWS * j + depth, c, 64 * e:64 * e + 64],
                                        right[ROWS * j:ROWS * j + depth, c, 64 * e:64 * e + 64],
                                        start=False, stop=(c == 3), skip_group_check=True)
                        return last

                    def body(n, it, u):
                        if valid(n, 0):
                            wait(pe, qk_ready, n + 1)
                            wait(pe, max_done, n)
                            if valid(n, -1):
                                wait(pe, rope_done, n + 2)
                                wait(pe, vlo_done, n + 2)
                            scores(0, q_t[:, u], k_t[:, u], it, 0, MAXROW).then_inc(s_done, 1)
                        if valid(n, 1):
                            wait(pe, q2_ready, n)
                            wait(pe, exp_done, n - 1)
                            wait(pe, norm_done, n - 2)
                            scores(4, k_t[:, 1 - u], q_t2[:, 1 - u], it if u else it - 1, 1, ROWS).then_inc(st_done, 1)
                        if valid(n, -2):
                            if valid(n, 0):
                                wait(pe, max_done, n + 1)
                            else:
                                wait(pe, rope_done, n + 2)
                                wait(pe, vlo_done, n + 2)
                            project(n + 2, it + 1, u)
                        if valid(n, -1):
                            wait(pe, lo_done, n + 2)
                            if valid(n, 0):
                                wait(pe, max_done, n + 1)
                            for c in range(4):
                                pe.transpose(ps[:, 2, 256:512].bitcast(F16)[:, 128 * c:128 * c + 128],
                                             q_rows[:, 1 - u, 4 * c:4 * c + 4, :].rearrange("p h r -> p (h r)"), ident16[:])
                                last = pe.transpose(ps[:, 3, 256:512].bitcast(F16)[:, 128 * c:128 * c + 128],
                                                    k_rows[:, 1 - u, 4 * c:4 * c + 4, :].rearrange("p h r -> p (h r)"), ident16[:])
                            last.then_inc(t1_done, 1)
                        if valid(n, 0):
                            wait(pe, mlo_done, n + 1)
                            wait(pe, exp_done, n)
                            for c in range(4):
                                last = pe.transpose(ps[:, 4, 256:512].bitcast(F16)[:, 128 * c:128 * c + 128],
                                                    q_rows[:, u, 4 * c:4 * c + 4, :].rearrange("p h r -> p (h r)"), ident16[:])
                            last.then_inc(t2_done, 1)
                        if valid(n, 2):
                            i = n - 2
                            wait(pe, plo_done, n - 1)
                            if valid(n, 1):
                                wait(pe, exp_done, n)
                            else:
                                wait(pe, norm_done, n - 2)
                            for hp in range(HP):
                                j, m = hp // 2, hp % 2
                                out = ps[:, 5 + hp // 4, 256 + 36 * (hp % 4):256 + 36 * (hp % 4) + 36]
                                for k, (p, v) in enumerate(((p_hi, v_hi), (p_hi, v_lo), (p_lo, v_hi))):
                                    last = pe.matmul(out, p[:, u, j, 128 * m:128 * m + 128],
                                                     v[:, at(i, 1), hp].rearrange("p a e r d -> p (a e r d)"),
                                                     start=(k == 0 and hp % 4 == 0), stop=(k == 2), skip_group_check=True)
                            last.then_inc(pv_done, 1)

                    steps(pe, body)

                @block.vector
                def _(dve):
                    dve.memset(q_rows[:], 0.0).then_inc(rows_set, 1)
                    dve.memset(k_rows[:], 0.0).then_inc(rows_set, 1)
                    dve.wait_ge(rows_set, 2)
                    dve.memset(k_rows[:, :, :, MAXROW:MAXROW + 2], MSCALE).then_inc(rows_set, 1)

                    def body(n, it, u):
                        if valid(n, 0):
                            dve.wait_ge(s_done, n + 1)
                            dve.tensor_reduce(mx[:, u, :], ps[:, 0:4, 0:256].rearrange("p j (c k) -> p c j k", c=4),
                                              AX.X, ALU.max).then_inc(max_done, 1)
                            dve.wait_ge(max_done, n + 1)
                            hi = q_rows[:, u, :, MAXROW]
                            lo = q_rows[:, u, :, MAXROW + 1]
                            dve.tensor_scalar(hi, mx[:, u, :], -1.0 / MSCALE, None, ALU.mult).then_inc(mhi_done, 1)
                            dve.wait_ge(mhi_done, n + 1)
                            dve.scalar_tensor_tensor(out=lo, in0=mx[:, u, :], scalar=-1.0 / MSCALE, in1=hi,
                                                     op0=ALU.mult, op1=ALU.subtract).then_inc(mlo_done, 1)
                        if valid(n, -2):
                            dve.wait_ge(qkv_done, n + 3)
                            wait(dve, r_done, n + 1)
                            x = ps[:, 0, 256:512].rearrange("p (a h d) -> p a h d", a=2, h=HEADS)
                            for dst, k in ((ta, 0), (tb, 1)):
                                for a in range(2):
                                    last = dve.tensor_tensor(dst[:, u, a], x[:, a],
                                                             rope[:, k, a:a + 1, :].broadcast_to([128, HEADS, HD]), ALU.mult)
                            last.then_inc(rope_done, 1)
                            dve.wait_ge(vhi_done, n + 3)
                            for e in range(2):
                                rows = slice(64 * e, 64 * e + 64)
                                last = dve.tensor_tensor(
                                    v_lo[rows, at(n + 2, 1), :, e, :, 0:HD].rearrange("p a h r d -> p (a h) r d"),
                                    ps[rows, 1, 256:384].rearrange("p (r h d) -> p h r d", r=2, d=HD),
                                    v_hi[rows, at(n + 2, 1), :, e, :, 0:HD].rearrange("p a h r d -> p (a h) r d"),
                                    ALU.subtract)
                            last.then_inc(vlo_done, 1)
                        if valid(n, -1):
                            dve.wait_ge(t1_done, n + 2)
                            dve.tensor_copy(q_t[:, 1 - u].rearrange("p c q -> p (c q)"), ps[:, 2, 256:512].bitcast(F16))
                            dve.tensor_copy(k_t[:, 1 - u].rearrange("p c q -> p (c q)"), ps[:, 3, 256:512].bitcast(F16))\
                                .then_inc(qk_ready, 1)
                        if valid(n, 2):
                            i = n - 2
                            dve.wait_ge(pv_done, n - 1)
                            o = ps[:, 5:7, 256:400].rearrange("p b (h e r d) -> p b h e r d", h=4, e=2, r=2)
                            for r in range(2):
                                rows = slice(64 * r, 64 * r + 64)
                                last = dve.reciprocal(rec[rows, u], o[rows, :, :, :, r, HD])
                            last.then_inc(rec_done, 1)
                            dve.wait_ge(rec_done, n - 1)
                            for r in range(2):
                                rows = slice(64 * r, 64 * r + 64)
                                for b in range(2):
                                    last = dve.tensor_tensor(
                                        a_all[rows, at(i, 1), :, 4 * b:4 * b + 4, :].rearrange("p a e h d -> p h (a e) d"),
                                        o[rows, b, :, :, r, 0:HD],
                                        rec[rows, u, b, :, :].unsqueeze(3).broadcast_to([64, 4, 2, HD]), ALU.mult)
                            last.then_inc(norm_done, 1)

                    steps(dve, body)

                @block.scalar
                def _(act):
                    act.wait_ge(rows_set, 3)
                    act.wait_ge(prep_pool, 4)

                    def body(n, it, u):
                        if valid(n, 1):
                            act.wait_ge(st_done, n)
                            wait(act, plo_done, n - 2)
                            act.activation(e_buf[:, 1 - u], ps[:, 4:8, 0:256], ACT.Exp).then_inc(exp_done, 1)
                        if valid(n, -2):
                            act.wait_ge(qkv_done, n + 3)
                            for e in range(2):
                                rows = slice(64 * e, 64 * e + 64)
                                last = act.activation(
                                    v_hi[rows, at(n + 2, 1), :, e, :, 0:HD].rearrange("p a h r d -> p (a h) r d"),
                                    ps[rows, 1, 256:384].rearrange("p (r h d) -> p h r d", r=2, d=HD),
                                    ACT.Copy)
                            last.then_inc(vhi_done, 1)
                        if valid(n, 1):
                            act.wait_ge(exp_done, n)
                            wait(act, pv_done, n - 2)
                            act.activation(p_hi[:, 1 - u], e_buf[:, 1 - u], ACT.Copy).then_inc(phi_done, 1)
                        if valid(n, 0):
                            act.wait_ge(t2_done, n + 1)
                            act.activation(q_t2[:, u].rearrange("p c q -> p (c q)"), ps[:, 4, 256:512].bitcast(F16),
                                           ACT.Copy).then_inc(q2_ready, 1)
                        if valid(n, -2):
                            act.wait_ge(r_done, n + 3)
                            act.activation(q_rows[:, u, :, 0:16].rearrange("p h (r d) -> p h r d", r=2),
                                           rot[:, u, 0].unsqueeze(2).broadcast_to([128, HEADS, 2, HD]), ACT.Copy)
                            act.activation(k_rows[:, u].rearrange("p h (r d) -> p h r d", d=HD)[:, :, 0:3:2, :],
                                           rot[:, u, 1].unsqueeze(2).broadcast_to([128, HEADS, 2, HD]), ACT.Copy)\
                                .then_inc(hi_done, 1)

                    steps(act, body)

                @block.gpsimd
                def _(pool):
                    def body(n, it, u):
                        if valid(n, -2):
                            pool.wait_ge(rope_done, n + 3)
                            wait(pool, hi_done, n + 1)
                            last = pool.tensor_tensor(
                                rot[:, u].rearrange("p a h (s d) -> p (a h) s d", s=2),
                                ta[:, u].rearrange("p a h (s d) -> p (a h) s d", s=2),
                                tb[:, u].rearrange("p a h (s d) -> p (a h) s d", s=2)[:, :, ::-1, :], ALU.add)
                            last.then_inc(r_done, 1)
                        if valid(n, 1):
                            pool.wait_ge(phi_done, n)
                            pool.tensor_tensor(p_lo[:, 1 - u], e_buf[:, 1 - u], p_hi[:, 1 - u], ALU.subtract)\
                                .then_inc(plo_done, 1)
                        if valid(n, -2):
                            pool.wait_ge(hi_done, n + 3)
                            pool.tensor_tensor(q_rows[:, u, :, 16:24], rot[:, u, 0], q_rows[:, u, :, 0:8], ALU.subtract)
                            pool.tensor_tensor(k_rows[:, u, :, 8:16], rot[:, u, 1], k_rows[:, u, :, 0:8], ALU.subtract)\
                                .then_inc(lo_done, 1)

                    steps(pool, body)

        until_mlp.close()
        x2_all = sb("x2_all", [128, B, NWIN, WTOK])
        a_ready = sem("a_ready")
        a_turned = sem("a_turned")
        at_act = sem("at_act")
        at_dve = sem("at_dve")
        xb_ready = sem("xb_ready")
        prj_done = sem("prj_done")
        x1_ready = sem("x1_ready")
        l2_stats = sem("l2_stats")
        l2_pool = sem("l2_pool")
        l2_rstd = sem("l2_rstd")
        l2_norm = sem("l2_norm")
        l2_hi = sem("l2_hi")
        l2_lo = sem("l2_lo")
        l2_turned = sem("l2_turned")
        l2_ready = sem("l2_ready")
        gate_done = sem("gate_done")
        up_done = sem("up_done")
        silu_done = sem("silu_done")
        h_done = sem("h_done")
        h_used = sem("h_used")
        mlp_done = sem("mlp_done")
        x2_done = sem("x2_done")
        with ExitStack() as st:
            def tmp(name, shape, dt=F32):
                return st.enter_context(nc.sbuf_tensor(name, shape, dt))

            a_s = tmp("a_s", [128, 2, TPC, 2, 64])
            a_t = tmp("a_t", [64, 2, 2, 2 * TPC, 64])
            xb = tmp("xb", [128, 2, TPC, DIM])
            x1 = tmp("x1", [128, 2, TPC, DIM])
            stats = tmp("stats2", [128, 2, TPC, 6])
            mv = tmp("mv2", [128, 2, TPC, 2])
            veps = tmp("veps2", [128, 2, TPC])
            rstd = tmp("rstd2", [128, 2, TPC])
            nmean = tmp("nmean2", [128, 2, TPC])
            nmr = tmp("nmr2", [128, 2, TPC])
            yn = tmp("yn", [128, 2, CHUNK])
            yh = tmp("yh", [128, 2, CHUNK], F16)
            yl = tmp("yl", [128, 2, CHUNK], F16)
            y_t = tmp("y_t", [128, 2, 2, CHUNK], F16)
            sg = tmp("sg", [128, 2, CHUNK])
            hid = tmp("hid", [128, 2, CHUNK])
            wait_here = tmp("wait_here", [128, 1])

            def steps(eng, body):
                body(0, 0, True, False)
                body(1, 1, True, True)
                with eng.Fori(1, CHUNKS // 2) as it:
                    for u in range(2):
                        body(it * 2 + u, u, True, True)
                body(CHUNKS, 0, False, True)

            with nc.Block() as block:
                @block.gpsimd
                def _(pool):
                    pool.wait_ge(norm_done, PAIRS)

                    def body(c, u, front, back):
                        if not front:
                            return
                        wait(pool, a_turned, c - 1)
                        pool.tensor_copy(a_s[:, u].rearrange("p t e d -> p (t e d)"),
                                         a_all[:, at(c * TPC, TPC)].rearrange("p t e h d -> p (t e h d)"))\
                            .then_inc(a_ready, 1)
                        wait(pool, x1_ready, c - 1)
                        pool.tensor_tensor(xb[:, u], x_all[:, at(c * TPC, TPC)],
                                           proj_b[:].unsqueeze(1).broadcast_to([128, TPC, DIM]), ALU.add).then_inc(xb_ready, 1)
                        pool.wait_ge(l2_stats, c * 2 + 2)
                        wait(pool, l2_norm, c - 1)
                        pool.tensor_tensor(veps[:, u, :], mv[:, u, :, 1], ln_const[:, 1, :], ALU.add).then_inc(l2_pool, 1)
                        pool.tensor_tensor(nmean[:, u, :], mv[:, u, :, 0], ln_const[:, 2, :], ALU.mult).then_inc(l2_pool, 1)
                        pool.wait_ge(l2_pool, c * 3 + 2)
                        pool.tensor_tensor(rstd[:, u, :], veps[:, u, :], ln_const[:, 0, :], ALU.pow).then_inc(l2_pool, 1)
                        pool.wait_ge(l2_pool, c * 3 + 3)
                        pool.tensor_tensor(nmr[:, u, :], nmean[:, u, :], rstd[:, u, :], ALU.mult).then_inc(l2_rstd, 1)
                        pool.wait_ge(l2_hi, c + 1)
                        wait(pool, l2_turned, c - 1)
                        pool.tensor_tensor(yl[:, u, :], yn[:, u, :], yh[:, u, :], ALU.subtract).then_inc(l2_lo, 1)

                    steps(pool, body)

                @block.tensor
                def _(pe):
                    pe.wait_ge(norm_done, PAIRS)

                    def fc1(c, u, k, bank, done):
                        for n, (ws, ys) in enumerate(((0, 0), (1, 0), (0, 1))):
                            last = pe.matmul(ps[:, bank, :], fc1_w16[:, ws, 128 * k:128 * k + 128], y_t[:, u, ys, :],
                                             start=(n == 0), stop=(n == 2))
                        last.then_inc(done, 1)

                    def fc2(c, k):
                        pe.wait_ge(h_done, c * HBLK + k + 1)
                        pe.matmul(ps[:, 7, :], fc2_ws[:, k, :], hid[:, k % 2, :], start=(k == 0), stop=False,
                                  skip_group_check=True).then_inc(h_used, 1)

                    def body(c, u, front, back):
                        if front:
                            pe.wait_ge(a_ready, c + 1)
                            wait(pe, at_act, c)
                            wait(pe, at_dve, c)
                            for k in range(2 * TPC):
                                last = pe.matmul(ps[0:64, k // 4, 128 * (k % 4):128 * (k % 4) + 128],
                                                 a_s[:, u, k // 2, k % 2, :], ident[:], start=(k % 4 == 0), stop=True,
                                                 skip_group_check=True)
                            last.then_inc(a_turned, 1)
                        if back:
                            b = c - 1
                            v = 1 - u
                            for k in range(HBLK):
                                if k == 0:
                                    pe.wait_ge(l2_ready, b + 1)
                                wait(pe, silu_done, b * HBLK + (k - 1) if not isinstance(b, int) or b * HBLK + k > 1 else 0)
                                fc1(b, v, HBLK + k, 3 + 2 * (k % 2), gate_done)
                                wait(pe, h_done, b * HBLK + (k - 1) if not isinstance(b, int) or b * HBLK + k > 1 else 0)
                                fc1(b, v, k, 4 + 2 * (k % 2), up_done)
                                if k == 1:
                                    wait(pe, x2_done, b)
                                if k >= 1:
                                    fc2(b, k - 1)
                        if front:
                            pe.wait_ge(at_act, c + 1)
                            pe.wait_ge(at_dve, c + 1)
                            wait(pe, l2_ready, c)
                            for k in range(TPC):
                                for r in range(2):
                                    last = pe.matmul(ps[:, 2, 128 * k:128 * k + 128],
                                                     a_t[:, u, r, 2 * k:2 * k + 2, :],
                                                     proj_w[:, r, :], start=(k == 0 and r == 0), stop=(r == 1),
                                                     skip_group_check=True)
                            last.then_inc(prj_done, 1)
                        if back:
                            b = c - 1
                            v = 1 - u
                            fc2(b, HBLK - 1)
                            for k in range(TPC):
                                last = pe.matmul(ps[:, 7, 128 * k:128 * k + 128], x1[:, v, k, :], ident[:], start=False,
                                                 stop=True, skip_group_check=True)
                            last.then_inc(mlp_done, 1)
                        if front:
                            pe.wait_ge(l2_lo, c + 1)
                            out = ps[:, 2, :].bitcast(F16).rearrange("p (s t q) -> p s t q", s=2, t=TPC)
                            for s, src in enumerate((yh, yl)):
                                for k in range(TPC):
                                    last = pe.transpose(out[:, s, k, :], src[:, u, 128 * k:128 * k + 128], ident16[:])
                            last.then_inc(l2_turned, 1)

                    steps(pe, body)

                @block.vector
                def _(dve):
                    def body(c, u, front, back):
                        if front:
                            dve.wait_ge(a_turned, c + 1)
                            wait(dve, prj_done, c - 1)
                            dve.tensor_copy(a_t[:, u, :, 0:TPC, :], ps[0:64, 0, :].rearrange("p (k r q) -> p r k q", r=2, q=64))\
                                .then_inc(at_dve, 1)
                        if back:
                            b = c - 1
                            for k in range(HBLK):
                                dve.wait_ge(up_done, b * HBLK + k + 1)
                                dve.wait_ge(silu_done, b * HBLK + k + 1)
                                if k >= 2 or not isinstance(b, int) or b > 0:
                                    dve.wait_ge(h_used, b * HBLK + k - 1)
                                dve.scalar_tensor_tensor(out=hid[:, k % 2, :], in0=ps[:, 4 + 2 * (k % 2), :],
                                                         scalar=fc1_bias[:, k:k + 1], in1=sg[:, k % 2, :], op0=ALU.add,
                                                         op1=ALU.mult).then_inc(h_done, 1)
                        if front:
                            dve.wait_ge(prj_done, c + 1)
                            dve.wait_ge(xb_ready, c + 1)
                            wait(dve, mlp_done, c - 1)
                            dve.tensor_tensor(x1[:, u].rearrange("p t q -> p (t q)"), ps[:, 2, :],
                                              xb[:, u].rearrange("p t q -> p (t q)"), ALU.add).then_inc(x1_ready, 1)
                            dve.wait_ge(x1_ready, c + 1)
                            wait(dve, l2_rstd, c - 1)
                            for k in range(TPC):
                                last = dve.bn_stats(stats[:, u, k, :], x1[:, u, k, :])
                            last.then_inc(l2_stats, 1)
                            dve.wait_ge(l2_stats, c * 2 + 1)
                            dve.memset(wait_here[:], 0.0)
                            for k in range(TPC):
                                last = dve.bn_aggr(mv[:, u, k, :], stats[:, u, k, :])
                            last.then_inc(l2_stats, 1)
                            dve.wait_ge(l2_rstd, c + 1)
                            wait(dve, l2_lo, c - 1)
                            for k in range(TPC):
                                last = dve.tensor_scalar(yn[:, u, 128 * k:128 * k + 128], x1[:, u, k, :],
                                                         rstd[:, u, k:k + 1], nmr[:, u, k:k + 1], ALU.mult, ALU.add)
                            last.then_inc(l2_norm, 1)
                            dve.wait_ge(l2_turned, c + 1)
                            dve.tensor_copy(y_t[:, u].rearrange("p s q -> p (s q)"), ps[:, 2, :].bitcast(F16))\
                                .then_inc(l2_ready, 1)

                    steps(dve, body)

                @block.scalar
                def _(act):
                    def body(c, u, front, back):
                        if front:
                            act.wait_ge(a_turned, c + 1)
                            wait(act, prj_done, c - 1)
                            act.activation(a_t[:, u, :, TPC:2 * TPC, :],
                                           ps[0:64, 1, :].rearrange("p (k r q) -> p r k q", r=2, q=64), ACT.Copy).then_inc(at_act, 1)
                        if back:
                            b = c - 1
                            for k in range(HBLK):
                                act.wait_ge(gate_done, b * HBLK + k + 1)
                                if k >= 2 or not isinstance(b, int) or b > 0:
                                    act.wait_ge(h_done, b * HBLK + k - 1)
                                act.activation(sg[:, k % 2, :], ps[:, 3 + 2 * (k % 2), :], ACT.Silu,
                                               bias=fc1_bias[:, HBLK + k:HBLK + k + 1], scale=1.0 / WSCALE)\
                                    .then_inc(silu_done, 1)
                        if front:
                            act.wait_ge(l2_norm, c + 1)
                            wait(act, l2_turned, c - 1)
                            act.activation(yh[:, u, :], yn[:, u, :], ACT.Copy).then_inc(l2_hi, 1)
                        if back:
                            b = c - 1
                            act.wait_ge(mlp_done, b + 1)
                            act.activation(x2_all[:, :, at(b * 2, 2), :],
                                           ps[:, 7, :].rearrange("p (w b q) -> p b w q", w=2, b=B),
                                           ACT.Identity, bias=cols[:, 0:1], scale=1.0).then_inc(x2_done, 1)

                    steps(act, body)

        xs_ready = sem("xs_ready")
        fg_done = sem("fg_done")
        fg_f32 = sem("fg_f32")
        fg_hi = sem("fg_hi")
        fg_ready = sem("fg_ready")
        v_done = sem("v_done")
        v_ready = sem("v_ready")
        s4_done = sem("s4_done")
        max4_done = sem("max4_done")
        mt_done = sem("mt_done")
        mrow_tmp = sem("mrow_tmp")
        mrow_ready = sem("mrow_ready")
        st4_done = sem("st4_done")
        exp4_done = sem("exp4_done")
        sum_done = sem("sum_done")
        pv4_done = sem("pv4_done")
        den_done = sem("den_done")
        rden_done = sem("rden_done")
        scaled_done = sem("scaled_done")
        o_ready = sem("o_ready")
        stored = [sem(f"stored{u}") for u in range(2)]
        pads_set = sem("pads_set")
        KR = 97
        with ExitStack() as st:
            def tmp(name, shape, dt=F32):
                return st.enter_context(nc.sbuf_tensor(name, shape, dt))

            xs = tmp("xs", [128, NB])
            fg = tmp("fg", [64, 2, NB])
            fgh = tmp("fgh", [64, 2, NB], F16)
            f_rows = tmp("f_rows", [128, NB], F16)
            g_rows = tmp("g_rows", [128, NB], F16)
            val = tmp("val", [128, BT, DIM])
            mx = tmp("mx4", [128, BT])
            mtmp = tmp("mtmp", [128, NB], F16)
            e4 = tmp("e4", [128, 3, NB])
            acc = tmp("acc", [128, 2, NB])
            rden = tmp("rden", [128, NB])
            o4 = tmp("o4", [128, NB])
            ob = tmp("ob", [128, 2, NB])

            def batches(eng, body):
                with eng.Fori(0, B // 2) as it:
                    for u in range(2):
                        body(it * 2 + u, it, u)

            with nc.Block() as block:
                @block.gpsimd
                def _(pool):
                    pool.memset(f_rows[64:128, :], 0.0).then_inc(pads_set, 1)
                    pool.memset(g_rows[64:128, :], 0.0).then_inc(pads_set, 1)
                    pool.wait_ge(pads_set, 2)
                    for r in (64, 96):
                        pool.memset(g_rows[r:r + 1, :], MSCALE).then_inc(pads_set, 1)
                    pool.wait_ge(pads_set, 4)
                    pool.wait_ge(x2_done, CHUNKS)
                    pool.sem_inc(o_ready, 1)

                    def body(b, it, u):
                        pool.wait_ge(o_ready, b + 1)
                        pool.tensor_copy(xs[:], x2_all[:, at(b, 1)].rearrange("p a w q -> p (a w q)")).then_inc(xs_ready, 1)
                        for k in range(1, BT):
                            pool.wait_ge(exp4_done, b * BT + k + 1)
                            a = e4[:, 0, :] if False else None
                            pool.wait_ge(sum_done, b * BT + k)
                            pool.tensor_tensor(acc[:, k % 2, :], acc[:, (k + 1) % 2, :], e4[:, k % 3, :], ALU.add)\
                                .then_inc(sum_done, 1)

                    batches(pool, body)

                @block.tensor
                def _(pe):
                    pe.wait_ge(pads_set, 4)

                    def body(b, it, u):
                        pe.wait_ge(xs_ready, b + 1)
                        for k in range(2):
                            for n in range(2):
                                last = pe.matmul(ps[0:64, 2 * k + n, :], fg_w[:, k, :], xs[:, 512 * n:512 * n + 512],
                                                 start=True, stop=True)
                            last.then_inc(fg_done, 1)
                        for n in range(BT):
                            last = pe.matmul(ps[:, 4 + n // 4, 128 * (n % 4):128 * (n % 4) + 128],
                                             xs[:, 128 * n:128 * n + 128], wv[:], start=(n % 4 == 0), stop=True,
                                             skip_group_check=True)
                        last.then_inc(v_done, 1)
                        pe.wait_ge(v_ready, b + 1)
                        pe.wait_ge(fg_ready, b * 2 + 2)
                        for n in range(BT):
                            if n >= 2:
                                pe.wait_ge(max4_done, b * BT + n - 1)
                            for m in range(2):
                                last = pe.matmul(ps[:, 4 + 2 * (n % 2) + m, :], f_rows[0:64, 128 * n:128 * n + 128],
                                                 g_rows[0:64, 512 * m:512 * m + 512], start=True, stop=True)
                            last.then_inc(s4_done, 1)
                        pe.wait_ge(max4_done, b * BT + BT)
                        for n in range(BT):
                            last = pe.matmul(ps[64:128, n // 4, 128 * (n % 4):128 * (n % 4) + 128],
                                             mx[:, n:n + 1].broadcast_to([128, 64]), ident[:], start=(n % 4 == 0),
                                             stop=True, skip_group_check=True)
                        last.then_inc(mt_done, 1)
                        pe.wait_ge(mrow_ready, b * 2 + 2)

                        def pv(m):
                            pe.wait_ge(exp4_done, b * BT + m + 1)
                            for k in range(2):
                                last = pe.matmul(ps[:, 2 + k, :], val[:, m, :], e4[:, m % 3, 512 * k:512 * k + 512],
                                                 start=(m == 0), stop=(m == BT - 1))
                            last.then_inc(pv4_done, 1)

                        for m in range(BT):
                            if m >= 2:
                                pe.wait_ge(exp4_done, b * BT + m - 1)
                            for k in range(2):
                                last = pe.matmul(ps[:, 4 + 2 * (m % 2) + k, :], g_rows[0:KR, 128 * m:128 * m + 128],
                                                 f_rows[0:KR, 512 * k:512 * k + 512], start=True, stop=True)
                            last.then_inc(st4_done, 1)
                            if m >= 1:
                                pv(m - 1)
                        pv(BT - 1)
                        pe.wait_ge(sum_done, b * BT + BT)
                        for k in range(2):
                            last = pe.matmul(ps[:, k, :], ones[:], acc[:, (BT - 1) % 2, 512 * k:512 * k + 512],
                                             start=True, stop=True)
                        last.then_inc(den_done, 1)

                    batches(pe, body)

                @block.vector
                def _(dve):
                    def body(b, it, u):
                        for k, rows in ((0, f_rows), (1, g_rows)):
                            dve.wait_ge(fg_f32, b * 2 + k + 1)
                            dve.tensor_copy(fgh[:, k, :], fg[:, k, :]).then_inc(fg_hi, 1)
                            dve.wait_ge(fg_hi, b * 2 + k + 1)
                            dve.scalar_tensor_tensor(out=rows[0:64, :], in0=fgh[:, k, :], scalar=fg_b[:, 2 + k:3 + k],
                                                     in1=fg[:, k, :], op0=ALU.mult, op1=ALU.add).then_inc(fg_ready, 1)
                        for n in range(BT):
                            dve.wait_ge(s4_done, b * BT + n + 1)
                            dve.tensor_reduce(mx[:, n:n + 1],
                                              ps[:, 4 + 2 * (n % 2):6 + 2 * (n % 2), :].rearrange("p a b -> p (a b)"),
                                              AX.X, ALU.max).then_inc(max4_done, 1)
                        dve.wait_ge(mt_done, b + 1)
                        m64 = ps[64:65, 0:2, :].rearrange("p a b -> p (a b)")
                        m96 = ps[96:97, 0:2, :].rearrange("p a b -> p (a b)")
                        dve.tensor_scalar(mtmp[96:97, :], m96, -1.0 / MSCALE, None, ALU.mult).then_inc(mrow_tmp, 1)
                        dve.tensor_scalar(f_rows[64:65, :], m64, -1.0 / MSCALE, None, ALU.mult).then_inc(mrow_ready, 1)
                        dve.wait_ge(mrow_tmp, b + 1)
                        dve.scalar_tensor_tensor(out=f_rows[96:97, :], in0=m96, scalar=-1.0 / MSCALE,
                                                 in1=mtmp[96:97, :], op0=ALU.mult, op1=ALU.subtract)\
                            .then_inc(mrow_ready, 1)
                        dve.wait_ge(exp4_done, b * BT + 1)
                        dve.tensor_copy(acc[:, 0, :], e4[:, 0, :]).then_inc(sum_done, 1)
                        dve.wait_ge(den_done, b + 1)
                        dve.reciprocal(rden[:], ps[:, 0:2, :].rearrange("p a b -> p (a b)")).then_inc(rden_done, 1)
                        dve.wait_ge(rden_done, b + 1)
                        dve.wait_ge(pv4_done, b * BT + BT)
                        dve.tensor_tensor(o4[:], ps[:, 2:4, :].rearrange("p a b -> p (a b)"), rden[:], ALU.mult)\
                            .then_inc(scaled_done, 1)
                        dve.wait_ge(scaled_done, b * 2 + 1)
                        dve.tensor_scalar(rden[:], o4[:], cols[:, 2:3], cols[:, 1:2], ALU.add, ALU.mult)\
                            .then_inc(scaled_done, 1)
                        dve.wait_ge(scaled_done, b * 2 + 2)
                        dve.wait_ge(stored[u], it * 16 + 16)
                        dve.tensor_tensor(ob[:, u, :], rden[:], xs[:], ALU.add).then_inc(o_ready, 1)

                    batches(dve, body)

                @block.scalar
                def _(act):
                    def body(b, it, u):
                        for k in range(2):
                            act.wait_ge(fg_done, b * 2 + k + 1)
                            act.activation(fg[:, k, :], ps[0:64, 2 * k:2 * k + 2, :].rearrange("p a b -> p (a b)"),
                                           ACT.Identity, bias=fg_b[:, k:k + 1], scale=1.0).then_inc(fg_f32, 1)
                        act.wait_ge(v_done, b + 1)
                        act.activation(val[:].rearrange("p n d -> p (n d)"), ps[:, 4:6, :].rearrange("p a b -> p (a b)"),
                                       ACT.Copy).then_inc(v_ready, 1)
                        for m in range(BT):
                            act.wait_ge(st4_done, b * BT + m + 1)
                            if m >= 3:
                                act.wait_ge(pv4_done, b * BT + m - 2)
                                act.wait_ge(sum_done, b * BT + m - 2)
                            act.activation(e4[:, m % 3, :], ps[:, 4 + 2 * (m % 2):6 + 2 * (m % 2), :]
                                           .rearrange("p a b -> p (a b)"), ACT.Exp).then_inc(exp4_done, 1)

                    batches(act, body)

                @block.sync
                def _(sp):
                    for u in range(2):
                        sp.sem_inc(stored[u], 16)

                    def body(b, it, u):
                        sp.wait_ge(o_ready, b + 2)
                        sp.dma_start(t["out"][at(b, 1)].rearrange("a p n -> (a p) n"), ob[:, u, :]).then_inc(stored[u], 16)

                    batches(sp, body)
                    for u in range(2):
                        sp.wait_ge(stored[u], 16 * (B // 2 + 1))


def _rope_tables():
    d1 = HD // 4
    inv = (10000.0 ** (-(np.arange(d1, dtype=np.float32) / d1))).astype(np.float32)
    pos = np.arange(WIN, dtype=np.float32)
    ang = pos[:, None] * inv
    rows = np.broadcast_to(ang[:, None, :], (WIN, WIN, d1)).reshape(WTOK, d1)
    cols = np.broadcast_to(ang[None, :, :], (WIN, WIN, d1)).reshape(WTOK, d1)
    a = np.concatenate([rows, cols], 1).astype(np.float32)
    cos, sin = np.cos(a), np.sin(a)
    c = np.concatenate([cos, cos], 1)
    s = np.concatenate([sin, -sin], 1)
    table = np.stack([c, s]) / WSCALE
    both = np.stack([table * HD ** -0.5, table], 2)
    both = np.concatenate([both, both], 1)
    return np.ascontiguousarray(both.transpose(1, 0, 2, 3)).astype(np.float32)


def kernel(**inputs):
    import concourse.bacc as bacc
    from concourse.bass_utils import run_bass_kernel_spmd

    def a(name):
        return np.asarray(inputs[name])

    def L0(name):
        return a("L0_conv_" + name)

    def L1(name):
        return a("L1_conv_" + name)

    x = np.roll(a("x"), (-SHIFT, -SHIFT), (1, 2))
    nh, nw = H // WIN, W // WIN
    x = x.reshape(B, nh, WIN, nw, WIN, DIM).transpose(1, 3, 0, 2, 4, 5).reshape(PAIRS, 2 * WTOK, DIM)
    ch = np.arange(DIM).reshape(2, 2, 4, HD).transpose(1, 2, 0, 3).reshape(DIM)
    order = np.concatenate([np.arange(2 * DIM), 2 * DIM + ch])
    qkv_w, qkv_b = L0("qkv_w")[order], L0("qkv_b")[order]
    proj = L0("proj_w")[:, ch].T.reshape(2, 64, DIM).transpose(1, 0, 2)
    mask = L0("attn_mask")
    both = np.stack([mask.transpose(1, 0, 2), mask.transpose(2, 0, 1)], 1)
    fc1_b = L0("fc1_b").reshape(2 * HBLK, 128).T
    zero = np.zeros(DIM, np.float32)
    lo_f = np.repeat(np.array([0, 0, -1, -1], np.float32), CQK)
    lo_g = np.repeat(np.array([0, -1, 0, -1], np.float32), CQK)
    sel = np.zeros((33, 128), np.float16)
    sel[0], sel[32] = 1, 1
    data = {
        "x": x.transpose(1, 0, 2),
        "qkv_w": qkv_w.T,
        "qkv_b": np.broadcast_to(qkv_b, (33, 3 * DIM)),
        "g1b1": np.stack([L0("norm1_g"), L0("norm1_b"), L0("norm2_g"), L0("norm2_b")], 1),
        "ident16": np.eye(128, dtype=np.float16),
        "ident": np.eye(128, dtype=np.float32),
        "sel33": sel,
        "rope": _rope_tables(),
        "mask": np.concatenate([both, both], 0),
        "identb": np.eye(128, dtype=np.float32).astype(mybir.dt.np(mybir.dt.bfloat16)),
        "proj_w": proj,
        "proj_b": np.broadcast_to(L0("proj_b"), (128, DIM)),
        "fc1_w": L0("fc1_w").T,
        "fc1_b": fc1_b,
        "fc2_w": L0("fc2_w").T.reshape(HBLK, 128, DIM).transpose(1, 0, 2),
        "cols": np.stack([L0("fc2_b"), np.broadcast_to(L1("gamma"), (DIM,)), L1("bv"), zero], 1),
        "fg_w": np.stack([np.tile(L1("Wq"), (1, 4)), np.tile(L1("Wk"), (1, 4))], 1),
        "fg_b": np.stack([np.tile(L1("bq"), 4), np.tile(L1("bk"), 4), lo_f, lo_g], 1),
        "wv": L1("Wv"),
        "ln_const": np.broadcast_to(np.array([-0.5, EPS, -1], np.float32)[:, None], (128, 3, TPC)),
        "ones": np.ones((128, 128), np.float32),
    }
    nc = bacc.Bacc("TRN2", target_bir_lowering=False, num_devices=1)
    arrays, t = {}, {}
    for name, v in data.items():
        v = np.ascontiguousarray(v)
        arrays["in_" + name] = v
        t[name] = nc.dram_tensor("in_" + name, v.shape, mybir.dt.from_np(v.dtype), kind="ExternalInput").ap()
    t["out"] = nc.dram_tensor("out", (B, DIM, NB), F32, kind="ExternalOutput").ap()
    build(nc, t)
    got = run_bass_kernel_spmd(nc, [arrays], core_ids=[0]).results[0]["out"]
    y = np.asarray(got).reshape(B, DIM, nh, nw, WIN, WIN).transpose(0, 2, 4, 3, 5, 1).reshape(B, H, W, DIM)
    return np.roll(y, (SHIFT, SHIFT), (1, 2))
```

```python
from contextlib import ExitStack

import concourse.bass as bass
import numpy as np
from concourse import mybir

F32 = mybir.dt.float32
F16 = mybir.dt.float16
BF16 = mybir.dt.bfloat16
ALU = mybir.AluOpType
ACT = mybir.ActivationFunctionType
AX = mybir.AxisListType

B, H, W, DIM = 4, 32, 32, 128
WIN, SHIFT = 8, 4
HEADS, HD = 16, 8
NWIN = (H // WIN) * (W // WIN)
WTOK = WIN * WIN
PAIRS = NWIN * B // 2
TOK = B * H * W
CHUNK = 512
CHUNKS = TOK // CHUNK
TPC = CHUNK // 128
HIDDEN = 4 * DIM
HBLK = HIDDEN // 128
CQK = DIM // 8
NB = H * W
BT = NB // 128
EPS = 1e-5
WSCALE = 64.0
MSCALE = 256.0
RSCALE = 1024.0
ROWS = 32
HP = HEADS // 2
MAXROW = 3 * HD


def at(start, size):
    return bass.ds(start, size)


def build(nc, t):
    ctx = ExitStack()
    with ctx:
        def sb(name, shape, dt=F32):
            return ctx.enter_context(nc.sbuf_tensor(name, shape, dt))

        def sem(name):
            return ctx.enter_context(nc.semaphore(name))

        qkv_w = sb("qkv_w", [128, 3 * DIM])
        qkv_b = sb("qkv_b", [33, 3 * DIM])
        g1b1 = sb("g1b1", [128, 4])
        w_scaled = sb("w_scaled", [128, 2 * HIDDEN])
        qkv_w16 = sb("qkv_w16", [128, 2, 3 * DIM], F16)
        qkv_b16 = sb("qkv_b16", [33, 3 * DIM], F16)
        sel33 = sb("sel33", [33, 128], F16)
        rope = sb("rope", [128, 2, 2, HD])
        ident = sb("ident", [128, 128])
        ident16 = sb("ident16", [128, 128], F16)
        identb = sb("identb", [128, 128], BF16)
        proj_w = sb("proj_w", [128, DIM])
        proj_ws = sb("proj_ws", [128, DIM])
        proj_w16 = sb("proj_w16", [128, 2, DIM], F16)
        proj_b = sb("proj_b", [128, DIM])
        fc1_w = sb("fc1_w", [128, 2 * HIDDEN])
        fc1_w16 = sb("fc1_w16", [128, 2, 2 * HIDDEN], F16)
        fc1_b = sb("fc1_b", [128, 2 * HBLK])
        fc1_bias = sb("fc1_bias", [128, 2 * HBLK])
        fc2_w = sb("fc2_w", [128, HBLK, DIM])
        fc2_ws = sb("fc2_ws", [128, HBLK, DIM])
        cols = sb("cols", [128, 4])
        fg_w = sb("fg_w", [128, 2, 64])
        fg_b = sb("fg_b", [64, 4])
        wv = sb("wv", [128, DIM])
        ln_const = sb("ln_const", [128, 3, TPC])
        ones = sb("ones", [128, 128])
        mask_f = sb("mask_f", [128, 2, NWIN, WTOK])
        mask16 = sb("mask16", [128, 3, 2, NWIN, WTOK], BF16)
        mask_max = sb("mask_max", [128, 1])
        mask_any = sb("mask_any", [128, 1])

        x_all = sb("x_all", [128, PAIRS, DIM])
        a_all = sb("a_all", [128, PAIRS, 2, HP, HD])
        until_mlp = ExitStack()
        xn_all = until_mlp.enter_context(nc.sbuf_tensor("xn_all", [128, PAIRS, 2, 128], F16))
        v_hi = until_mlp.enter_context(nc.sbuf_tensor("v_hi", [128, 2, HP, 2, 2, HD + 1], F16))
        v_lo = until_mlp.enter_context(nc.sbuf_tensor("v_lo", [128, 2, HP, 2, 2, HD + 1], F16))

        ps = ctx.enter_context(nc.psum_tensor("ps", [128, 8, 512], F32))

        loaded = sem("loaded")
        x_loaded = [sem(f"x_loaded{c}") for c in range(CHUNKS)]
        prep_dve = sem("prep_dve")
        prep_proj = sem("prep_proj")
        prep_pe = sem("prep_pe")
        prep_pool = sem("prep_pool")
        ln_stats = sem("ln_stats")
        ln_pool = sem("ln_pool")
        ln_rstd = sem("ln_rstd")
        ln_norm = sem("ln_norm")
        ln_hi = sem("ln_hi")
        ln_lo = sem("ln_lo")
        ln_turned = sem("ln_turned")
        ln_ready = sem("ln_ready")

        qk_done = sem("qk_done")
        v_done = sem("v_done")
        rope_done = sem("rope_done")
        vhi_done = sem("vhi_done")
        vlo_done = sem("vlo_done")
        r_done = sem("r_done")
        hi_done = sem("hi_done")
        lo_done = sem("lo_done")
        t1_done = sem("t1_done")
        qt_ready = sem("qt_ready")
        kd_ready = sem("kd_ready")
        ka_ready = sem("ka_ready")
        s_done = sem("s_done")
        max_done = sem("max_done")
        mhi_done = sem("mhi_done")
        mlo_done = sem("mlo_done")
        t2_done = sem("t2_done")
        q2_ready = sem("q2_ready")
        st_done = sem("st_done")
        exp_done = sem("exp_done")
        phi_done = sem("phi_done")
        plo_done = sem("plo_done")
        pv_done = sem("pv_done")
        rec_done = sem("rec_done")
        norm_done = sem("norm_done")

        def wait(eng, s, value):
            if not isinstance(value, int) or value > 0:
                eng.wait_ge(s, value)

        N_LOADS = 20
        with ExitStack() as st:
            def tmp(name, shape, dt=F32):
                return st.enter_context(nc.sbuf_tensor(name, shape, dt))

            stats = tmp("stats", [128, 2, TPC, 6])
            mv = tmp("mv", [128, 2, TPC, 2])
            veps = tmp("veps", [128, 2, TPC])
            rstd = tmp("rstd", [128, 2, TPC])
            nmean = tmp("nmean", [128, 2, TPC])
            nmr = tmp("nmr", [128, 2, TPC])
            xn = tmp("xn", [128, 2, CHUNK])
            xh = tmp("xh", [128, 2, CHUNK], F16)
            xl = tmp("xl", [128, 2, CHUNK], F16)
            mrest = tmp("mrest", [128, 2, NWIN, WTOK])

            with nc.Block() as block:
                @block.sync
                def _(sp):
                    for c in range(CHUNKS):
                        sp.dma_start(x_all[:, TPC * c:TPC * c + TPC, :],
                                     t["x"][:, TPC * c:TPC * c + TPC, :]).then_inc(x_loaded[c], 16)
                        if c == 0:
                            for dst, name in ((qkv_w, "qkv_w"), (qkv_b, "qkv_b"), (g1b1, "g1b1"), (ident16, "ident16"),
                                              (ident, "ident"), (sel33, "sel33")):
                                sp.dma_start(dst[:], t[name]).then_inc(loaded, 16)
                    for dst, name in ((rope, "rope"), (mask_f, "mask"), (identb, "identb"), (proj_w, "proj_w"),
                                      (proj_b, "proj_b"), (fc1_w, "fc1_w"), (fc1_b, "fc1_b"), (fc2_w, "fc2_w"),
                                      (cols, "cols"), (fg_w, "fg_w"), (fg_b, "fg_b"), (wv, "wv"), (ln_const, "ln_const"),
                                      (ones, "ones")):
                        sp.dma_start(dst[:], t[name]).then_inc(loaded, 16)

                @block.vector
                def _(dve):
                    def norm(c):
                        dve.wait_ge(ln_rstd, c + 1)
                        if c >= 2:
                            dve.wait_ge(ln_lo, c - 1)
                            dve.wait_ge(ln_hi, c - 1)
                        for k in range(TPC):
                            last = dve.tensor_scalar(xn[:, c % 2, 128 * k:128 * k + 128], x_all[:, TPC * c + k, :],
                                                     rstd[:, c % 2, k:k + 1], nmr[:, c % 2, k:k + 1], ALU.mult, ALU.add)
                        last.then_inc(ln_norm, 1)

                    def ready(c):
                        dve.wait_ge(ln_turned, c + 1)
                        dve.tensor_copy(xn_all[:, TPC * c:TPC * c + TPC].rearrange("p t s q -> p (t s q)"),
                                        ps[:, c % 2, :].bitcast(F16)).then_inc(ln_ready, 1)

                    for c in range(CHUNKS + 2):
                        if c < CHUNKS:
                            dve.wait_ge(x_loaded[c], 16)
                            if c >= 2:
                                dve.wait_ge(ln_rstd, c - 1)
                            for k in range(TPC):
                                last = dve.bn_stats(stats[:, c % 2, k, :], x_all[:, TPC * c + k, :])
                            last.then_inc(ln_stats, 1)
                            dve.wait_ge(ln_stats, 2 * c + 1)
                            for k in range(TPC):
                                last = dve.bn_aggr(mv[:, c % 2, k, :], stats[:, c % 2, k, :])
                            last.then_inc(ln_stats, 1)
                        if 1 <= c <= CHUNKS:
                            norm(c - 1)
                        if c >= 2:
                            ready(c - 2)
                    dve.wait_ge(loaded, 16 * N_LOADS)
                    dve.tensor_scalar(w_scaled[:, 0:3 * DIM], qkv_w[:], g1b1[:, 0:1], WSCALE, ALU.mult, ALU.mult)\
                        .then_inc(prep_dve, 1)
                    dve.wait_ge(prep_dve, 1)
                    dve.tensor_copy(qkv_w16[:, 0, :], w_scaled[:, 0:3 * DIM]).then_inc(prep_dve, 1)
                    dve.wait_ge(prep_dve, 2)
                    dve.tensor_tensor(qkv_w16[:, 1, :], w_scaled[:, 0:3 * DIM], qkv_w16[:, 0, :], ALU.subtract)\
                        .then_inc(prep_dve, 1)
                    dve.wait_ge(prep_pe, 1)
                    dve.wait_ge(prep_dve, 3)
                    dve.tensor_tensor(w_scaled[0:33, 0:3 * DIM], ps[0:33, 2, 0:3 * DIM], qkv_b[:], ALU.add)\
                        .then_inc(prep_dve, 1)
                    dve.wait_ge(prep_dve, 4)
                    dve.tensor_scalar(qkv_b16[:], w_scaled[0:33, 0:3 * DIM], WSCALE, None, ALU.mult)\
                        .then_inc(prep_dve, 1)
                    dve.wait_ge(prep_dve, 5)
                    dve.scalar_tensor_tensor(out=qkv_b16[32:33, :], in0=w_scaled[32:33, 0:3 * DIM], scalar=WSCALE,
                                             in1=qkv_b16[32:33, :], op0=ALU.mult, op1=ALU.subtract)\
                        .then_inc(prep_dve, 1)
                    dve.wait_ge(prep_dve, 6)
                    dve.tensor_scalar(w_scaled[:], fc1_w[:], g1b1[:, 2:3], WSCALE, ALU.mult, ALU.mult)\
                        .then_inc(prep_dve, 1)
                    dve.wait_ge(prep_dve, 7)
                    dve.tensor_copy(fc1_w16[:, 0, :], w_scaled[:]).then_inc(prep_dve, 1)
                    dve.wait_ge(prep_dve, 8)
                    dve.tensor_tensor(fc1_w16[:, 1, :], w_scaled[:], fc1_w16[:, 0, :], ALU.subtract)\
                        .then_inc(prep_dve, 1)
                    dve.wait_ge(prep_pe, 2)
                    dve.tensor_tensor(fc1_bias[:], ps[:, 3, 0:2 * HBLK], fc1_b[:], ALU.add).then_inc(prep_dve, 1)
                    dve.wait_ge(prep_dve, 10)
                    dve.tensor_scalar(fc1_bias[:, 0:HBLK], fc1_bias[:, 0:HBLK], WSCALE, None, ALU.mult)\
                        .then_inc(prep_dve, 1)
                    dve.tensor_scalar(fc2_ws[:], fc2_w[:], 1.0 / WSCALE, None, ALU.mult).then_inc(prep_dve, 1)
                    dve.tensor_scalar(proj_ws[:], proj_w[:], WSCALE, None, ALU.mult).then_inc(prep_proj, 1)
                    dve.wait_ge(prep_proj, 1)
                    dve.tensor_copy(proj_w16[:, 0, :], proj_ws[:]).then_inc(prep_proj, 1)
                    dve.wait_ge(prep_proj, 2)
                    dve.tensor_tensor(proj_w16[:, 1, :], proj_ws[:], proj_w16[:, 0, :], ALU.subtract).then_inc(prep_proj, 1)
                    m = mask_f[:]
                    dve.tensor_copy(mask16[:, 0], m).then_inc(prep_dve, 1)
                    dve.wait_ge(prep_dve, 13)
                    dve.tensor_tensor(mrest[:], m, mask16[:, 0], ALU.subtract).then_inc(prep_dve, 1)
                    dve.wait_ge(prep_dve, 14)
                    dve.tensor_copy(mask16[:, 1], mrest[:]).then_inc(prep_dve, 1)
                    dve.wait_ge(prep_dve, 15)
                    dve.tensor_tensor(mask16[:, 2], mrest[:], mask16[:, 1], ALU.subtract).then_inc(prep_dve, 1)
                    dve.wait_ge(prep_dve, 16)
                    dve.tensor_reduce(mask_max[:], mask16[:, 1, 0].rearrange("p w k -> p (w k)"), AX.X, ALU.max,
                                      apply_absolute_value=True).then_inc(prep_dve, 1)

                @block.gpsimd
                def _(pool):
                    pool.wait_ge(loaded, 16 * N_LOADS)
                    for c in range(CHUNKS):
                        pool.wait_ge(ln_stats, 2 * c + 2)
                        if c >= 2:
                            pool.wait_ge(ln_norm, c - 1)
                        pool.tensor_tensor(veps[:, c % 2, :], mv[:, c % 2, :, 1], ln_const[:, 1, :], ALU.add)\
                            .then_inc(ln_pool, 1)
                        pool.tensor_tensor(nmean[:, c % 2, :], mv[:, c % 2, :, 0], ln_const[:, 2, :], ALU.mult)\
                            .then_inc(ln_pool, 1)
                        pool.wait_ge(ln_pool, 3 * c + 2)
                        pool.tensor_tensor(rstd[:, c % 2, :], veps[:, c % 2, :], ln_const[:, 0, :], ALU.pow)\
                            .then_inc(ln_pool, 1)
                        pool.wait_ge(ln_pool, 3 * c + 3)
                        pool.tensor_tensor(nmr[:, c % 2, :], nmean[:, c % 2, :], rstd[:, c % 2, :], ALU.mult)\
                            .then_inc(ln_rstd, 1)
                        pool.wait_ge(ln_hi, c + 1)
                        if c >= 2:
                            pool.wait_ge(ln_turned, c - 1)
                        pool.tensor_tensor(xl[:, c % 2, :], xn[:, c % 2, :], xh[:, c % 2, :], ALU.subtract)\
                            .then_inc(ln_lo, 1)
                    pool.wait_ge(prep_dve, 17)
                    pool.partition_all_reduce(mask_any[:], mask_max[:], 128, bass.bass_isa.ReduceOp.max)\
                        .then_inc(prep_pool, 1)
                    pool.memset(v_hi[:], 0.0).then_inc(prep_pool, 1)
                    pool.memset(v_lo[:], 0.0).then_inc(prep_pool, 1)
                    pool.wait_ge(prep_pool, 3)
                    for e in range(2):
                        pool.memset(v_hi[64 * e:64 * e + 64, :, :, e, :, HD:HD + 1], WSCALE).then_inc(prep_pool, 1)

                @block.scalar
                def _(act):
                    for c in range(CHUNKS):
                        act.wait_ge(ln_norm, c + 1)
                        if c >= 2:
                            act.wait_ge(ln_turned, c - 1)
                            act.wait_ge(ln_lo, c - 1)
                        act.activation(xh[:, c % 2, :], xn[:, c % 2, :], ACT.Copy).then_inc(ln_hi, 1)

                @block.tensor
                def _(pe):
                    pe.wait_ge(loaded, 16 * N_LOADS)
                    for c in range(CHUNKS):
                        pe.wait_ge(ln_lo, c + 1)
                        if c >= 2:
                            pe.wait_ge(ln_ready, c - 1)
                        out = ps[:, c % 2, :].bitcast(F16).rearrange("p (t s q) -> p t s q", s=2, t=TPC)
                        for s, src in enumerate((xh, xl)):
                            for k in range(TPC):
                                last = pe.transpose(out[:, k, s, :], src[:, c % 2, 128 * k:128 * k + 128], ident16[:])
                        last.then_inc(ln_turned, 1)
                    pe.matmul(ps[0:33, 2, 0:3 * DIM], g1b1[:, 1:2].broadcast_to([128, 33]), qkv_w[:], start=True,
                              stop=True).then_inc(prep_pe, 1)
                    for k in range(2 * HBLK):
                        last = pe.matmul(ps[:, 3, k:k + 1], fc1_w[:, 128 * k:128 * k + 128], g1b1[:, 3:4],
                                         start=True, stop=True)
                    last.then_inc(prep_pe, 1)

        with ExitStack() as st:
            def tmp(name, shape, dt=F32):
                return st.enter_context(nc.sbuf_tensor(name, shape, dt))

            ta = tmp("ta", [128, 2, 2, HEADS, HD])
            tb = tmp("tb", [128, 2, 2, HEADS, HD])
            rot = tmp("rot", [128, 2, 2, HEADS, HD])
            q_rows = tmp("q_rows", [128, 2, HEADS, ROWS], F16)
            k_rows = tmp("k_rows", [128, 2, HEADS, ROWS], F16)
            q_t = tmp("q_t", [128, 2, 4, 128], F16)
            k_t = tmp("k_t", [128, 2, 4, 4, 128], F16)
            q_t2 = tmp("q_t2", [128, 2, 4, 128], F16)
            mx = tmp("mx", [128, 2, HEADS])
            e_buf = tmp("e_buf", [128, 2, HEADS, WTOK])
            p_hi = tmp("p_hi", [128, 2, HEADS, WTOK], F16)
            p_lo = tmp("p_lo", [128, 2, HEADS, WTOK], F16)
            rec = tmp("rec", [128, 2, HP, 2])
            rows_set = st.enter_context(nc.semaphore("rows_set"))

            S_BANK, ST_BANK, QKV_BANK, T1_BANK, T2_BANK, PV_BANK = 0, 2, 4, 5, 6, 7
            qkv_ps = ps[:, QKV_BANK, :]
            v_ps = ps[:, T2_BANK, 256:256 + DIM]
            t1_ps = ps[:, T1_BANK, :].bitcast(F16).rearrange("p (a c q) -> p a c q", a=2, c=4)
            t2_ps = ps[:, T2_BANK, 0:256].bitcast(F16).rearrange("p (c q) -> p c q", c=4)
            pv_ps = ps[:, PV_BANK, 0:HP * 4 * (HD + 1)].rearrange("p (h e r d) -> p h e r d", h=HP, e=2, r=2)

            FIRST, LAST = -2, PAIRS + 2
            LOOP_FROM, LOOP_TO = 4, PAIRS - 2

            def steps(eng, body):
                for n in range(FIRST, LOOP_FROM):
                    body(n, n // 2, n % 2)
                with eng.Fori(LOOP_FROM // 2, LOOP_TO // 2) as it:
                    for u in range(2):
                        body(it * 2 + u, it, u)
                for n in range(LOOP_TO, LAST + 1):
                    body(n, n // 2, n % 2)

            def valid(n, lag):
                return not isinstance(n, int) or 0 <= n - lag < PAIRS

            def turned_keys(copy, u, groups):
                for j in groups:
                    rows = slice(ROWS * j, ROWS * j + ROWS)
                    last = copy(k_t[rows, u, j], t1_ps[rows, 1])
                return last

            with nc.Block() as block:
                @block.tensor
                def _(pe):
                    pe.wait_ge(ln_ready, CHUNKS)
                    pe.wait_ge(prep_dve, 17)
                    pe.wait_ge(prep_pool, 5)
                    pe.wait_ge(rows_set, 4)

                    def project(out, i, cols):
                        for n, (xs, ws) in enumerate(((0, 0), (0, 1), (1, 0))):
                            pe.matmul(out, xn_all[:, at(i, 1), xs, :].rearrange("p a q -> p (a q)"),
                                      qkv_w16[:, ws, cols], start=(n == 0), stop=False, skip_group_check=True)
                        return pe.matmul(out, sel33[:], qkv_b16[:, cols], start=False, stop=True,
                                         skip_group_check=True)

                    def scores(bank, left, right, w, side, parts):
                        for part in range(parts):
                            for b in range(2):
                                mm = mask16[:, part, side, at(w, 1), :].broadcast_to([128, 8, WTOK])
                                pe.matmul(ps[:, bank + b, :].rearrange("p (h k) -> p h k", h=8), identb[:], mm,
                                          start=(part == 0), stop=False, skip_group_check=True)
                        for h in range(HEADS):
                            for e in range(2):
                                last = pe.matmul(
                                    ps[64 * e:64 * e + 64, bank + h // 8, WTOK * (h % 8):WTOK * (h % 8) + WTOK],
                                    left(h, e), right(h, e), start=False, stop=True, skip_group_check=True)
                        return last

                    def turn(out, rows):
                        for c in range(4):
                            last = pe.transpose(out[:, c, :], rows[:, 4 * c:4 * c + 4, :].rearrange("p h r -> p (h r)"),
                                                ident16[:])
                        return last

                    def body(n, it, u, parts):
                        v = 1 - u

                        def queries(buf, par):
                            return lambda h, e: buf[:, par, h // 4, 64 * e:64 * e + 64]

                        def keys(par):
                            return lambda h, e: k_t[:, par, h % 4, h // 4, 64 * e:64 * e + 64]

                        if valid(n, -2):
                            wait(pe, rope_done, n + 2)
                            project(qkv_ps[:, 0:2 * DIM], n + 2, slice(0, 2 * DIM)).then_inc(qk_done, 1)
                        if valid(n, 0):
                            wait(pe, kd_ready, n + 1)
                            wait(pe, ka_ready, n + 1)
                            wait(pe, max_done, n)
                            scores(S_BANK, queries(q_t, u), keys(u), it, 0, parts).then_inc(s_done, 1)
                        if valid(n, 1):
                            wait(pe, q2_ready, n)
                            wait(pe, exp_done, n - 1)
                            scores(ST_BANK, keys(v), queries(q_t2, v), it if u else it - 1, 1, parts).then_inc(st_done, 1)
                        if valid(n, -1):
                            wait(pe, lo_done, n + 2)
                            wait(pe, kd_ready, n + 1)
                            wait(pe, ka_ready, n + 1)
                            turn(t1_ps[:, 0], q_rows[:, v])
                            turn(t1_ps[:, 1], k_rows[:, v]).then_inc(t1_done, 1)
                        if valid(n, 3):
                            wait(pe, plo_done, n - 2)
                            wait(pe, norm_done, n - 3)
                            for hp in range(HP):
                                out = pv_ps[:, hp].rearrange("p e r d -> p (e r d)")
                                for k, (p, w) in enumerate(((p_hi, v_hi), (p_hi, v_lo), (p_lo, v_hi))):
                                    last = pe.matmul(out, p[:, v, 2 * hp:2 * hp + 2, :].rearrange("p h q -> p (h q)"),
                                                     w[:, v, hp].rearrange("p e r d -> p (e r d)"),
                                                     start=(k == 0 and hp == 0), stop=(k == 2), skip_group_check=True)
                            last.then_inc(pv_done, 1)
                        if valid(n, 1):
                            wait(pe, vlo_done, n - 1)
                            wait(pe, q2_ready, n)
                            project(v_ps, n - 1, slice(2 * DIM, 3 * DIM)).then_inc(v_done, 1)
                        if valid(n, 0):
                            wait(pe, mlo_done, n + 1)
                            wait(pe, q2_ready, n)
                            turn(t2_ps, q_rows[:, u]).then_inc(t2_done, 1)

                    rest = pe.value_load(mask_any[0:1, 0:1].bitcast(mybir.dt.int32))
                    with pe.If(rest > 0):
                        steps(pe, lambda n, it, u: body(n, it, u, 3))
                    with pe.If(rest < 1):
                        steps(pe, lambda n, it, u: body(n, it, u, 1))

                @block.vector
                def _(dve):
                    dve.memset(k_t[:].bitcast(F32), 0.0).then_inc(rows_set, 1)
                    dve.memset(q_rows[:], 0.0).then_inc(rows_set, 1)
                    dve.memset(k_rows[:], 0.0).then_inc(rows_set, 1)
                    dve.wait_ge(rows_set, 3)
                    dve.memset(k_rows[:, :, :, MAXROW:MAXROW + 2], MSCALE).then_inc(rows_set, 1)

                    def body(n, it, u):
                        v = 1 - u
                        if valid(n, -2):
                            dve.wait_ge(qk_done, n + 3)
                            wait(dve, r_done, n + 1)
                            x = qkv_ps[:, 0:2 * DIM].rearrange("p (a h d) -> p a h d", a=2, h=HEADS)
                            for dst, k in ((ta, 0), (tb, 1)):
                                last = dve.tensor_tensor(dst[:, u], x,
                                                         rope[:, k].unsqueeze(2).broadcast_to([128, 2, HEADS, HD]), ALU.mult)
                            last.then_inc(rope_done, 1)
                        if valid(n, 0):
                            dve.wait_ge(s_done, n + 1)
                            dve.tensor_reduce(mx[:, u, :], ps[:, S_BANK:S_BANK + 2, :].rearrange("p b (h k) -> p (b h) k", h=8),
                                              AX.X, ALU.max).then_inc(max_done, 1)
                            dve.wait_ge(max_done, n + 1)
                            hi = q_rows[:, u, :, MAXROW]
                            lo = q_rows[:, u, :, MAXROW + 1]
                            dve.tensor_scalar(hi, mx[:, u, :], -1.0 / MSCALE, None, ALU.mult).then_inc(mhi_done, 1)
                            dve.wait_ge(mhi_done, n + 1)
                            dve.scalar_tensor_tensor(out=lo, in0=mx[:, u, :], scalar=-1.0 / MSCALE, in1=hi,
                                                     op0=ALU.mult, op1=ALU.subtract).then_inc(mlo_done, 1)
                        if valid(n, 2):
                            dve.wait_ge(vhi_done, n - 1)
                            for e in range(2):
                                rows = slice(64 * e, 64 * e + 64)
                                last = dve.tensor_tensor(
                                    v_lo[rows, u, :, e, :, 0:HD], v_ps[rows, :].rearrange("p (h r d) -> p h r d", r=2, d=HD),
                                    v_hi[rows, u, :, e, :, 0:HD], ALU.subtract)
                            last.then_inc(vlo_done, 1)
                        if valid(n, -1):
                            dve.wait_ge(t1_done, n + 2)
                            dve.tensor_copy(q_t[:, v], t1_ps[:, 0]).then_inc(qt_ready, 1)
                            turned_keys(dve.tensor_copy, v, (0, 1)).then_inc(kd_ready, 1)
                        if valid(n, 3):
                            i = n - 3
                            dve.wait_ge(pv_done, n - 2)
                            for r in range(2):
                                rows = slice(64 * r, 64 * r + 64)
                                last = dve.reciprocal(rec[rows, v], pv_ps[rows, :, :, r, HD])
                            last.then_inc(rec_done, 1)
                            dve.wait_ge(rec_done, n - 2)
                            for r in range(2):
                                rows = slice(64 * r, 64 * r + 64)
                                last = dve.tensor_tensor(
                                    a_all[rows, at(i, 1)].rearrange("p a e h d -> p h (a e) d"),
                                    pv_ps[rows, :, :, r, 0:HD],
                                    rec[rows, v].unsqueeze(3).broadcast_to([64, HP, 2, HD]), ALU.mult)
                            last.then_inc(norm_done, 1)

                    steps(dve, body)

                @block.scalar
                def _(act):
                    act.wait_ge(rows_set, 4)
                    act.wait_ge(prep_pool, 5)

                    def copy(out, in_):
                        return act.activation(out, in_, ACT.Copy)

                    def body(n, it, u):
                        v = 1 - u
                        if valid(n, 1):
                            act.wait_ge(st_done, n)
                            wait(act, plo_done, n - 2)
                            act.activation(e_buf[:, v], ps[:, ST_BANK:ST_BANK + 2, :].rearrange("p b (h q) -> p (b h) q", h=8),
                                           ACT.Exp).then_inc(exp_done, 1)
                        if valid(n, -1):
                            act.wait_ge(qt_ready, n + 2)
                            turned_keys(copy, v, (2, 3)).then_inc(ka_ready, 1)
                        if valid(n, 0):
                            act.wait_ge(t2_done, n + 1)
                            copy(q_t2[:, u], t2_ps).then_inc(q2_ready, 1)
                        if valid(n, 1):
                            act.wait_ge(v_done, n)
                            wait(act, pv_done, n - 2)
                            for e in range(2):
                                rows = slice(64 * e, 64 * e + 64)
                                last = copy(v_hi[rows, v, :, e, :, 0:HD],
                                            v_ps[rows, :].rearrange("p (h r d) -> p h r d", r=2, d=HD))
                            last.then_inc(vhi_done, 1)
                        if valid(n, -2):
                            act.wait_ge(r_done, n + 3)
                            copy(q_rows[:, u, :, 0:16].rearrange("p h (r d) -> p h r d", r=2),
                                 rot[:, u, 0].unsqueeze(2).broadcast_to([128, HEADS, 2, HD]))
                            copy(k_rows[:, u].rearrange("p h (r d) -> p h r d", d=HD)[:, :, 0:3:2, :],
                                 rot[:, u, 1].unsqueeze(2).broadcast_to([128, HEADS, 2, HD])).then_inc(hi_done, 1)
                        if valid(n, 1):
                            act.wait_ge(exp_done, n)
                            wait(act, pv_done, n - 2)
                            copy(p_hi[:, v], e_buf[:, v]).then_inc(phi_done, 1)

                    steps(act, body)

                @block.gpsimd
                def _(pool):
                    pool.wait_ge(rows_set, 4)

                    def body(n, it, u):
                        v = 1 - u
                        if valid(n, -1):
                            pool.wait_ge(hi_done, n + 2)
                            pool.tensor_tensor(q_rows[:, v, :, 16:24], rot[:, v, 0], q_rows[:, v, :, 0:8], ALU.subtract)
                            pool.memset(q_rows[:, v, :, MAXROW:MAXROW + 2], 0.0)
                            pool.tensor_tensor(k_rows[:, v, :, 8:16], rot[:, v, 1], k_rows[:, v, :, 0:8], ALU.subtract)\
                                .then_inc(lo_done, 1)
                        if valid(n, -2):
                            pool.wait_ge(rope_done, n + 3)
                            wait(pool, hi_done, n + 1)
                            pool.tensor_tensor(
                                rot[:, u].rearrange("p a h (s d) -> p (a h) s d", s=2),
                                ta[:, u].rearrange("p a h (s d) -> p (a h) s d", s=2),
                                tb[:, u].rearrange("p a h (s d) -> p (a h) s d", s=2)[:, :, ::-1, :], ALU.add)\
                                .then_inc(r_done, 1)
                        if valid(n, 2):
                            pool.wait_ge(phi_done, n - 1)
                            pool.tensor_tensor(p_lo[:, u], e_buf[:, u], p_hi[:, u], ALU.subtract).then_inc(plo_done, 1)

                    steps(pool, body)

        until_mlp.close()
        x2_all = sb("x2_all", [128, B, NWIN, WTOK])
        a_hi = sem("a_hi")
        a_lo = sem("a_lo")
        a_turned = sem("a_turned")
        at_ready = sem("at_ready")
        xb_ready = sem("xb_ready")
        prj_done = sem("prj_done")
        x1_ready = sem("x1_ready")
        l2_stats = sem("l2_stats")
        l2_pool = sem("l2_pool")
        l2_rstd = sem("l2_rstd")
        l2_norm = sem("l2_norm")
        l2_hi = sem("l2_hi")
        l2_lo = sem("l2_lo")
        l2_turned = sem("l2_turned")
        l2_ready = sem("l2_ready")
        gate_done = sem("gate_done")
        up_done = sem("up_done")
        silu_done = sem("silu_done")
        h_done = sem("h_done")
        h_used = sem("h_used")
        mlp_done = sem("mlp_done")
        x2_done = sem("x2_done")
        with ExitStack() as st:
            def tmp(name, shape, dt=F32):
                return st.enter_context(nc.sbuf_tensor(name, shape, dt))

            ah = tmp("ah", [128, 2, TPC, 128], F16)
            al = tmp("al", [128, 2, TPC, 128], F16)
            a_t = tmp("a_t", [128, 2, TPC, 2, 128], F16)
            xb = tmp("xb", [128, 2, TPC, DIM])
            x1 = tmp("x1", [128, 2, TPC, DIM])
            stats = tmp("stats2", [128, 2, TPC, 6])
            mv = tmp("mv2", [128, 2, TPC, 2])
            veps = tmp("veps2", [128, 2, TPC])
            rstd = tmp("rstd2", [128, 2, TPC])
            nmean = tmp("nmean2", [128, 2, TPC])
            nmr = tmp("nmr2", [128, 2, TPC])
            yn = tmp("yn", [128, 2, CHUNK])
            yh = tmp("yh", [128, 2, CHUNK], F16)
            yl = tmp("yl", [128, 2, CHUNK], F16)
            y_t = tmp("y_t", [128, 2, 2, CHUNK], F16)
            sg = tmp("sg", [128, 2, CHUNK])
            hid = tmp("hid", [128, 2, CHUNK])
            wait_here = tmp("wait_here", [128, 1])

            AT_BANK, PRJ_BANK, YT_BANK, OUT_BANK = 0, 1, 2, 7
            GATE_BANK, UP_BANK = (3, 5), (4, 6)

            def steps(eng, body):
                for c in range(-1, 2):
                    body(c, c % 2)
                with eng.Fori(1, CHUNKS // 2 - 1) as it:
                    for u in range(2):
                        body(it * 2 + u, u)
                for c in range(CHUNKS - 2, CHUNKS + 2):
                    body(c, c % 2)

            def valid(c, lag):
                return not isinstance(c, int) or 0 <= c - lag < CHUNKS

            with nc.Block() as block:
                @block.gpsimd
                def _(pool):
                    pool.wait_ge(norm_done, PAIRS)

                    def body(c, u):
                        v = 1 - u
                        if valid(c, 0):
                            pool.wait_ge(l2_stats, c * 2 + 2)
                            wait(pool, l2_norm, c - 1)
                            pool.tensor_tensor(veps[:, u, :], mv[:, u, :, 1], ln_const[:, 1, :], ALU.add).then_inc(l2_pool, 1)
                            pool.tensor_tensor(nmean[:, u, :], mv[:, u, :, 0], ln_const[:, 2, :], ALU.mult).then_inc(l2_pool, 1)
                            pool.wait_ge(l2_pool, c * 3 + 2)
                            pool.tensor_tensor(rstd[:, u, :], veps[:, u, :], ln_const[:, 0, :], ALU.pow).then_inc(l2_pool, 1)
                            pool.wait_ge(l2_pool, c * 3 + 3)
                            pool.tensor_tensor(nmr[:, u, :], nmean[:, u, :], rstd[:, u, :], ALU.mult).then_inc(l2_rstd, 1)
                        if valid(c, -1):
                            pool.wait_ge(a_hi, c + 2)
                            wait(pool, a_turned, c)
                            pool.tensor_tensor(al[:, v].rearrange("p t d -> p (t d)"),
                                               a_all[:, at(c * TPC + TPC, TPC)].rearrange("p t e h d -> p (t e h d)"),
                                               ah[:, v].rearrange("p t d -> p (t d)"), ALU.subtract).then_inc(a_lo, 1)
                        if valid(c, 0):
                            pool.wait_ge(l2_hi, c + 1)
                            wait(pool, l2_turned, c - 1)
                            pool.tensor_tensor(yl[:, u, :], yn[:, u, :], yh[:, u, :], ALU.subtract).then_inc(l2_lo, 1)
                        if valid(c, -1):
                            wait(pool, x1_ready, c)
                            pool.tensor_tensor(xb[:, v], x_all[:, at(c * TPC + TPC, TPC)],
                                               proj_b[:].unsqueeze(1).broadcast_to([128, TPC, DIM]), ALU.add).then_inc(xb_ready, 1)

                    steps(pool, body)

                @block.tensor
                def _(pe):
                    pe.wait_ge(norm_done, PAIRS)
                    pe.wait_ge(prep_proj, 3)

                    def fc1(b, v, k):
                        if k == 0:
                            pe.wait_ge(l2_ready, b + 1)
                        for block_, bank, done, used in ((HBLK + k, GATE_BANK[k % 2], gate_done, silu_done),
                                                         (k, UP_BANK[k % 2], up_done, h_done)):
                            wait(pe, used, b * HBLK + k - 1)
                            for n, (ws, ys) in enumerate(((0, 0), (1, 0), (0, 1))):
                                last = pe.matmul(ps[:, bank, :], fc1_w16[:, ws, 128 * block_:128 * block_ + 128],
                                                 y_t[:, v, ys, :], start=(n == 0), stop=(n == 2))
                            last.then_inc(done, 1)

                    def fc2(b, k):
                        if k == 0:
                            wait(pe, x2_done, b)
                        pe.wait_ge(h_done, b * HBLK + k + 1)
                        pe.matmul(ps[:, OUT_BANK, :], fc2_ws[:, k, :], hid[:, k % 2, :], start=(k == 0), stop=False,
                                  skip_group_check=True).then_inc(h_used, 1)

                    def body(c, u):
                        v = 1 - u
                        if valid(c, 0):
                            pe.wait_ge(at_ready, c + 1)
                            wait(pe, x1_ready, c)
                            for k in range(TPC):
                                for n, (xs, ws) in enumerate(((0, 0), (0, 1), (1, 0))):
                                    last = pe.matmul(ps[:, PRJ_BANK, 128 * k:128 * k + 128], a_t[:, u, k, xs, :],
                                                     proj_w16[:, ws, :], start=(k == 0 and n == 0), stop=(n == 2),
                                                     skip_group_check=True)
                            last.then_inc(prj_done, 1)
                        if valid(c, 1):
                            for k in range(HBLK):
                                fc1(c - 1, v, k)
                                if 1 <= k < HBLK - 1:
                                    fc2(c - 1, k - 1)
                        if valid(c, -1):
                            pe.wait_ge(a_lo, c + 2)
                            wait(pe, at_ready, c + 1)
                        if valid(c, 1):
                            fc2(c - 1, HBLK - 2)
                        if valid(c, -1):
                            out = ps[:, AT_BANK, :].bitcast(F16).rearrange("p (t s q) -> p t s q", t=TPC, s=2)
                            for s, src in enumerate((ah, al)):
                                for k in range(TPC):
                                    for e in range(2):
                                        for r in range(2):
                                            rows = slice(64 * r, 64 * r + 64)
                                            last = pe.transpose(out[rows, k, s, 64 * e:64 * e + 64],
                                                                src[rows, v, k, 64 * e:64 * e + 64], ident16[rows, rows])
                            last.then_inc(a_turned, 1)
                        if valid(c, 0):
                            pe.wait_ge(l2_lo, c + 1)
                            wait(pe, l2_ready, c)
                            out = ps[:, YT_BANK, :].bitcast(F16).rearrange("p (s t q) -> p s t q", s=2, t=TPC)
                            for s, src in enumerate((yh, yl)):
                                for k in range(TPC):
                                    last = pe.transpose(out[:, s, k, :], src[:, u, 128 * k:128 * k + 128], ident16[:])
                            last.then_inc(l2_turned, 1)
                        if valid(c, 1):
                            fc2(c - 1, HBLK - 1)
                            for k in range(TPC):
                                last = pe.matmul(ps[:, OUT_BANK, 128 * k:128 * k + 128], x1[:, v, k, :], ident[:],
                                                 start=False, stop=True, skip_group_check=True)
                            last.then_inc(mlp_done, 1)

                    steps(pe, body)

                @block.vector
                def _(dve):
                    def hidden(b, k):
                        dve.wait_ge(up_done, b * HBLK + k + 1)
                        dve.wait_ge(silu_done, b * HBLK + k + 1)
                        wait(dve, h_used, b * HBLK + k - 1)
                        dve.scalar_tensor_tensor(out=hid[:, k % 2, :], in0=ps[:, UP_BANK[k % 2], :],
                                                 scalar=fc1_bias[:, k:k + 1], in1=sg[:, k % 2, :], op0=ALU.add,
                                                 op1=ALU.mult).then_inc(h_done, 1)

                    def body(c, u):
                        v = 1 - u
                        if valid(c, 0):
                            dve.wait_ge(prj_done, c + 1)
                            dve.wait_ge(xb_ready, c + 1)
                            wait(dve, mlp_done, c - 1)
                            dve.scalar_tensor_tensor(out=x1[:, u].rearrange("p t q -> p (t q)"), in0=ps[:, PRJ_BANK, :],
                                                     scalar=1.0 / WSCALE, in1=xb[:, u].rearrange("p t q -> p (t q)"),
                                                     op0=ALU.mult, op1=ALU.add).then_inc(x1_ready, 1)
                            dve.wait_ge(x1_ready, c + 1)
                            wait(dve, l2_rstd, c - 1)
                            for k in range(TPC):
                                last = dve.bn_stats(stats[:, u, k, :], x1[:, u, k, :])
                            last.then_inc(l2_stats, 1)
                        if valid(c, 1):
                            hidden(c - 1, 0)
                        if valid(c, 0):
                            dve.wait_ge(l2_stats, c * 2 + 1)
                            dve.memset(wait_here[:], 0.0)
                            for k in range(TPC):
                                last = dve.bn_aggr(mv[:, u, k, :], stats[:, u, k, :])
                            last.then_inc(l2_stats, 1)
                        if valid(c, 1):
                            hidden(c - 1, 1)
                        if valid(c, 0):
                            dve.wait_ge(l2_rstd, c + 1)
                            wait(dve, l2_lo, c - 1)
                            for k in range(TPC):
                                last = dve.tensor_scalar(yn[:, u, 128 * k:128 * k + 128], x1[:, u, k, :],
                                                         rstd[:, u, k:k + 1], nmr[:, u, k:k + 1], ALU.mult, ALU.add)
                            last.then_inc(l2_norm, 1)
                        if valid(c, 1):
                            hidden(c - 1, 2)
                            hidden(c - 1, 3)
                        if valid(c, -1):
                            dve.wait_ge(a_turned, c + 2)
                            wait(dve, prj_done, c)
                            dve.tensor_copy(a_t[:, v].rearrange("p t s q -> p (t s q)"), ps[:, AT_BANK, :].bitcast(F16))\
                                .then_inc(at_ready, 1)
                        if valid(c, 0):
                            dve.wait_ge(l2_turned, c + 1)
                            dve.tensor_copy(y_t[:, u].rearrange("p s q -> p (s q)"), ps[:, YT_BANK, :].bitcast(F16))\
                                .then_inc(l2_ready, 1)

                    steps(dve, body)

                @block.scalar
                def _(act):
                    act.wait_ge(norm_done, PAIRS)

                    def gate(b, k):
                        act.wait_ge(gate_done, b * HBLK + k + 1)
                        wait(act, h_done, b * HBLK + k - 1)
                        act.activation(sg[:, k % 2, :], ps[:, GATE_BANK[k % 2], :], ACT.Silu,
                                       bias=fc1_bias[:, HBLK + k:HBLK + k + 1], scale=1.0 / WSCALE).then_inc(silu_done, 1)

                    def body(c, u):
                        v = 1 - u
                        if valid(c, 2):
                            act.wait_ge(mlp_done, c - 1)
                            act.activation(x2_all[:, :, at(c * 2 - 4, 2), :],
                                           ps[:, OUT_BANK, :].rearrange("p (w b q) -> p b w q", w=2, b=B),
                                           ACT.Identity, bias=cols[:, 0:1], scale=1.0).then_inc(x2_done, 1)
                        if valid(c, 1):
                            gate(c - 1, 0)
                            gate(c - 1, 1)
                        if valid(c, -1):
                            wait(act, a_turned, c)
                            wait(act, a_lo, c)
                            act.activation(ah[:, v].rearrange("p t d -> p (t d)"),
                                           a_all[:, at(c * TPC + TPC, TPC)].rearrange("p t e h d -> p (t e h d)"), ACT.Copy)\
                                .then_inc(a_hi, 1)
                        if valid(c, 1):
                            gate(c - 1, 2)
                        if valid(c, 0):
                            act.wait_ge(l2_norm, c + 1)
                            wait(act, l2_turned, c - 1)
                            act.activation(yh[:, u, :], yn[:, u, :], ACT.Copy).then_inc(l2_hi, 1)
                        if valid(c, 1):
                            gate(c - 1, 3)

                    steps(act, body)

        xs_ready = sem("xs_ready")
        xg_done = sem("xg_done")
        fg_done = sem("fg_done")
        fg_hi = sem("fg_hi")
        fg_ready = sem("fg_ready")
        v4_done = sem("v4_done")
        v4_ready = sem("v4_ready")
        s4_done = sem("s4_done")
        max4_done = sem("max4_done")
        mh_tmp = sem("mh_tmp")
        mh_ready = sem("mh_ready")
        mq_ready = sem("mq_ready")
        mt_done = sem("mt_done")
        mrow_ready = sem("mrow_ready")
        st4_done = sem("st4_done")
        exp4_done = sem("exp4_done")
        sum4_done = sem("sum4_done")
        pv4_done = sem("pv4_done")
        rrow_ready = sem("rrow_ready")
        rec4_done = sem("rec4_done")
        r_turned = sem("r_turned")
        div_done = sem("div_done")
        o_ready = sem("o_ready")
        stored = [sem(f"stored{u}") for u in range(2)]
        pads_set = sem("pads_set")
        E_BUFS = 4
        with ExitStack() as st:
            def tmp(name, shape, dt=F32):
                return st.enter_context(nc.sbuf_tensor(name, shape, dt))

            xs = tmp("xs", [128, 2, NB])
            xg = tmp("xg", [128, 2, NB])
            gbv = tmp("gbv", [128, 1])
            fg = tmp("fg", [64, 2, NB])
            fgh = tmp("fgh", [64, 2, NB], F16)
            f_rows = tmp("f_rows", [128, 2, NB], F16)
            g_rows = tmp("g_rows", [128, 2, NB], F16)
            val = tmp("val", [128, 2, BT, DIM])
            mx = tmp("mx4", [128, BT])
            mh = tmp("mh", [128, BT, 64], F16)
            mq = tmp("mq", [128, BT])
            e4 = tmp("e4", [128, E_BUFS, NB])
            e_sum = tmp("e_sum", [128, 2, NB], F16)
            den = tmp("den", [128, 2, BT])
            r_rows = tmp("r_rows", [128, NB])
            gamma_s = tmp("gamma_s", [128, 1])
            rec4 = tmp("rec4", [128, BT])
            rh = tmp("rh", [128, 2, 2, BT], F16)
            o4 = tmp("o4", [128, 2, 512])
            ob = tmp("ob", [128, 2, NB])

            S4, AUX, ST4, PV4 = 0, 6, 2, 4
            S_PAIR = (S4, AUX)

            def two(bank, rows=slice(0, 128)):
                return ps[rows, bank:bank + 2, :].rearrange("p a b -> p (a b)")

            def steps(eng, body):
                body(-1, -1, 1, False, True)
                with eng.Fori(0, (B - 2) // 2) as it:
                    for u in range(2):
                        body(it * 2 + u, it, u, True, True)
                body(B - 2, B // 2 - 1, 0, True, True)
                body(B - 1, B // 2 - 1, 1, True, False)

            with nc.Block() as block:
                @block.gpsimd
                def _(pool):
                    for k, (rows, value) in enumerate(((f_rows[64:128], 0.0), (g_rows[64:128], 0.0), (mh[:], 0.0),
                                                       (g_rows[64:65], MSCALE), (g_rows[96:97], 1.0))):
                        wait(pool, pads_set, k)
                        pool.memset(rows, value).then_inc(pads_set, 1)

                    def fixed_place(b, u):
                        pool.tensor_copy(xs[:, u], x2_all[:, at(b, 1)].rearrange("p a w q -> p (a w q)")).then_inc(xs_ready, 1)

                    def body(b, half, u, cur, nxt):
                        if not cur:
                            pool.wait_ge(pads_set, 5)
                            pool.wait_ge(x2_done, CHUNKS)
                            for k in range(2):
                                fixed_place(k, k)
                            return
                        if not isinstance(b, int) or b + 2 < B:
                            pool.wait_ge(xg_done, b + 1)
                            fixed_place(b + 2, u)

                    steps(pool, body)

                @block.tensor
                def _(pe):
                    pe.wait_ge(pads_set, 5)

                    def out4(b, u, m):
                        pe.wait_ge(exp4_done, b * BT + m + 1)
                        if m == 0:
                            wait(pe, div_done, b * 2)
                        for k in range(2):
                            last = pe.matmul(ps[:, PV4 + k, :], val[:, u, m, :], e4[:, m % E_BUFS, 512 * k:512 * k + 512],
                                             start=(m == 0), stop=(m == BT - 1))
                        last.then_inc(pv4_done, 1)

                    def project_fg(k, bank, v):
                        for n in range(2):
                            last = pe.matmul(ps[0:64, bank + n, :], fg_w[:, k, :], xs[:, v, 512 * n:512 * n + 512],
                                             start=True, stop=True)
                        last.then_inc(fg_done, 1)

                    def body(b, half, u, cur, nxt):
                        v = 1 - u
                        if nxt:
                            pe.wait_ge(xs_ready, b + 2)
                            wait(pe, sum4_done, b * BT + BT - 1)
                            project_fg(0, S4, v)
                        if cur:
                            pe.wait_ge(mh_ready, b * BT + BT)
                            pe.wait_ge(sum4_done, b * BT + BT)
                            for n in range(BT):
                                last = pe.matmul(ps[64:128, S4 + n // 4, 128 * (n % 4):128 * (n % 4) + 128], mh[:, n, :],
                                                 ident16[:], start=(n % 4 == 0), stop=True, skip_group_check=True)
                            last.then_inc(mt_done, 1)
                        if nxt:
                            wait(pe, rrow_ready, b)
                            project_fg(1, ST4, v)
                            wait(pe, sum4_done, b * BT + BT)
                            for n in range(BT):
                                last = pe.matmul(ps[:, AUX + n // 4, 128 * (n % 4):128 * (n % 4) + 128],
                                                 xs[:, v, 128 * n:128 * n + 128], wv[:], start=(n % 4 == 0), stop=True,
                                                 skip_group_check=True)
                            last.then_inc(v4_done, 1)
                            pe.wait_ge(fg_hi, b * 2 + 4)
                        for n in range(BT):
                            if cur:
                                if n == 0:
                                    pe.wait_ge(mrow_ready, b + 1)
                                wait(pe, exp4_done, b * BT + n)
                                for k in range(2):
                                    last = pe.matmul(ps[:, ST4 + k, :], g_rows[:, u, 128 * n:128 * n + 128],
                                                     f_rows[:, u, 512 * k:512 * k + 512], start=True, stop=True)
                                last.then_inc(st4_done, 1)
                                if n >= 1:
                                    out4(b, u, n - 1)
                            if nxt:
                                if n == 0:
                                    pe.wait_ge(fg_ready, b * 2 + 4)
                                if n == 1:
                                    pe.wait_ge(v4_ready, b + 2)
                                if n >= 2:
                                    pe.wait_ge(sum4_done, b * BT + BT + n - 1)
                                for m in range(2):
                                    last = pe.matmul(ps[:, S_PAIR[n % 2] + m, :], f_rows[0:64, v, 128 * n:128 * n + 128],
                                                     g_rows[0:64, v, 512 * m:512 * m + 512], start=True, stop=True)
                                last.then_inc(s4_done, 1)
                        if cur:
                            out4(b, u, BT - 1)
                            pe.wait_ge(rec4_done, b * 3 + 3)
                            for n in range(BT):
                                for k in range(2):
                                    last = pe.matmul(ps[:, ST4 + n // 4, 128 * (n % 4):128 * (n % 4) + 128],
                                                     rh[:, u, k, n:n + 1].broadcast_to([128, 128]), ident16[:],
                                                     start=(n % 4 == 0 and k == 0), stop=(k == 1), skip_group_check=True)
                            last.then_inc(r_turned, 1)

                    steps(pe, body)

                @block.vector
                def _(dve):
                    dve.wait_ge(pads_set, 5)
                    dve.tensor_tensor(gbv[:], cols[:, 1:2], cols[:, 2:3], ALU.mult).then_inc(pads_set, 1)
                    dve.tensor_scalar(gamma_s[:], cols[:, 1:2], 1.0 / RSCALE, None, ALU.mult).then_inc(pads_set, 1)
                    dve.wait_ge(pads_set, 7)

                    def body(b, half, u, cur, nxt):
                        v = 1 - u
                        if cur:
                            dve.wait_ge(mt_done, b + 1)
                            dve.tensor_copy(f_rows[64:128, u, :], two(S4, slice(64, 128))).then_inc(mrow_ready, 1)
                        if nxt:
                            for k, rows in ((0, f_rows), (1, g_rows)):
                                dve.wait_ge(fg_hi, b * 2 + k + 3)
                                dve.scalar_tensor_tensor(out=rows[0:64, v, :], in0=fgh[:, k, :],
                                                         scalar=fg_b[:, 2 + k:3 + k], in1=fg[:, k, :], op0=ALU.mult,
                                                         op1=ALU.add).then_inc(fg_ready, 1)
                            for n in range(BT):
                                tile = b * BT + BT + n
                                dve.wait_ge(s4_done, tile + 1)
                                dve.tensor_reduce(mx[:, n:n + 1], two(S_PAIR[n % 2]), AX.X, ALU.max, negate=True)\
                                    .then_inc(max4_done, 1)
                                dve.wait_ge(max4_done, tile + 1)
                                dve.tensor_scalar(mh[:, n, 0:1], mx[:, n:n + 1], 1.0 / MSCALE, None, ALU.mult)\
                                    .then_inc(mh_tmp, 1)
                                dve.wait_ge(mh_tmp, tile + 1)
                                dve.scalar_tensor_tensor(out=mh[:, n, 32:33], in0=mh[:, n, 0:1], scalar=-MSCALE,
                                                         in1=mx[:, n:n + 1], op0=ALU.mult, op1=ALU.add)\
                                    .then_inc(mh_ready, 1)
                                dve.wait_ge(mh_ready, tile + 1)
                                dve.scalar_tensor_tensor(out=mq[:, n:n + 1], in0=mh[:, n, 0:1], scalar=MSCALE,
                                                         in1=mh[:, n, 32:33], op0=ALU.mult, op1=ALU.add)\
                                    .then_inc(mq_ready, 1)
                        if cur:
                            dve.wait_ge(rrow_ready, b + 1)
                            wait(dve, o_ready, b * 2)
                            dve.wait_ge(pv4_done, b * BT + BT)
                            for k in range(2):
                                dve.tensor_tensor(o4[:, k, :], ps[:, PV4 + k, :], r_rows[:, 512 * k:512 * k + 512], ALU.mult)\
                                    .then_inc(div_done, 1)
                            dve.wait_ge(stored[u], half * 32 + 32)
                            for k in range(2):
                                dve.wait_ge(div_done, b * 2 + k + 1)
                                dve.scalar_tensor_tensor(out=ob[:, u, 512 * k:512 * k + 512], in0=o4[:, k, :],
                                                         scalar=gamma_s[:], in1=xg[:, u, 512 * k:512 * k + 512],
                                                         op0=ALU.mult, op1=ALU.add).then_inc(o_ready, 1)
                        if nxt:
                            dve.wait_ge(sum4_done, b * BT + 2 * BT)
                            dve.reciprocal(rec4[:], den[:, v, :]).then_inc(rec4_done, 1)
                            dve.wait_ge(rec4_done, b * 3 + 4)
                            dve.tensor_scalar(rh[:, v, 0, :], rec4[:], RSCALE, None, ALU.mult).then_inc(rec4_done, 1)
                            dve.wait_ge(rec4_done, b * 3 + 5)
                            dve.scalar_tensor_tensor(out=rh[:, v, 1, :], in0=rec4[:], scalar=RSCALE, in1=rh[:, v, 0, :],
                                                     op0=ALU.mult, op1=ALU.subtract).then_inc(rec4_done, 1)

                    steps(dve, body)

                @block.scalar
                def _(act):
                    act.wait_ge(pads_set, 7)

                    def body(b, half, u, cur, nxt):
                        v = 1 - u
                        if nxt:
                            for k, bank in enumerate((S4, ST4)):
                                act.wait_ge(fg_done, b * 2 + k + 3)
                                wait(act, fg_ready, b * 2 + 2)
                                for dst, done in ((fg, None), (fgh, fg_hi)):
                                    last = act.activation(dst[:, k, :], two(bank, slice(0, 64)), ACT.Identity,
                                                          bias=fg_b[:, k:k + 1], scale=1.0)
                                last.then_inc(fg_hi, 1)
                            act.wait_ge(v4_done, b + 2)
                            act.activation(val[:, v].rearrange("p n d -> p (n d)"), two(AUX), ACT.Copy).then_inc(v4_ready, 1)
                        for m in range(BT + 1):
                            if cur and m < BT:
                                act.wait_ge(st4_done, b * BT + m + 1)
                                if m >= E_BUFS:
                                    act.wait_ge(pv4_done, b * BT + m - E_BUFS + 1)
                                act.activation(e4[:, m % E_BUFS, :], two(ST4), ACT.Exp).then_inc(exp4_done, 1)
                            if cur and m == 1:
                                act.activation(xg[:, u, :], xs[:, u, :], ACT.Identity, bias=gbv[:], scale=1.0)\
                                    .then_inc(xg_done, 1)
                            if cur and m == BT:
                                act.wait_ge(r_turned, b + 1)
                                wait(act, div_done, b * 2)
                                act.activation(r_rows[:], two(ST4), ACT.Copy).then_inc(rrow_ready, 1)
                            if nxt and m >= 1:
                                act.wait_ge(mq_ready, b * BT + BT + m)
                                wait(act, sum4_done, b * BT + BT + m - 2)
                                act.activation(e_sum[:, m % 2, :], two(S_PAIR[(m - 1) % 2]), ACT.Exp, bias=mq[:, m - 1:m],
                                               scale=1.0, accum_out=den[:, v, m - 1:m]).then_inc(sum4_done, 1)

                    steps(act, body)

                @block.sync
                def _(sp):
                    for u in range(2):
                        sp.sem_inc(stored[u], 32)

                    def body(b, half, u, cur, nxt):
                        if cur:
                            for k in range(2):
                                sp.wait_ge(o_ready, b * 2 + k + 1)
                                sp.dma_start(t["out"][at(b, 1), :, 512 * k:512 * k + 512].rearrange("a p n -> (a p) n"),
                                             ob[:, u, 512 * k:512 * k + 512]).then_inc(stored[u], 16)

                    steps(sp, body)
                    for u in range(2):
                        sp.wait_ge(stored[u], 32 * (B // 2 + 1))


def _rope_tables():
    d1 = HD // 4
    inv = (10000.0 ** (-(np.arange(d1, dtype=np.float32) / d1))).astype(np.float32)
    pos = np.arange(WIN, dtype=np.float32)
    ang = pos[:, None] * inv
    rows = np.broadcast_to(ang[:, None, :], (WIN, WIN, d1)).reshape(WTOK, d1)
    cols = np.broadcast_to(ang[None, :, :], (WIN, WIN, d1)).reshape(WTOK, d1)
    a = np.concatenate([rows, cols], 1).astype(np.float32)
    cos, sin = np.cos(a), np.sin(a)
    c = np.concatenate([cos, cos], 1)
    s = np.concatenate([sin, -sin], 1)
    table = np.stack([c, s]) / WSCALE
    both = np.stack([table * HD ** -0.5, table], 2)
    both = np.concatenate([both, both], 1)
    return np.ascontiguousarray(both.transpose(1, 0, 2, 3)).astype(np.float32)


def kernel(**inputs):
    import concourse.bacc as bacc
    from concourse.bass_utils import run_bass_kernel_spmd

    def a(name):
        return np.asarray(inputs[name])

    def L0(name):
        return a("L0_conv_" + name)

    def L1(name):
        return a("L1_conv_" + name)

    x = np.roll(a("x"), (-SHIFT, -SHIFT), (1, 2))
    nh, nw = H // WIN, W // WIN
    x = x.reshape(B, nh, WIN, nw, WIN, DIM).transpose(1, 3, 0, 2, 4, 5).reshape(PAIRS, 2 * WTOK, DIM)
    ch = np.arange(DIM).reshape(HP, 2, HD).transpose(1, 0, 2).reshape(DIM)
    qkv_w, qkv_b = L0("qkv_w"), L0("qkv_b")
    proj = L0("proj_w")[:, ch].T
    mask = L0("attn_mask")
    both = np.stack([mask.transpose(1, 0, 2), mask.transpose(2, 0, 1)], 1)
    fc1_b = L0("fc1_b").reshape(2 * HBLK, 128).T
    zero = np.zeros(DIM, np.float32)
    lo_f = np.repeat(np.array([0, 0, -1, -1], np.float32), CQK)
    lo_g = np.repeat(np.array([0, -1, 0, -1], np.float32), CQK)
    sel = np.zeros((33, 128), np.float16)
    sel[0], sel[32] = 1, 1
    data = {
        "x": x.transpose(1, 0, 2),
        "qkv_w": qkv_w.T,
        "qkv_b": np.broadcast_to(qkv_b, (33, 3 * DIM)),
        "g1b1": np.stack([L0("norm1_g"), L0("norm1_b"), L0("norm2_g"), L0("norm2_b")], 1),
        "ident16": np.eye(128, dtype=np.float16),
        "ident": np.eye(128, dtype=np.float32),
        "sel33": sel,
        "rope": _rope_tables(),
        "mask": np.concatenate([both, both], 0),
        "identb": np.eye(128, dtype=np.float32).astype(mybir.dt.np(mybir.dt.bfloat16)),
        "proj_w": proj,
        "proj_b": np.broadcast_to(L0("proj_b"), (128, DIM)),
        "fc1_w": L0("fc1_w").T,
        "fc1_b": fc1_b,
        "fc2_w": L0("fc2_w").T.reshape(HBLK, 128, DIM).transpose(1, 0, 2),
        "cols": np.stack([L0("fc2_b"), np.broadcast_to(L1("gamma"), (DIM,)), L1("bv"), zero], 1),
        "fg_w": np.stack([np.tile(L1("Wq"), (1, 4)), np.tile(L1("Wk"), (1, 4))], 1),
        "fg_b": np.stack([np.tile(L1("bq"), 4), np.tile(L1("bk"), 4), lo_f, lo_g], 1),
        "wv": L1("Wv"),
        "ln_const": np.broadcast_to(np.array([-0.5, EPS, -1], np.float32)[:, None], (128, 3, TPC)),
        "ones": np.ones((128, 128), np.float32),
    }
    nc = bacc.Bacc("TRN2", target_bir_lowering=False, num_devices=1)
    arrays, t = {}, {}
    for name, v in data.items():
        v = np.ascontiguousarray(v)
        arrays["in_" + name] = v
        t[name] = nc.dram_tensor("in_" + name, v.shape, mybir.dt.from_np(v.dtype), kind="ExternalInput").ap()
    t["out"] = nc.dram_tensor("out", (B, DIM, NB), F32, kind="ExternalOutput").ap()
    build(nc, t)
    got = run_bass_kernel_spmd(nc, [arrays], core_ids=[0]).results[0]["out"]
    y = np.asarray(got).reshape(B, DIM, nh, nw, WIN, WIN).transpose(0, 2, 4, 3, 5, 1).reshape(B, H, W, DIM)
    return np.roll(y, (SHIFT, SHIFT), (1, 2))
```

```python
from contextlib import ExitStack

import concourse.bass as bass
import numpy as np
from concourse import mybir

F32 = mybir.dt.float32
F16 = mybir.dt.float16
BF16 = mybir.dt.bfloat16
ALU = mybir.AluOpType
ACT = mybir.ActivationFunctionType
AX = mybir.AxisListType

B, H, W, DIM = 4, 32, 32, 128
WIN, SHIFT = 8, 4
HEADS, HD = 16, 8
NWIN = (H // WIN) * (W // WIN)
WTOK = WIN * WIN
PAIRS = NWIN * B // 2
TOK = B * H * W
CHUNK = 512
CHUNKS = TOK // CHUNK
TPC = CHUNK // 128
HIDDEN = 4 * DIM
HBLK = HIDDEN // 128
CQK = DIM // 8
NB = H * W
BT = NB // 128
EPS = 1e-5
WSCALE = 64.0
MSCALE = 256.0
RSCALE = 1024.0
ROWS = 32
HP = HEADS // 2
MAXROW = 3 * HD


def at(start, size):
    return bass.ds(start, size)


def build(nc, t):
    ctx = ExitStack()
    with ctx:
        def sb(name, shape, dt=F32):
            return ctx.enter_context(nc.sbuf_tensor(name, shape, dt))

        def sem(name):
            return ctx.enter_context(nc.semaphore(name))

        qkv_w = sb("qkv_w", [128, 3 * DIM])
        qkv_b = sb("qkv_b", [33, 3 * DIM])
        g1b1 = sb("g1b1", [128, 4])
        gains = sb("gains", [128, 4])
        w_scaled = sb("w_scaled", [128, 2 * HIDDEN])
        b_sum = sb("b_sum", [33, 3 * DIM])
        qkv_w16 = sb("qkv_w16", [128, 2, 3 * DIM], F16)
        qkv_b16 = sb("qkv_b16", [33, 3 * DIM], F16)
        sel33 = sb("sel33", [33, 128], F16)
        rope = sb("rope", [128, 2, 2, HD])
        ident = sb("ident", [128, 128])
        ident16 = sb("ident16", [128, 128], F16)
        identb = sb("identb", [128, 128], BF16)
        proj_w = sb("proj_w", [128, DIM])
        proj_ws = sb("proj_ws", [128, DIM])
        proj_w16 = sb("proj_w16", [128, 2, DIM], F16)
        proj_b = sb("proj_b", [128, DIM])
        fc1_w = sb("fc1_w", [128, 2 * HIDDEN])
        fc1_w16 = sb("fc1_w16", [128, 2, 2 * HIDDEN], F16)
        fc1_b = sb("fc1_b", [128, 2 * HBLK])
        fc1_bias = sb("fc1_bias", [128, 2 * HBLK])
        fc2_w = sb("fc2_w", [128, HBLK, DIM])
        fc2_ws = sb("fc2_ws", [128, HBLK, DIM])
        cols = sb("cols", [128, 4])
        fg_w = sb("fg_w", [128, 2, 64])
        fg_b = sb("fg_b", [64, 4])
        wv = sb("wv", [128, DIM])
        ln_const = sb("ln_const", [128, 3, TPC])
        mask_max = sb("mask_max", [128, 1])
        mask_any = sb("mask_any", [128, 1])

        x_all = sb("x_all", [128, PAIRS, DIM])
        a_all = sb("a_all", [128, PAIRS, 2, HP, HD])
        ah = sb("ah", [128, 2, TPC, 128], F16)
        al = sb("al", [128, 2, TPC, 128], F16)
        a_t = sb("a_t", [128, 2, TPC, 2, 128], F16)
        xb = sb("xb", [128, 2, TPC, DIM])
        x1 = sb("x1", [128, 2, TPC, DIM])
        stats2 = sb("stats2", [128, 2, TPC, 6])
        mv2 = sb("mv2", [128, 2, TPC, 2])
        veps2 = sb("veps2", [128, 2, TPC])
        rstd2 = sb("rstd2", [128, 2, TPC])
        nmean2 = sb("nmean2", [128, 2, TPC])
        nmr2 = sb("nmr2", [128, 2, TPC])
        yn = sb("yn", [128, 2, CHUNK])
        yh = sb("yh", [128, 2, CHUNK], F16)
        yl = sb("yl", [128, 2, CHUNK], F16)
        y_t = sb("y_t", [128, 2, 2, CHUNK], F16)
        wait_here = sb("wait_here", [128, 1])
        until_mlp = ExitStack()
        mask_f = until_mlp.enter_context(nc.sbuf_tensor("mask_f", [128, 2, NWIN, WTOK], F32))
        mask16 = until_mlp.enter_context(nc.sbuf_tensor("mask16", [128, 3, 2, NWIN, WTOK], BF16))
        xn_all = until_mlp.enter_context(nc.sbuf_tensor("xn_all", [128, PAIRS, 2, 128], F16))
        v_hi = until_mlp.enter_context(nc.sbuf_tensor("v_hi", [128, 2, HP, 2, 2, HD + 1], F16))
        v_lo = until_mlp.enter_context(nc.sbuf_tensor("v_lo", [128, 2, HP, 2, 2, HD + 1], F16))

        q_rows = until_mlp.enter_context(nc.sbuf_tensor("q_rows", [128, 2, HEADS, ROWS], F16))
        k_rows = until_mlp.enter_context(nc.sbuf_tensor("k_rows", [128, 2, HEADS, ROWS], F16))
        k_t = until_mlp.enter_context(nc.sbuf_tensor("k_t", [128, 2, 4, 4, 128], F16))

        ps = ctx.enter_context(nc.psum_tensor("ps", [128, 8, 512], F32))

        const_loaded = sem("const_loaded")
        qkv_loaded = sem("qkv_loaded")
        mask_loaded = sem("mask_loaded")
        attn_loaded = sem("attn_loaded")
        rest_loaded = sem("rest_loaded")
        x_loaded = [sem(f"x_loaded{c}") for c in range(CHUNKS)]
        rows_set = sem("rows_set")
        v_set = sem("v_set")
        gains_ready = sem("gains_ready")
        qkv_w_scaled = sem("qkv_w_scaled")
        qkv_w_hi = sem("qkv_w_hi")
        qkv_w_lo = sem("qkv_w_lo")
        qkv_b_sum = sem("qkv_b_sum")
        qkv_b_ready = sem("qkv_b_ready")
        proj_w_scaled = sem("proj_w_scaled")
        proj_w_hi = sem("proj_w_hi")
        proj_w_lo = sem("proj_w_lo")
        mask_hi = sem("mask_hi")
        mask_rest = sem("mask_rest")
        mask_mid = sem("mask_mid")
        mask_lo = sem("mask_lo")
        mask_top = sem("mask_top")
        mask_known = sem("mask_known")
        fc1_b_sum = sem("fc1_b_sum")
        fc1_b_ready = sem("fc1_b_ready")
        fc1_w_scaled = sem("fc1_w_scaled")
        fc1_w_hi = sem("fc1_w_hi")
        fc1_w_lo = sem("fc1_w_lo")
        fc2_w_ready = sem("fc2_w_ready")
        ln_stats = sem("ln_stats")
        ln_pool = sem("ln_pool")
        ln_rstd = sem("ln_rstd")
        ln_norm = sem("ln_norm")
        ln_hi = sem("ln_hi")
        ln_lo = sem("ln_lo")
        ln_turned = sem("ln_turned")
        ln_ready = sem("ln_ready")

        qk_done = sem("qk_done")
        v_done = sem("v_done")
        rope_done = sem("rope_done")
        vhi_done = sem("vhi_done")
        vlo_done = sem("vlo_done")
        r_done = sem("r_done")
        hi_done = sem("hi_done")
        lo_done = sem("lo_done")
        t1_done = sem("t1_done")
        qt_ready = sem("qt_ready")
        kd_ready = sem("kd_ready")
        ka_ready = sem("ka_ready")
        s_done = sem("s_done")
        max_done = sem("max_done")
        mhi_done = sem("mhi_done")
        mlo_done = sem("mlo_done")
        t2_done = sem("t2_done")
        q2_ready = sem("q2_ready")
        st_done = sem("st_done")
        exp_done = sem("exp_done")
        phi_done = sem("phi_done")
        plo_done = sem("plo_done")
        pv_done = sem("pv_done")
        rec_done = sem("rec_done")
        norm_done = sem("norm_done")

        def wait(eng, s, value):
            if not isinstance(value, int) or value > 0:
                eng.wait_ge(s, value)

        block = ctx.enter_context(nc.Block())

        REST = ((fc1_w, "fc1_w"), (fc1_b, "fc1_b"), (fc2_w, "fc2_w"), (ident, "ident"), (proj_b, "proj_b"),
                (cols, "cols"), (fg_w, "fg_w"), (fg_b, "fg_b"), (wv, "wv"))
        REST_LOADS = 16 * len(REST)

        a_hi = sem("a_hi")
        a_lo = sem("a_lo")
        a_turned = sem("a_turned")
        at_ready = sem("at_ready")
        xb_ready = sem("xb_ready")
        prj_done = sem("prj_done")
        x1_ready = sem("x1_ready")
        l2_stats = sem("l2_stats")
        l2_pool = sem("l2_pool")
        l2_rstd = sem("l2_rstd")
        l2_norm = sem("l2_norm")
        l2_hi = sem("l2_hi")
        l2_lo = sem("l2_lo")
        l2_turned = sem("l2_turned")
        l2_ready = sem("l2_ready")
        gate_done = sem("gate_done")
        up_done = sem("up_done")
        silu_done = sem("silu_done")
        h_done = sem("h_done")
        h_used = sem("h_used")
        mlp_done = sem("mlp_done")
        x2_done = sem("x2_done")
        pads_set = sem("pads_set")
        AT_BANK, PRJ_BANK, YT_BANK, OUT_BANK = 4, 5, 0, 7
        GATE_BANK, UP_BANK = (1, 2), (3, 6)

        def in_range(c, lag):
            return not isinstance(c, int) or 0 <= c - lag < CHUNKS

        def mlp_pool(pool):
            def rstd_of(c, u):
                pool.wait_ge(l2_stats, c * 2 + 2)
                wait(pool, l2_norm, c - 1)
                pool.tensor_tensor(veps2[:, u, :], mv2[:, u, :, 1], ln_const[:, 1, :], ALU.add).then_inc(l2_pool, 1)
                pool.tensor_tensor(nmean2[:, u, :], mv2[:, u, :, 0], ln_const[:, 2, :], ALU.mult).then_inc(l2_pool, 1)
                pool.wait_ge(l2_pool, c * 3 + 2)
                pool.tensor_tensor(rstd2[:, u, :], veps2[:, u, :], ln_const[:, 0, :], ALU.pow).then_inc(l2_pool, 1)
                pool.wait_ge(l2_pool, c * 3 + 3)
                pool.tensor_tensor(nmr2[:, u, :], nmean2[:, u, :], rstd2[:, u, :], ALU.mult).then_inc(l2_rstd, 1)

            def low_of_a(c, u):
                pool.wait_ge(a_hi, c + 1)
                wait(pool, a_turned, c - 1)
                pool.tensor_tensor(al[:, u].rearrange("p t d -> p (t d)"),
                                   a_all[:, at(c * TPC, TPC)].rearrange("p t e h d -> p (t e h d)"),
                                   ah[:, u].rearrange("p t d -> p (t d)"), ALU.subtract).then_inc(a_lo, 1)

            def low_of_y(c, u):
                pool.wait_ge(l2_hi, c + 1)
                wait(pool, l2_turned, c - 1)
                pool.tensor_tensor(yl[:, u, :], yn[:, u, :], yh[:, u, :], ALU.subtract).then_inc(l2_lo, 1)

            def residual(c, u):
                pool.wait_ge(rest_loaded, REST_LOADS)
                wait(pool, x1_ready, c - 1)
                pool.tensor_tensor(xb[:, u], x_all[:, at(c * TPC, TPC)],
                                   proj_b[:].unsqueeze(1).broadcast_to([128, TPC, DIM]), ALU.add).then_inc(xb_ready, 1)

            def body(c, u):
                if in_range(c, 0):
                    rstd_of(c, u)
                if in_range(c, -1):
                    low_of_a(c + 1, 1 - u)
                if in_range(c, 0):
                    low_of_y(c, u)
                if in_range(c, -1):
                    residual(c + 1, 1 - u)

            def early(left):
                if left == 4:
                    low_of_a(0, 0)
                if left == 3:
                    residual(0, 0)
                if left == 1:
                    rstd_of(0, 0)
                    pool.wait_ge(fc1_w_hi, 1)
                    pool.tensor_tensor(fc1_w16[:, 1, :], w_scaled[:], fc1_w16[:, 0, :], ALU.subtract).then_inc(fc1_w_lo, 1)
                    low_of_y(0, 0)
                    low_of_a(1, 1)
                if left == 0:
                    residual(1, 1)

            def pads():
                pool.wait_ge(xb_ready, 3)
                for k, (rows, value) in enumerate(((f_rows[64:128], 0.0), (g_rows[64:128], 0.0), (mh[:], 0.0),
                                                   (g_rows[64:65], MSCALE), (g_rows[96:97], 1.0))):
                    wait(pool, pads_set, k)
                    pool.memset(rows, value).then_inc(pads_set, 1)
                pool.wait_ge(pads_set, 5)

            return body, early, pads

        def mlp_pe(pe):
            def fc1(b, v, k):
                if k == 0:
                    pe.wait_ge(l2_ready, b + 1)
                for block_, bank, done, used in ((HBLK + k, GATE_BANK[k % 2], gate_done, silu_done),
                                                 (k, UP_BANK[k % 2], up_done, h_done)):
                    wait(pe, used, b * HBLK + k - 1)
                    for n, (ws, ys) in enumerate(((0, 0), (1, 0), (0, 1))):
                        last = pe.matmul(ps[:, bank, :], fc1_w16[:, ws, 128 * block_:128 * block_ + 128],
                                         y_t[:, v, ys, :], start=(n == 0), stop=(n == 2))
                    last.then_inc(done, 1)

            def fc2(b, k):
                if k == 0:
                    wait(pe, x2_done, b)
                pe.wait_ge(h_done, b * HBLK + k + 1)
                pe.matmul(ps[:, OUT_BANK, :], fc2_ws[:, k, :], hid[:, k % 2, :], start=(k == 0), stop=False,
                          skip_group_check=True).then_inc(h_used, 1)

            def project(c, u):
                pe.wait_ge(at_ready, c + 1)
                wait(pe, x1_ready, c)
                for k in range(TPC):
                    for n, (xs, ws) in enumerate(((0, 0), (0, 1), (1, 0))):
                        last = pe.matmul(ps[:, PRJ_BANK, 128 * k:128 * k + 128], a_t[:, u, k, xs, :],
                                         proj_w16[:, ws, :], start=(k == 0 and n == 0), stop=(n == 2),
                                         skip_group_check=True)
                last.then_inc(prj_done, 1)

            def turn_a_waits(c):
                pe.wait_ge(a_lo, c + 1)
                wait(pe, at_ready, c)

            def turn_a(u):
                out = ps[:, AT_BANK, :].bitcast(F16).rearrange("p (t s q) -> p t s q", t=TPC, s=2)
                for s, src in enumerate((ah, al)):
                    for k in range(TPC):
                        for e in range(2):
                            for r in range(2):
                                rows = slice(64 * r, 64 * r + 64)
                                last = pe.transpose(out[rows, k, s, 64 * e:64 * e + 64],
                                                    src[rows, u, k, 64 * e:64 * e + 64], ident16[rows, rows])
                last.then_inc(a_turned, 1)

            def turn_y(c, u):
                pe.wait_ge(l2_lo, c + 1)
                wait(pe, l2_ready, c)
                out = ps[:, YT_BANK, :].bitcast(F16).rearrange("p (s t q) -> p s t q", s=2, t=TPC)
                for s, src in enumerate((yh, yl)):
                    for k in range(TPC):
                        last = pe.transpose(out[:, s, k, :], src[:, u, 128 * k:128 * k + 128], ident16[:])
                last.then_inc(l2_turned, 1)

            def body(c, u):
                v = 1 - u
                if in_range(c, 0):
                    project(c, u)
                if in_range(c, 1):
                    for k in range(HBLK):
                        fc1(c - 1, v, k)
                        if 1 <= k < HBLK - 1:
                            fc2(c - 1, k - 1)
                if in_range(c, -1):
                    turn_a_waits(c + 1)
                if in_range(c, 1):
                    fc2(c - 1, HBLK - 2)
                if in_range(c, -1):
                    turn_a(v)
                if in_range(c, 0):
                    turn_y(c, u)
                if in_range(c, 1):
                    fc2(c - 1, HBLK - 1)
                    for k in range(TPC):
                        last = pe.matmul(ps[:, OUT_BANK, 128 * k:128 * k + 128], x1[:, v, k, :], ident[:],
                                         start=False, stop=True, skip_group_check=True)
                    last.then_inc(mlp_done, 1)

            def early(left):
                if left == 3:
                    turn_a_waits(0)
                    turn_a(0)
                if left == 2:
                    project(0, 0)
                    pe.wait_ge(rest_loaded, REST_LOADS)
                    for k in range(2 * HBLK):
                        last = pe.matmul(ps[:, GATE_BANK[0], k:k + 1], fc1_w[:, 128 * k:128 * k + 128], g1b1[:, 3:4],
                                         start=True, stop=True)
                    last.then_inc(fc1_b_sum, 1)
                if left == 0:
                    turn_y(0, 0)
                    turn_a_waits(1)
                    turn_a(1)

            return body, early

        def mlp_dve(dve):
            def hidden(b, k):
                dve.wait_ge(up_done, b * HBLK + k + 1)
                dve.wait_ge(silu_done, b * HBLK + k + 1)
                wait(dve, h_used, b * HBLK + k - 1)
                dve.scalar_tensor_tensor(out=hid[:, k % 2, :], in0=ps[:, UP_BANK[k % 2], :],
                                         scalar=fc1_bias[:, k:k + 1], in1=sg[:, k % 2, :], op0=ALU.add,
                                         op1=ALU.mult).then_inc(h_done, 1)

            def residual_sum(c, u):
                dve.wait_ge(prj_done, c + 1)
                dve.wait_ge(xb_ready, c + 1)
                wait(dve, mlp_done, c - 1)
                dve.scalar_tensor_tensor(out=x1[:, u].rearrange("p t q -> p (t q)"), in0=ps[:, PRJ_BANK, :],
                                         scalar=1.0 / WSCALE, in1=xb[:, u].rearrange("p t q -> p (t q)"),
                                         op0=ALU.mult, op1=ALU.add).then_inc(x1_ready, 1)
                dve.wait_ge(x1_ready, c + 1)
                wait(dve, l2_rstd, c - 1)
                for k in range(TPC):
                    last = dve.bn_stats(stats2[:, u, k, :], x1[:, u, k, :])
                last.then_inc(l2_stats, 1)

            def statistics(c, u):
                dve.wait_ge(l2_stats, c * 2 + 1)
                dve.memset(wait_here[:], 0.0)
                for k in range(TPC):
                    last = dve.bn_aggr(mv2[:, u, k, :], stats2[:, u, k, :])
                last.then_inc(l2_stats, 1)

            def normalise(c, u):
                dve.wait_ge(l2_rstd, c + 1)
                wait(dve, l2_lo, c - 1)
                for k in range(TPC):
                    last = dve.tensor_scalar(yn[:, u, 128 * k:128 * k + 128], x1[:, u, k, :],
                                             rstd2[:, u, k:k + 1], nmr2[:, u, k:k + 1], ALU.mult, ALU.add)
                last.then_inc(l2_norm, 1)

            def turned_a(c, u):
                dve.wait_ge(a_turned, c + 1)
                wait(dve, prj_done, c - 1)
                dve.tensor_copy(a_t[:, u].rearrange("p t s q -> p (t s q)"), ps[:, AT_BANK, :].bitcast(F16))\
                    .then_inc(at_ready, 1)

            def turned_y(c, u):
                dve.wait_ge(l2_turned, c + 1)
                dve.tensor_copy(y_t[:, u].rearrange("p s q -> p (s q)"), ps[:, YT_BANK, :].bitcast(F16))\
                    .then_inc(l2_ready, 1)

            def body(c, u):
                if in_range(c, 0):
                    residual_sum(c, u)
                if in_range(c, 1):
                    hidden(c - 1, 0)
                if in_range(c, 0):
                    statistics(c, u)
                if in_range(c, 1):
                    hidden(c - 1, 1)
                if in_range(c, 0):
                    normalise(c, u)
                if in_range(c, 1):
                    hidden(c - 1, 2)
                    hidden(c - 1, 3)
                if in_range(c, -1):
                    turned_a(c + 1, 1 - u)
                if in_range(c, 0):
                    turned_y(c, u)

            def early(left):
                if left == 3:
                    turned_a(0, 0)
                if left == 2:
                    residual_sum(0, 0)
                    statistics(0, 0)
                if left == 1:
                    dve.wait_ge(rest_loaded, REST_LOADS)
                    dve.wait_ge(fc1_b_sum, 1)
                    dve.tensor_tensor(fc1_bias[:], ps[:, GATE_BANK[0], 0:2 * HBLK], fc1_b[:], ALU.add)\
                        .then_inc(fc1_b_ready, 1)
                    dve.wait_ge(fc1_b_ready, 1)
                    dve.tensor_scalar(fc1_bias[:, 0:HBLK], fc1_bias[:, 0:HBLK], WSCALE, None, ALU.mult)\
                        .then_inc(fc1_b_ready, 1)
                    normalise(0, 0)
                if left == 0:
                    turned_y(0, 0)
                    turned_a(1, 1)

            return body, early

        def mlp_act(act):
            def gate(b, k):
                act.wait_ge(gate_done, b * HBLK + k + 1)
                wait(act, h_done, b * HBLK + k - 1)
                act.activation(sg[:, k % 2, :], ps[:, GATE_BANK[k % 2], :], ACT.Silu,
                               bias=fc1_bias[:, HBLK + k:HBLK + k + 1], scale=1.0 / WSCALE).then_inc(silu_done, 1)

            def high_of_a(c, u):
                act.wait_ge(norm_done, min(c * TPC + TPC, PAIRS) if isinstance(c, int) else PAIRS)
                wait(act, a_turned, c - 1)
                wait(act, a_lo, c - 1)
                act.activation(ah[:, u].rearrange("p t d -> p (t d)"),
                               a_all[:, at(c * TPC, TPC)].rearrange("p t e h d -> p (t e h d)"), ACT.Copy)\
                    .then_inc(a_hi, 1)

            def high_of_y(c, u):
                act.wait_ge(l2_norm, c + 1)
                wait(act, l2_turned, c - 1)
                act.activation(yh[:, u, :], yn[:, u, :], ACT.Copy).then_inc(l2_hi, 1)

            def body(c, u):
                if in_range(c, 2):
                    act.wait_ge(mlp_done, c - 1)
                    act.activation(x2_all[:, :, at(c * 2 - 4, 2), :],
                                   ps[:, OUT_BANK, :].rearrange("p (w b q) -> p b w q", w=2, b=B),
                                   ACT.Identity, bias=cols[:, 0:1], scale=1.0).then_inc(x2_done, 1)
                if in_range(c, 1):
                    gate(c - 1, 0)
                    gate(c - 1, 1)
                if in_range(c, -1):
                    high_of_a(c + 1, 1 - u)
                if in_range(c, 1):
                    gate(c - 1, 2)
                if in_range(c, 0):
                    high_of_y(c, u)
                if in_range(c, 1):
                    gate(c - 1, 3)

            def early(left):
                if left == 4:
                    high_of_a(0, 0)
                if left == 3:
                    act.wait_ge(rest_loaded, REST_LOADS)
                    act.activation(w_scaled[:], fc1_w[:], ACT.Identity, bias=0.0, scale=gains[:, 2:3])\
                        .then_inc(fc1_w_scaled, 1)
                if left == 2:
                    act.wait_ge(fc1_w_scaled, 1)
                    act.activation(fc1_w16[:, 0, :], w_scaled[:], ACT.Copy).then_inc(fc1_w_hi, 1)
                if left == 1:
                    high_of_a(1, 1)
                    high_of_y(0, 0)
                    act.activation(fc2_ws[:].rearrange("p k d -> p (k d)"), fc2_w[:].rearrange("p k d -> p (k d)"),
                                   ACT.Copy, scale=1.0 / WSCALE).then_inc(fc2_w_ready, 1)

            return body, early


        with ExitStack() as st:
            def tmp(name, shape, dt=F32):
                return st.enter_context(nc.sbuf_tensor(name, shape, dt))

            stats = tmp("stats", [128, CHUNKS, TPC, 6])
            mv = tmp("mv", [128, CHUNKS, TPC, 2])
            veps = tmp("veps", [128, CHUNKS, TPC])
            rstd = tmp("rstd", [128, CHUNKS, TPC])
            nmean = tmp("nmean", [128, CHUNKS, TPC])
            nmr = tmp("nmr", [128, CHUNKS, TPC])
            warm = tmp("warm", [128, 1])
            xn = tmp("xn", [128, 2, CHUNK])
            xh = tmp("xh", [128, 2, CHUNK], F16)
            xl = tmp("xl", [128, 2, CHUNK], F16)
            mrest = tmp("mrest", [128, 2, NWIN, WTOK])
            ta = tmp("ta", [128, 2, 2, HEADS, HD])
            tb = tmp("tb", [128, 2, 2, HEADS, HD])
            rot = tmp("rot", [128, 2, 2, HEADS, HD])
            q_t = tmp("q_t", [128, 2, 4, 128], F16)
            q_t2 = tmp("q_t2", [128, 2, 4, 128], F16)
            mx = tmp("mx", [128, 2, HEADS])
            e_buf = tmp("e_buf", [128, 2, HEADS, WTOK])
            p_hi = tmp("p_hi", [128, 2, HEADS, WTOK], F16)
            p_lo = tmp("p_lo", [128, 2, HEADS, WTOK], F16)
            rec = tmp("rec", [128, 2, HP, 2])

            S_BANK, ST_BANK, QKV_BANK, T1_BANK, T2_BANK, PV_BANK = 0, 2, 4, 5, 6, 7
            qkv_ps = ps[:, QKV_BANK, :]
            v_ps = ps[:, T2_BANK, 256:256 + DIM]
            t1_ps = ps[:, T1_BANK, :].bitcast(F16).rearrange("p (a c q) -> p a c q", a=2, c=4)
            t2_ps = ps[:, T2_BANK, 0:256].bitcast(F16).rearrange("p (c q) -> p c q", c=4)
            pv_ps = ps[:, PV_BANK, 0:HP * 4 * (HD + 1)].rearrange("p (h e r d) -> p h e r d", h=HP, e=2, r=2)

            FIRST, LAST = -2, PAIRS + 2
            LOOP_FROM, LOOP_TO = 4, PAIRS - 2
            EARLY = 3

            def nothing(c):
                pass

            def peeled(body, norm, low, turn, numbers):
                for n in numbers:
                    c = n - FIRST + EARLY
                    if c < CHUNKS:
                        low(c)
                    body(n, n // 2, n % 2)
                    if c < CHUNKS:
                        turn(c)
                    if c + 1 < CHUNKS:
                        norm(c + 1)

            def first_steps(eng, body, norm=nothing, low=nothing, turn=nothing):
                peeled(body, norm, low, turn, range(FIRST, 0))

            def other_steps(eng, body, mlp_early, norm=nothing, low=nothing, turn=nothing):
                peeled(body, norm, low, turn, range(0, LOOP_FROM))
                with eng.Fori(LOOP_FROM // 2, LOOP_TO // 2) as it:
                    for u in range(2):
                        body(it * 2 + u, it, u)
                for n in range(LOOP_TO, LAST + 1):
                    body(n, n // 2, n % 2)
                    mlp_early(LAST - n)

            def steps(eng, body, mlp_early, **parts):
                first_steps(eng, body, **parts)
                other_steps(eng, body, mlp_early, **parts)

            def valid(n, lag):
                return not isinstance(n, int) or 0 <= n - lag < PAIRS

            def turned_keys(copy, u, groups):
                for j in groups:
                    rows = slice(ROWS * j, ROWS * j + ROWS)
                    last = copy(k_t[rows, u, j], t1_ps[rows, 1])
                return last

            ATTN = ((sel33, "sel33"), (rope, "rope"), (identb, "identb"), (proj_w, "proj_w"))
            @block.sync
            def _(sp):
                for c in range(CHUNKS):
                    sp.dma_start(x_all[:, TPC * c:TPC * c + TPC, :],
                                 t["x"][:, TPC * c:TPC * c + TPC, :]).then_inc(x_loaded[c], 16)
                for dst, name in REST:
                    sp.dma_start(dst[:], t[name]).then_inc(rest_loaded, 16)

            @block.tensor
            def _(pe):
                def ln_turn(c):
                    pe.wait_ge(ln_lo, c + 1)
                    wait(pe, ln_ready, c)
                    out = ps[:, PV_BANK, :].bitcast(F16).rearrange("p (t s q) -> p t s q", s=2, t=TPC)
                    for s, src in enumerate((xh, xl)):
                        for k in range(TPC):
                            last = pe.transpose(out[:, k, s, :], src[:, c % 2, 128 * k:128 * k + 128], ident16[:])
                    last.then_inc(ln_turned, 1)

                pe.wait_ge(const_loaded, 32)
                ln_turn(0)
                pe.wait_ge(qkv_loaded, 48)
                pe.matmul(ps[0:33, S_BANK, 0:3 * DIM], g1b1[:, 1:2].broadcast_to([128, 33]), qkv_w[:], start=True,
                          stop=True).then_inc(qkv_b_sum, 1)
                ln_turn(1)
                ln_turn(2)
                pe.wait_ge(qkv_w_lo, 1)
                pe.wait_ge(qkv_b_ready, 3)
                pe.wait_ge(attn_loaded, 16 * len(ATTN))
                pe.wait_ge(v_set, 4)
                pe.wait_ge(rows_set, 4)

                def project(out, i, cols):
                    for n, (xs, ws) in enumerate(((0, 0), (0, 1), (1, 0))):
                        pe.matmul(out, xn_all[:, at(i, 1), xs, :].rearrange("p a q -> p (a q)"),
                                  qkv_w16[:, ws, cols], start=(n == 0), stop=False, skip_group_check=True)
                    return pe.matmul(out, sel33[:], qkv_b16[:, cols], start=False, stop=True,
                                     skip_group_check=True)

                def scores(bank, left, right, w, side, parts):
                    for part in range(parts):
                        for b in range(2):
                            mm = mask16[:, part, side, at(w, 1), :].broadcast_to([128, 8, WTOK])
                            pe.matmul(ps[:, bank + b, :].rearrange("p (h k) -> p h k", h=8), identb[:], mm,
                                      start=(part == 0), stop=False, skip_group_check=True)
                    for h in range(HEADS):
                        for e in range(2):
                            last = pe.matmul(
                                ps[64 * e:64 * e + 64, bank + h // 8, WTOK * (h % 8):WTOK * (h % 8) + WTOK],
                                left(h, e), right(h, e), start=False, stop=True, skip_group_check=True)
                    return last

                def turn(out, rows):
                    for c in range(4):
                        last = pe.transpose(out[:, c, :], rows[:, 4 * c:4 * c + 4, :].rearrange("p h r -> p (h r)"),
                                            ident16[:])
                    return last

                def body(n, it, u, parts):
                    v = 1 - u

                    def queries(buf, par):
                        return lambda h, e: buf[:, par, h // 4, 64 * e:64 * e + 64]

                    def keys(par):
                        return lambda h, e: k_t[:, par, h % 4, h // 4, 64 * e:64 * e + 64]

                    if valid(n, -2):
                        wait(pe, rope_done, n + 2)
                        pe.wait_ge(ln_ready, (n + 2) // TPC + 1 if isinstance(n, int) and n < LOOP_FROM else CHUNKS)
                        project(qkv_ps[:, 0:2 * DIM], n + 2, slice(0, 2 * DIM)).then_inc(qk_done, 1)
                    if valid(n, 0):
                        wait(pe, kd_ready, n + 1)
                        wait(pe, ka_ready, n + 1)
                        wait(pe, max_done, n)
                        scores(S_BANK, queries(q_t, u), keys(u), it, 0, parts).then_inc(s_done, 1)
                    if valid(n, 1):
                        wait(pe, q2_ready, n)
                        wait(pe, exp_done, n - 1)
                        scores(ST_BANK, keys(v), queries(q_t2, v), it if u else it - 1, 1, parts).then_inc(st_done, 1)
                    if valid(n, -1):
                        wait(pe, lo_done, n + 2)
                        wait(pe, kd_ready, n + 1)
                        wait(pe, ka_ready, n + 1)
                        turn(t1_ps[:, 0], q_rows[:, v])
                        turn(t1_ps[:, 1], k_rows[:, v]).then_inc(t1_done, 1)
                    if valid(n, 3):
                        wait(pe, plo_done, n - 2)
                        wait(pe, norm_done, n - 3)
                        pe.wait_ge(ln_ready, CHUNKS)
                        for hp in range(HP):
                            out = pv_ps[:, hp].rearrange("p e r d -> p (e r d)")
                            for k, (p, w) in enumerate(((p_hi, v_hi), (p_hi, v_lo), (p_lo, v_hi))):
                                last = pe.matmul(out, p[:, v, 2 * hp:2 * hp + 2, :].rearrange("p h q -> p (h q)"),
                                                 w[:, v, hp].rearrange("p e r d -> p (e r d)"),
                                                 start=(k == 0 and hp == 0), stop=(k == 2), skip_group_check=True)
                        last.then_inc(pv_done, 1)
                    if valid(n, 1):
                        wait(pe, vlo_done, n - 1)
                        wait(pe, q2_ready, n)
                        project(v_ps, n - 1, slice(2 * DIM, 3 * DIM)).then_inc(v_done, 1)
                    if valid(n, 0):
                        wait(pe, mlo_done, n + 1)
                        wait(pe, q2_ready, n)
                        turn(t2_ps, q_rows[:, u]).then_inc(t2_done, 1)

                first_steps(pe, lambda n, it, u: body(n, it, u, 1), turn=ln_turn)
                pe.wait_ge(mask_hi, 1)
                pe.wait_ge(mask_known, 1)
                rest = pe.value_load(mask_any[0:1, 0:1].bitcast(mybir.dt.int32))
                with pe.If(rest > 0):
                    pe.wait_ge(mask_lo, 1)
                    other_steps(pe, lambda n, it, u: body(n, it, u, 3), mlp_pe(pe)[1], turn=ln_turn)
                with pe.If(rest < 1):
                    other_steps(pe, lambda n, it, u: body(n, it, u, 1), mlp_pe(pe)[1], turn=ln_turn)

            @block.vector
            def _(dve):
                for rows in (k_t, q_rows, k_rows):
                    dve.memset(rows[:].bitcast(F32), 0.0).then_inc(rows_set, 1)
                dve.wait_ge(rows_set, 3)
                dve.memset(k_rows[:, :, :, MAXROW:MAXROW + 2], MSCALE).then_inc(rows_set, 1)

                def ln_stats_of(c):
                    dve.wait_ge(x_loaded[c], 16)
                    for k in range(TPC):
                        last = dve.bn_stats(stats[:, c, k, :], x_all[:, TPC * c + k, :])
                    last.then_inc(ln_stats, 1)
                    dve.wait_ge(ln_stats, 2 * c + 1)
                    for k in range(TPC):
                        last = dve.bn_aggr(mv[:, c, k, :], stats[:, c, k, :])
                    last.then_inc(ln_stats, 1)

                def ln_norm_of(c):
                    dve.wait_ge(ln_rstd, c + 1)
                    if c >= 2:
                        dve.wait_ge(ln_lo, c - 1)
                        dve.wait_ge(ln_hi, c - 1)
                    for k in range(TPC):
                        last = dve.tensor_scalar(xn[:, c % 2, 128 * k:128 * k + 128], x_all[:, TPC * c + k, :],
                                                 rstd[:, c, k:k + 1], nmr[:, c, k:k + 1], ALU.mult, ALU.add)
                    last.then_inc(ln_norm, 1)

                ln_stats_of(0)
                ln_stats_of(1)
                dve.wait_ge(qkv_loaded, 48)
                dve.tensor_scalar(gains[:], g1b1[:], WSCALE, None, ALU.mult).then_inc(gains_ready, 1)
                ln_norm_of(0)
                ln_stats_of(2)
                ln_norm_of(1)
                ln_stats_of(3)
                dve.wait_ge(qkv_b_sum, 1)
                dve.tensor_tensor(b_sum[:], ps[0:33, S_BANK, 0:3 * DIM], qkv_b[:], ALU.add).then_inc(qkv_b_ready, 1)
                ln_norm_of(2)
                dve.wait_ge(qkv_b_ready, 1)
                dve.tensor_scalar(qkv_b16[:], b_sum[:], WSCALE, None, ALU.mult).then_inc(qkv_b_ready, 1)
                dve.wait_ge(qkv_b_ready, 2)
                dve.scalar_tensor_tensor(out=qkv_b16[32:33, :], in0=b_sum[32:33, :], scalar=WSCALE,
                                         in1=qkv_b16[32:33, :], op0=ALU.mult, op1=ALU.subtract).then_inc(qkv_b_ready, 1)
                dve.wait_ge(mask_hi, 1)
                dve.tensor_tensor(mrest[:], mask_f[:], mask16[:, 0], ALU.subtract).then_inc(mask_rest, 1)
                ln_norm_of(3)
                ln_stats_of(EARLY + 1)

                def norm(c):
                    if c == EARLY + 1:
                        dve.wait_ge(mask_mid, 1)
                        dve.tensor_reduce(mask_max[:], mask16[:, 1, 0].rearrange("p w k -> p (w k)"), AX.X, ALU.max,
                                          apply_absolute_value=True).then_inc(mask_top, 1)
                    ln_norm_of(c)
                    if c + 1 < CHUNKS:
                        ln_stats_of(c + 1)

                dve.wait_ge(attn_loaded, 16 * len(ATTN))

                def body(n, it, u):
                    v = 1 - u
                    if valid(n, -2):
                        dve.wait_ge(qk_done, n + 3)
                        wait(dve, r_done, n + 1)
                        x = qkv_ps[:, 0:2 * DIM].rearrange("p (a h d) -> p a h d", a=2, h=HEADS)
                        for dst, k in ((ta, 0), (tb, 1)):
                            last = dve.tensor_tensor(dst[:, u], x,
                                                     rope[:, k].unsqueeze(2).broadcast_to([128, 2, HEADS, HD]), ALU.mult)
                        last.then_inc(rope_done, 1)
                    if valid(n, 2):
                        dve.wait_ge(vhi_done, n - 1)
                        for e in range(2):
                            rows = slice(64 * e, 64 * e + 64)
                            last = dve.tensor_tensor(
                                v_lo[rows, u, :, e, :, 0:HD], v_ps[rows, :].rearrange("p (h r d) -> p h r d", r=2, d=HD),
                                v_hi[rows, u, :, e, :, 0:HD], ALU.subtract)
                        last.then_inc(vlo_done, 1)
                    if valid(n, 0):
                        dve.wait_ge(s_done, n + 1)
                        dve.tensor_reduce(mx[:, u, :], ps[:, S_BANK:S_BANK + 2, :].rearrange("p b (h k) -> p (b h) k", h=8),
                                          AX.X, ALU.max).then_inc(max_done, 1)
                        dve.wait_ge(max_done, n + 1)
                        hi = q_rows[:, u, :, MAXROW]
                        lo = q_rows[:, u, :, MAXROW + 1]
                        dve.tensor_scalar(hi, mx[:, u, :], -1.0 / MSCALE, None, ALU.mult).then_inc(mhi_done, 1)
                        dve.wait_ge(mhi_done, n + 1)
                        dve.scalar_tensor_tensor(out=lo, in0=mx[:, u, :], scalar=-1.0 / MSCALE, in1=hi,
                                                 op0=ALU.mult, op1=ALU.subtract).then_inc(mlo_done, 1)
                    if valid(n, -1):
                        dve.wait_ge(t1_done, n + 2)
                        dve.tensor_copy(q_t[:, v], t1_ps[:, 0]).then_inc(qt_ready, 1)
                        turned_keys(dve.tensor_copy, v, (0, 1)).then_inc(kd_ready, 1)
                    if valid(n, 3):
                        i = n - 3
                        dve.wait_ge(pv_done, n - 2)
                        for r in range(2):
                            rows = slice(64 * r, 64 * r + 64)
                            last = dve.reciprocal(rec[rows, v], pv_ps[rows, :, :, r, HD])
                        last.then_inc(rec_done, 1)
                        dve.wait_ge(rec_done, n - 2)
                        for r in range(2):
                            rows = slice(64 * r, 64 * r + 64)
                            last = dve.tensor_tensor(
                                a_all[rows, at(i, 1)].rearrange("p a e h d -> p h (a e) d"),
                                pv_ps[rows, :, :, r, 0:HD],
                                rec[rows, v].unsqueeze(3).broadcast_to([64, HP, 2, HD]), ALU.mult)
                        last.then_inc(norm_done, 1)

                steps(dve, body, mlp_dve(dve)[1], norm=norm)

            @block.scalar
            def _(act):
                for dst, name in ((ln_const, "ln_const"), (ident16, "ident16")):
                    act.dma_start(dst[:], t[name]).then_inc(const_loaded, 16)
                for dst, name in ((g1b1, "g1b1"), (qkv_w, "qkv_w"), (qkv_b, "qkv_b")):
                    act.dma_start(dst[:], t[name]).then_inc(qkv_loaded, 16)
                act.dma_start(mask_f[:], t["mask"]).then_inc(mask_loaded, 16)
                for dst, name in ATTN:
                    act.dma_start(dst[:], t[name]).then_inc(attn_loaded, 16)

                def copy(out, in_):
                    return act.activation(out, in_, ACT.Copy)

                def ln_hi_of(c):
                    act.wait_ge(ln_norm, c + 1)
                    if c >= 2:
                        act.wait_ge(ln_turned, c - 1)
                        act.wait_ge(ln_lo, c - 1)
                    copy(xh[:, c % 2, :], xn[:, c % 2, :]).then_inc(ln_hi, 1)

                def ln_turned_of(c):
                    act.wait_ge(ln_turned, c + 1)
                    copy(xn_all[:, TPC * c:TPC * c + TPC].rearrange("p t s q -> p (t s q)"),
                         ps[:, PV_BANK, :].bitcast(F16)).then_inc(ln_ready, 1)

                act.wait_ge(v_set, 4)
                act.wait_ge(rows_set, 4)
                act.activation(warm[:], v_hi[:, 0, 0, 0, 0, 0:1], ACT.Exp)
                ln_hi_of(0)
                act.wait_ge(gains_ready, 1)
                act.activation(w_scaled[:, 0:3 * DIM], qkv_w[:], ACT.Identity, bias=0.0, scale=gains[:, 0:1])\
                    .then_inc(qkv_w_scaled, 1)
                act.wait_ge(qkv_w_scaled, 1)
                copy(qkv_w16[:, 0, :], w_scaled[:, 0:3 * DIM]).then_inc(qkv_w_hi, 1)
                ln_hi_of(1)
                ln_turned_of(0)
                act.wait_ge(mask_loaded, 16)
                copy(mask16[:, 0], mask_f[:]).then_inc(mask_hi, 1)
                ln_turned_of(1)
                ln_hi_of(2)
                ln_turned_of(2)
                act.wait_ge(mask_rest, 1)
                copy(mask16[:, 1], mrest[:]).then_inc(mask_mid, 1)
                ln_hi_of(3)
                act.wait_ge(attn_loaded, 16 * len(ATTN))
                act.activation(proj_ws[:], proj_w[:], ACT.Copy, scale=WSCALE).then_inc(proj_w_scaled, 1)
                act.wait_ge(proj_w_scaled, 1)
                copy(proj_w16[:, 0, :], proj_ws[:]).then_inc(proj_w_hi, 1)

                def body(n, it, u):
                    v = 1 - u
                    if valid(n, 1):
                        act.wait_ge(st_done, n)
                        wait(act, plo_done, n - 2)
                        act.activation(e_buf[:, v], ps[:, ST_BANK:ST_BANK + 2, :].rearrange("p b (h q) -> p (b h) q", h=8),
                                       ACT.Exp).then_inc(exp_done, 1)
                    if valid(n, -1):
                        act.wait_ge(qt_ready, n + 2)
                        turned_keys(copy, v, (2, 3)).then_inc(ka_ready, 1)
                    if valid(n, 0):
                        act.wait_ge(t2_done, n + 1)
                        copy(q_t2[:, u], t2_ps).then_inc(q2_ready, 1)
                    if valid(n, 1):
                        act.wait_ge(v_done, n)
                        wait(act, pv_done, n - 2)
                        for e in range(2):
                            rows = slice(64 * e, 64 * e + 64)
                            last = copy(v_hi[rows, v, :, e, :, 0:HD],
                                        v_ps[rows, :].rearrange("p (h r d) -> p h r d", r=2, d=HD))
                        last.then_inc(vhi_done, 1)
                    if valid(n, -2):
                        act.wait_ge(r_done, n + 3)
                        copy(q_rows[:, u, :, 0:16].rearrange("p h (r d) -> p h r d", r=2),
                             rot[:, u, 0].unsqueeze(2).broadcast_to([128, HEADS, 2, HD]))
                        copy(k_rows[:, u].rearrange("p h (r d) -> p h r d", d=HD)[:, :, 0:3:2, :],
                             rot[:, u, 1].unsqueeze(2).broadcast_to([128, HEADS, 2, HD])).then_inc(hi_done, 1)
                    if valid(n, 1):
                        act.wait_ge(exp_done, n)
                        wait(act, pv_done, n - 2)
                        copy(p_hi[:, v], e_buf[:, v]).then_inc(phi_done, 1)

                steps(act, body, mlp_act(act)[1], norm=ln_hi_of, turn=ln_turned_of)

            @block.gpsimd
            def _(pool):
                for k, (part, value) in enumerate(((v_hi[:], 0.0), (v_lo[:], 0.0),
                                                   (v_hi[0:64, :, :, 0, :, HD:HD + 1], WSCALE),
                                                   (v_hi[64:128, :, :, 1, :, HD:HD + 1], WSCALE))):
                    if k >= 1:
                        pool.wait_ge(v_set, k)
                    pool.memset(part, value).then_inc(v_set, 1)
                pool.wait_ge(v_set, 4)
                pool.wait_ge(const_loaded, 32)

                def ln_rstd_of(c):
                    pool.wait_ge(ln_stats, 2 * c + 2)
                    pool.tensor_tensor(veps[:, c, :], mv[:, c, :, 1], ln_const[:, 1, :], ALU.add).then_inc(ln_pool, 1)
                    pool.tensor_tensor(nmean[:, c, :], mv[:, c, :, 0], ln_const[:, 2, :], ALU.mult).then_inc(ln_pool, 1)
                    pool.wait_ge(ln_pool, 3 * c + 2)
                    pool.tensor_tensor(rstd[:, c, :], veps[:, c, :], ln_const[:, 0, :], ALU.pow).then_inc(ln_pool, 1)
                    pool.wait_ge(ln_pool, 3 * c + 3)
                    pool.tensor_tensor(nmr[:, c, :], nmean[:, c, :], rstd[:, c, :], ALU.mult).then_inc(ln_rstd, 1)

                def ln_lo_of(c):
                    pool.wait_ge(ln_hi, c + 1)
                    if c >= 2:
                        pool.wait_ge(ln_turned, c - 1)
                    pool.tensor_tensor(xl[:, c % 2, :], xn[:, c % 2, :], xh[:, c % 2, :], ALU.subtract)\
                        .then_inc(ln_lo, 1)

                ln_rstd_of(0)
                ln_rstd_of(1)
                ln_lo_of(0)
                ln_rstd_of(2)
                ln_lo_of(1)
                pool.wait_ge(qkv_w_hi, 1)
                pool.tensor_tensor(qkv_w16[:, 1, :], w_scaled[:, 0:3 * DIM], qkv_w16[:, 0, :], ALU.subtract)\
                    .then_inc(qkv_w_lo, 1)
                ln_rstd_of(3)
                ln_lo_of(2)
                ln_rstd_of(EARLY + 1)

                def norm(c):
                    if c == EARLY + 1:
                        pool.wait_ge(mask_top, 1)
                        pool.partition_all_reduce(mask_any[:], mask_max[:], 128, bass.bass_isa.ReduceOp.max)\
                            .then_inc(mask_known, 1)
                    if c + 1 < CHUNKS:
                        ln_rstd_of(c + 1)
                    if c + 1 == CHUNKS:
                        pool.wait_ge(proj_w_hi, 1)
                        pool.tensor_tensor(proj_w16[:, 1, :], proj_ws[:], proj_w16[:, 0, :], ALU.subtract)\
                            .then_inc(proj_w_lo, 1)
                    if c == EARLY + 2:
                        pool.wait_ge(mask_known, 1)
                        with pool.If(pool.value_load(mask_any[0:1, 0:1].bitcast(mybir.dt.int32)) > 0):
                            pool.tensor_tensor(mask16[:, 2].rearrange("p s w k -> p (s w k)"),
                                               mrest[:].rearrange("p s w k -> p (s w k)"),
                                               mask16[:, 1].rearrange("p s w k -> p (s w k)"), ALU.subtract)\
                                .then_inc(mask_lo, 1)

                pool.wait_ge(rows_set, 4)

                def body(n, it, u):
                    v = 1 - u
                    if valid(n, -1):
                        pool.wait_ge(hi_done, n + 2)
                        pool.tensor_tensor(q_rows[:, v, :, 16:24], rot[:, v, 0], q_rows[:, v, :, 0:8], ALU.subtract)
                        pool.memset(q_rows[:, v, :, MAXROW:MAXROW + 2], 0.0)
                        pool.tensor_tensor(k_rows[:, v, :, 8:16], rot[:, v, 1], k_rows[:, v, :, 0:8], ALU.subtract)\
                            .then_inc(lo_done, 1)
                    if valid(n, -2):
                        pool.wait_ge(rope_done, n + 3)
                        wait(pool, hi_done, n + 1)
                        pool.tensor_tensor(
                            rot[:, u].rearrange("p a h (s d) -> p (a h) s d", s=2),
                            ta[:, u].rearrange("p a h (s d) -> p (a h) s d", s=2),
                            tb[:, u].rearrange("p a h (s d) -> p (a h) s d", s=2)[:, :, ::-1, :], ALU.add)\
                            .then_inc(r_done, 1)
                    if valid(n, 2):
                        pool.wait_ge(phi_done, n - 1)
                        pool.tensor_tensor(p_lo[:, u], e_buf[:, u], p_hi[:, u], ALU.subtract).then_inc(plo_done, 1)

                steps(pool, body, mlp_pool(pool)[1], norm=norm, low=ln_lo_of)

        until_mlp.close()
        x2_all = sb("x2_all", [128, B, NWIN, WTOK])
        sg = sb("sg", [128, 2, CHUNK])
        hid = sb("hid", [128, 2, CHUNK])
        f_rows = sb("f_rows", [128, 2, NB], F16)
        g_rows = sb("g_rows", [128, 2, NB], F16)
        mh = sb("mh", [128, BT, 64], F16)

        def mlp_steps(eng, body, pads=lambda: None):
            body(1, 1)
            pads()
            with eng.Fori(1, CHUNKS // 2 - 1) as it:
                for u in range(2):
                    body(it * 2 + u, u)
            for c in range(CHUNKS - 2, CHUNKS + 2):
                body(c, c % 2)

        @block.gpsimd
        def _(pool):
            body, early, pads = mlp_pool(pool)
            mlp_steps(pool, body, pads)

        @block.tensor
        def _(pe):
            body, early = mlp_pe(pe)
            pe.wait_ge(fc1_w_lo, 1)
            pe.wait_ge(fc2_w_ready, 1)
            pe.wait_ge(fc1_b_ready, 2)
            mlp_steps(pe, body)

        @block.vector
        def _(dve):
            body, early = mlp_dve(dve)
            mlp_steps(dve, body)

        @block.scalar
        def _(act):
            body, early = mlp_act(act)
            act.wait_ge(fc1_b_ready, 2)
            mlp_steps(act, body)

        xg_done = sem("xg_done")
        fg_done = sem("fg_done")
        fg_hi = sem("fg_hi")
        fg_ready = sem("fg_ready")
        v4_done = sem("v4_done")
        v4_ready = sem("v4_ready")
        s4_done = sem("s4_done")
        max4_done = sem("max4_done")
        mh_tmp = sem("mh_tmp")
        mh_ready = sem("mh_ready")
        mq_ready = sem("mq_ready")
        mt_done = sem("mt_done")
        mrow_ready = sem("mrow_ready")
        st4_done = sem("st4_done")
        exp4_done = sem("exp4_done")
        eh_done = sem("eh_done")
        el_done = sem("el_done")
        v4_lo = sem("v4_lo")
        sum4_done = sem("sum4_done")
        pv4_done = sem("pv4_done")
        rrow_ready = sem("rrow_ready")
        rec4_done = sem("rec4_done")
        r_turned = sem("r_turned")
        div_done = sem("div_done")
        o_ready = sem("o_ready")
        stored = [sem(f"stored{u}") for u in range(2)]
        E_BUFS, H_BUFS = 4, 3
        VSCALE = 16.0
        with ExitStack() as st:
            def tmp(name, shape, dt=F32):
                return st.enter_context(nc.sbuf_tensor(name, shape, dt))

            xg = tmp("xg", [128, 2, NB])
            gbv = tmp("gbv", [128, 1])
            fg_bm = tmp("fg_bm", [64, 2])
            fgh = tmp("fgh", [64, 2, NB], F16)
            val = tmp("val", [128, 2, 2, BT, DIM], F16)
            mx = tmp("mx4", [128, BT])
            mq = tmp("mq", [128, BT])
            e4 = tmp("e4", [128, E_BUFS, NB])
            eh = tmp("eh", [128, H_BUFS, NB], F16)
            el = tmp("el", [128, H_BUFS, NB], F16)
            e_sum = tmp("e_sum", [128, 2, NB], F16)
            den = tmp("den", [128, 2, BT])
            r_rows = tmp("r_rows", [128, NB])
            gamma_s = tmp("gamma_s", [128, 1])
            rec4 = tmp("rec4", [128, BT])
            rh = tmp("rh", [128, 2, 2, BT], F16)
            o4 = tmp("o4", [128, 2, 512])
            ob = tmp("ob", [128, 2, NB])

            LAG = 2

            S4, AUX, ST4, PV4 = 0, 6, 2, 4
            S_PAIR = (S4, AUX)
            S_FIRST = (S4, PV4, AUX, ST4)

            def two(bank, rows=slice(0, 128)):
                return ps[rows, bank:bank + 2, :].rearrange("p a b -> p (a b)")

            def low_weights(eng, key):
                wait(eng, pv4_done, key - H_BUFS + 1)
                eng.tensor_tensor(el[:, key % H_BUFS, :], e4[:, key % E_BUFS, :], eh[:, key % H_BUFS, :],
                                  ALU.subtract).then_inc(el_done, 1)

            def output(eng, b, half, u, k):
                eng.wait_ge(xg_done, b + 1)
                eng.wait_ge(stored[u], half * 32 + 32)
                eng.wait_ge(div_done, b * 2 + k + 1)
                eng.tensor_tensor(ob[:, u, 512 * k:512 * k + 512], o4[:, k, :], xg[:, u, 512 * k:512 * k + 512],
                                  ALU.add).then_inc(o_ready, 1)

            def st_bank(n, nxt):
                return ST4 if nxt else (ST4, AUX)[n % 2]

            def g_bank(b):
                return PV4 if b == 0 else ST4

            def last_use(b, bank):
                return BT - 4 + S_FIRST.index(bank) + 1 if b == 0 else BT - 1 + S_PAIR.index(bank)

            def s_bank(n, cur):
                return S_PAIR[n % 2] if cur else S_FIRST[n % 4]

            def steps(eng, body):
                for b in range(-1, B):
                    body(b, b // 2, b % 2, b >= 0, b + 1 < B)

            @block.tensor
            def _(pe):

                def tokens(b, first, count):
                    return x2_all[:, b].rearrange("p w q -> p (w q)")[:, first:first + count]

                def out4(b, u, m):
                    pe.wait_ge(el_done, b * BT + m + 1)
                    if m == 0:
                        pe.wait_ge(rrow_ready, b + 1)
                    for n, (part, weights) in enumerate(((0, eh), (1, eh), (0, el))):
                        for k in range(2):
                            last = pe.matmul(ps[:, PV4 + k, :], val[:, u, part, m, :],
                                             weights[:, (b * BT + m) % H_BUFS, 512 * k:512 * k + 512],
                                             start=(m == 0 and n == 0), stop=(m == BT - 1 and n == 2),
                                             skip_group_check=True)
                    last.then_inc(pv4_done, 1)

                def project_fg(k, bank, b, halves=(0, 1)):
                    for n in halves:
                        last = pe.matmul(ps[0:64, bank + n, :], fg_w[:, k, :], tokens(b, 512 * n, 512),
                                         start=True, stop=True)
                    if 1 in halves:
                        last.then_inc(fg_done, 1)

                def project_v(b):
                    for n in range(BT):
                        last = pe.matmul(ps[:, AUX + n // 4, 128 * (n % 4):128 * (n % 4) + 128],
                                         tokens(b, 128 * n, 128), wv[:], start=(n % 4 == 0), stop=True,
                                         skip_group_check=True)
                    last.then_inc(v4_done, 1)

                pe.wait_ge(x2_done, CHUNKS // 2)
                pe.wait_ge(silu_done, CHUNKS * HBLK)
                pe.wait_ge(h_done, CHUNKS * HBLK)
                project_fg(0, S4, 0, (0,))
                project_fg(1, ST4, 0, (0,))
                pe.wait_ge(x2_done, CHUNKS)

                def body(b, half, u, cur, nxt):
                    v = 1 - u
                    if nxt:
                        wait(pe, sum4_done, b * BT + last_use(b, S4))
                        project_fg(0, S4, b + 1, (0, 1) if cur else (1,))
                    if cur:
                        pe.wait_ge(mh_ready, b * BT + BT)
                        pe.wait_ge(sum4_done, b * BT + last_use(b, S4))
                        for n in range(BT):
                            last = pe.matmul(ps[64:128, S4 + n // 4, 128 * (n % 4):128 * (n % 4) + 128], mh[:, n, :],
                                             ident16[:], start=(n % 4 == 0), stop=True, skip_group_check=True)
                        last.then_inc(mt_done, 1)
                    if nxt:
                        wait(pe, exp4_done, b * BT)
                        if b == 0:
                            pe.wait_ge(sum4_done, last_use(b, PV4))
                        project_fg(1, g_bank(b), b + 1, (0, 1) if cur else (1,))
                    if b >= 1:
                        out4(b - 1, v, BT - 1)
                    if nxt:
                        wait(pe, sum4_done, b * BT + last_use(b, AUX))
                        project_v(b + 1)
                        pe.wait_ge(fg_ready, b * 2 + 4)
                    for n in range(BT):
                        if cur:
                            if n == 0:
                                pe.wait_ge(mrow_ready, b + 1)
                                pe.wait_ge(sum4_done, b * BT + BT)
                            wait(pe, exp4_done, b * BT + n - (0 if nxt or n == 0 else 1))
                            for k in range(2):
                                last = pe.matmul(ps[:, st_bank(n, nxt) + k, :], g_rows[:, u, 128 * n:128 * n + 128],
                                                 f_rows[:, u, 512 * k:512 * k + 512], start=True, stop=True)
                            last.then_inc(st4_done, 1)
                            if n >= LAG:
                                out4(b, u, n - LAG)
                        if nxt:
                            if n == 0:
                                pe.wait_ge(fg_ready, b * 2 + 4)
                                pe.wait_ge(pads_set, 5)
                            ahead = 2 if cur else 4
                            if s_bank(n, cur) == AUX and n < ahead:
                                pe.wait_ge(v4_lo, b + 2)
                            if n >= ahead:
                                pe.wait_ge(sum4_done, b * BT + BT + n - ahead + 1)
                            for m in range(2):
                                last = pe.matmul(ps[:, s_bank(n, cur) + m, :], f_rows[0:64, v, 128 * n:128 * n + 128],
                                                 g_rows[0:64, v, 512 * m:512 * m + 512], start=True, stop=True)
                            last.then_inc(s4_done, 1)
                        if cur and n == 0:
                            pe.wait_ge(rec4_done, b * 3 + 3)
                            wait(pe, div_done, b * 2)
                            for m in range(BT):
                                for k in range(2):
                                    last = pe.matmul(ps[:, PV4 + m // 4, 128 * (m % 4):128 * (m % 4) + 128],
                                                     rh[:, u, k, m:m + 1].broadcast_to([128, 128]), ident16[:],
                                                     start=(m % 4 == 0 and k == 0), stop=(k == 1), skip_group_check=True)
                            last.then_inc(r_turned, 1)
                    if cur:
                        for m in range(BT - LAG, BT - 1):
                            out4(b, u, m)
                        if not nxt:
                            out4(b, u, BT - 1)

                steps(pe, body)

            @block.vector
            def _(dve):
                dve.wait_ge(pads_set, 5)
                dve.tensor_tensor(gbv[:], cols[:, 1:2], cols[:, 2:3], ALU.mult).then_inc(pads_set, 1)
                dve.tensor_scalar(gamma_s[:], cols[:, 1:2], 1.0 / (RSCALE * VSCALE), None, ALU.mult).then_inc(pads_set, 1)
                dve.tensor_tensor(fg_bm[:], fg_b[:, 0:2], fg_b[:, 2:4], ALU.mult).then_inc(pads_set, 1)
                dve.wait_ge(pads_set, 8)

                def divided(b, half, u, nxt):
                    dve.wait_ge(rrow_ready, b + 1)
                    wait(dve, o_ready, b * 2)
                    dve.wait_ge(pv4_done, b * BT + BT)
                    for k in range(2):
                        dve.tensor_tensor(o4[:, k, :], ps[:, PV4 + k, :], r_rows[:, 512 * k:512 * k + 512], ALU.mult)\
                            .then_inc(div_done, 1)
                        if not nxt:
                            output(dve, b, half, u, k)

                def maximum_hi(tile, n):
                    dve.wait_ge(max4_done, tile + 1)
                    dve.tensor_scalar(mh[:, n, 0:1], mx[:, n:n + 1], 1.0 / MSCALE, None, ALU.mult).then_inc(mh_tmp, 1)

                def maximum_lo(tile, n):
                    dve.wait_ge(mh_tmp, tile + 1)
                    dve.scalar_tensor_tensor(out=mh[:, n, 32:33], in0=mh[:, n, 0:1], scalar=-MSCALE,
                                             in1=mx[:, n:n + 1], op0=ALU.mult, op1=ALU.add).then_inc(mh_ready, 1)

                def maximum_sum(tile, n):
                    dve.wait_ge(mh_ready, tile + 1)
                    dve.scalar_tensor_tensor(out=mq[:, n:n + 1], in0=mh[:, n, 0:1], scalar=MSCALE,
                                             in1=mh[:, n, 32:33], op0=ALU.mult, op1=ALU.add).then_inc(mq_ready, 1)

                def body(b, half, u, cur, nxt):
                    v = 1 - u
                    if cur:
                        dve.wait_ge(mt_done, b + 1)
                        dve.tensor_copy(f_rows[64:128, u, :], two(S4, slice(64, 128))).then_inc(mrow_ready, 1)
                    if nxt:
                        for k, (rows, bank) in enumerate(((f_rows, S4), (g_rows, g_bank(b)))):
                            dve.wait_ge(fg_hi, b * 2 + k + 3)
                            dve.scalar_tensor_tensor(out=rows[0:64, v, :], in0=two(bank, slice(0, 64)),
                                                     scalar=fg_b[:, k:k + 1], in1=fgh[:, k, :], op0=ALU.add,
                                                     op1=ALU.subtract).then_inc(fg_ready, 1)
                    if b >= 1:
                        divided(b - 1, 0, v, True)
                    if nxt:
                        dve.wait_ge(v4_ready, b + 2)
                        dve.scalar_tensor_tensor(out=val[:, v, 1].rearrange("p n d -> p (n d)"), in0=two(AUX),
                                                 scalar=VSCALE, in1=val[:, v, 0].rearrange("p n d -> p (n d)"),
                                                 op0=ALU.mult, op1=ALU.subtract).then_inc(v4_lo, 1)
                    for n in range(BT):
                        if cur:
                            key = b * BT + n
                            dve.wait_ge(exp4_done, key + 1)
                            wait(dve, pv4_done, key - H_BUFS + 1)
                            dve.tensor_copy(eh[:, key % H_BUFS, :], e4[:, n % E_BUFS, :]).then_inc(eh_done, 1)
                            if not nxt:
                                dve.wait_ge(eh_done, key + 1)
                                if n == 0:
                                    dve.wait_ge(el_done, key)
                                low_weights(dve, key)
                        if nxt:
                            tile = b * BT + BT + n
                            dve.wait_ge(s4_done, tile + 1)
                            dve.tensor_reduce(mx[:, n:n + 1], two(s_bank(n, cur)), AX.X, ALU.max, negate=True)\
                                .then_inc(max4_done, 1)
                            if not cur and n >= 1:
                                maximum_lo(tile - 1, n - 1)
                            maximum_hi(tile, n)
                            if not cur and n >= 1:
                                maximum_sum(tile - 1, n - 1)
                            if cur or n == BT - 1:
                                maximum_lo(tile, n)
                                maximum_sum(tile, n)
                    if cur and not nxt:
                        divided(b, half, u, nxt)
                    if nxt:
                        dve.wait_ge(sum4_done, b * BT + 2 * BT)
                        dve.reciprocal(rec4[:], den[:, v, :]).then_inc(rec4_done, 1)
                        dve.wait_ge(rec4_done, b * 3 + 4)
                        dve.tensor_scalar(rh[:, v, 0, :], rec4[:], RSCALE, None, ALU.mult).then_inc(rec4_done, 1)
                        dve.wait_ge(rec4_done, b * 3 + 5)
                        dve.scalar_tensor_tensor(out=rh[:, v, 1, :], in0=rec4[:], scalar=RSCALE, in1=rh[:, v, 0, :],
                                                 op0=ALU.mult, op1=ALU.subtract).then_inc(rec4_done, 1)

                steps(dve, body)

            @block.scalar
            def _(act):
                act.wait_ge(pads_set, 8)

                def body(b, half, u, cur, nxt):
                    v = 1 - u
                    if nxt:
                        for k, bank in enumerate((S4, g_bank(b))):
                            act.wait_ge(fg_done, b * 2 + k + 3)
                            wait(act, fg_ready, b * 2 + 2)
                            act.activation(fgh[:, k, :], two(bank, slice(0, 64)), ACT.Identity,
                                           bias=fg_bm[:, k:k + 1], scale=fg_b[:, 2 + k:3 + k]).then_inc(fg_hi, 1)
                        act.wait_ge(v4_done, b + 2)
                        act.activation(val[:, v, 0].rearrange("p n d -> p (n d)"), two(AUX), ACT.Copy, scale=VSCALE)\
                            .then_inc(v4_ready, 1)
                    for m in range(BT + 1):
                        if cur and m < BT:
                            act.wait_ge(st4_done, b * BT + m + 1)
                            wait(act, el_done, b * BT + m - E_BUFS + 1)
                            act.activation(e4[:, m % E_BUFS, :], two(st_bank(m, nxt)), ACT.Exp).then_inc(exp4_done, 1)
                        if cur and m == 1:
                            act.wait_ge(r_turned, b + 1)
                            wait(act, div_done, b * 2)
                            act.activation(r_rows[:], two(PV4), ACT.Identity, bias=0.0, scale=gamma_s[:])\
                                .then_inc(rrow_ready, 1)
                        if cur and m == 4:
                            act.activation(xg[:, u, :], x2_all[:, b].rearrange("p w q -> p (w q)"), ACT.Identity,
                                           bias=gbv[:], scale=1.0).then_inc(xg_done, 1)
                        if nxt and m >= 1:
                            act.wait_ge(mq_ready, b * BT + BT + m)
                            wait(act, sum4_done, b * BT + BT + m - 2)
                            act.activation(e_sum[:, m % 2, :], two(s_bank(m - 1, cur)), ACT.Exp, bias=mq[:, m - 1:m],
                                           scale=1.0, accum_out=den[:, v, m - 1:m]).then_inc(sum4_done, 1)

                steps(act, body)

            @block.gpsimd
            def _(pool):
                def body(b, half, u, cur, nxt):
                    for m in range(BT):
                        if cur and nxt:
                            pool.wait_ge(eh_done, b * BT + m + 1)
                            low_weights(pool, b * BT + m)
                    if cur and nxt:
                        for k in range(2):
                            output(pool, b, half, u, k)

                steps(pool, body)

            @block.sync
            def _(sp):
                for u in range(2):
                    sp.sem_inc(stored[u], 32)

                def body(b, half, u, cur, nxt):
                    if cur:
                        for k in range(2):
                            sp.wait_ge(o_ready, b * 2 + k + 1)
                            sp.dma_start(t["out"][at(b, 1), :, 512 * k:512 * k + 512].rearrange("a p n -> (a p) n"),
                                         ob[:, u, 512 * k:512 * k + 512]).then_inc(stored[u], 16)

                steps(sp, body)
                for u in range(2):
                    sp.wait_ge(stored[u], 32 * (B // 2 + 1))


def _rope_tables():
    d1 = HD // 4
    inv = (10000.0 ** (-(np.arange(d1, dtype=np.float32) / d1))).astype(np.float32)
    pos = np.arange(WIN, dtype=np.float32)
    ang = pos[:, None] * inv
    rows = np.broadcast_to(ang[:, None, :], (WIN, WIN, d1)).reshape(WTOK, d1)
    cols = np.broadcast_to(ang[None, :, :], (WIN, WIN, d1)).reshape(WTOK, d1)
    a = np.concatenate([rows, cols], 1).astype(np.float32)
    cos, sin = np.cos(a), np.sin(a)
    c = np.concatenate([cos, cos], 1)
    s = np.concatenate([sin, -sin], 1)
    table = np.stack([c, s]) / WSCALE
    both = np.stack([table * HD ** -0.5, table], 2)
    both = np.concatenate([both, both], 1)
    return np.ascontiguousarray(both.transpose(1, 0, 2, 3)).astype(np.float32)


def kernel(**inputs):
    import concourse.bacc as bacc
    from concourse.bass_utils import run_bass_kernel_spmd

    def a(name):
        return np.asarray(inputs[name])

    def L0(name):
        return a("L0_conv_" + name)

    def L1(name):
        return a("L1_conv_" + name)

    x = np.roll(a("x"), (-SHIFT, -SHIFT), (1, 2))
    nh, nw = H // WIN, W // WIN
    x = x.reshape(B, nh, WIN, nw, WIN, DIM).transpose(1, 3, 0, 2, 4, 5).reshape(PAIRS, 2 * WTOK, DIM)
    ch = np.arange(DIM).reshape(HP, 2, HD).transpose(1, 0, 2).reshape(DIM)
    qkv_w, qkv_b = L0("qkv_w"), L0("qkv_b")
    proj = L0("proj_w")[:, ch].T
    mask = L0("attn_mask")
    both = np.stack([mask.transpose(1, 0, 2), mask.transpose(2, 0, 1)], 1)
    fc1_b = L0("fc1_b").reshape(2 * HBLK, 128).T
    zero = np.zeros(DIM, np.float32)
    lo_f = np.repeat(np.array([0, 0, 1, 1], np.float32), CQK)
    lo_g = np.repeat(np.array([0, 1, 0, 1], np.float32), CQK)
    sel = np.zeros((33, 128), np.float16)
    sel[0], sel[32] = 1, 1
    data = {
        "x": x.transpose(1, 0, 2),
        "qkv_w": qkv_w.T,
        "qkv_b": np.broadcast_to(qkv_b, (33, 3 * DIM)),
        "g1b1": np.stack([L0("norm1_g"), L0("norm1_b"), L0("norm2_g"), L0("norm2_b")], 1),
        "ident16": np.eye(128, dtype=np.float16),
        "ident": np.eye(128, dtype=np.float32),
        "sel33": sel,
        "rope": _rope_tables(),
        "mask": np.concatenate([both, both], 0),
        "identb": np.eye(128, dtype=np.float32).astype(mybir.dt.np(mybir.dt.bfloat16)),
        "proj_w": proj,
        "proj_b": np.broadcast_to(L0("proj_b"), (128, DIM)),
        "fc1_w": L0("fc1_w").T,
        "fc1_b": fc1_b,
        "fc2_w": L0("fc2_w").T.reshape(HBLK, 128, DIM).transpose(1, 0, 2),
        "cols": np.stack([L0("fc2_b"), np.broadcast_to(L1("gamma"), (DIM,)), L1("bv"), zero], 1),
        "fg_w": np.stack([np.tile(L1("Wq"), (1, 4)), np.tile(L1("Wk"), (1, 4))], 1),
        "fg_b": np.stack([np.tile(L1("bq"), 4), np.tile(L1("bk"), 4), lo_f, lo_g], 1),
        "wv": L1("Wv"),
        "ln_const": np.broadcast_to(np.array([-0.5, EPS, -1], np.float32)[:, None], (128, 3, TPC)),
    }
    nc = bacc.Bacc("TRN2", target_bir_lowering=False, num_devices=1)
    arrays, t = {}, {}
    for name, v in data.items():
        v = np.ascontiguousarray(v)
        arrays["in_" + name] = v
        t[name] = nc.dram_tensor("in_" + name, v.shape, mybir.dt.from_np(v.dtype), kind="ExternalInput").ap()
    t["out"] = nc.dram_tensor("out", (B, DIM, NB), F32, kind="ExternalOutput").ap()
    build(nc, t)
    got = run_bass_kernel_spmd(nc, [arrays], core_ids=[0]).results[0]["out"]
    y = np.asarray(got).reshape(B, DIM, nh, nw, WIN, WIN).transpose(0, 2, 4, 3, 5, 1).reshape(B, H, W, DIM)
    return np.roll(y, (SHIFT, SHIFT), (1, 2))
```
